# Optimizing a Trainium2 kernel written in Bass

```python
import numpy as np
import jax
import jax.numpy as jnp

def _softmax(x, axis=-1):
    return jax.nn.softmax(x, axis=axis)

def _gelu(x):
    return jax.nn.gelu(x, approximate=True)

def _silu(x):
    return jax.nn.silu(x)

def _sigmoid(x):
    return jax.nn.sigmoid(x)

def _layernorm(x, axis=-1, eps=1e-05):
    m = jnp.mean(x, axis=axis, keepdims=True)
    v = jnp.var(x, axis=axis, keepdims=True)
    return (x - m) / jnp.sqrt(v + eps)

def _scatter_add(tgt, idx, src, axis=0):
    return tgt.at[idx].add(src)

def _segment_sum(src, seg, n):
    return jax.ops.segment_sum(src, seg, n)
kernel_name = 'mk_xattn_ffn_d2_seqx_r8_ad4d0c'

def setup_inputs(seed: int=0):
    np.random.seed(seed)
    _w = jnp.asarray

    def _rec_inputs():
        import jax
        import jax.numpy as jnp
        _rk = jax.random.key(seed)
        x = -0.0002928 + 1 * jax.random.normal(jax.random.fold_in(_rk, 1), (2, 512, 128), jnp.float32)
        _lenS = 512 - jax.random.randint(jax.random.fold_in(_rk, 7), (2,), 0, max(1, 512 // 4) + 1, jnp.int32)
        _lenS2 = 77 - jax.random.randint(jax.random.fold_in(_rk, 8), (2,), 0, max(1, 77 // 4) + 1, jnp.int32)
        _ctx_1024P = jax.random.normal(jax.random.fold_in(_rk, 11), (2, 16, 128), jnp.float32)
        _ctx_1024c = jax.random.dirichlet(jax.random.fold_in(_rk, 511), 0.3 * jnp.ones((16,), jnp.float32), (2, 77))
        _ctx_1024t = jnp.einsum('bsk,bkd->bsd', _ctx_1024c, _ctx_1024P)
        _ctx_1024t = _ctx_1024t * jax.lax.rsqrt(jnp.mean(jnp.square(_ctx_1024t)) + 1e-12) * 0.953939
        ctx_1024 = -1.39393e-06 + 0.999914 * (_ctx_1024t + 0.3 * jax.random.normal(jax.random.fold_in(_rk, 611), (2, 77, 128), jnp.float32))
        _validS = jnp.arange(512)[None, :] < _lenS[:, None]
        _validS2 = jnp.arange(77)[None, :] < _lenS2[:, None]
        _causal = jnp.tril(jnp.ones((512, 512), dtype=bool))
        mask_BxS2_bk0 = jnp.logical_not(jnp.broadcast_to(_validS2[:, :], (2, 77)))
        return (x, ctx_1024, mask_BxS2_bk0)
    x, ctx_1024, mask_BxS2_bk0 = _rec_inputs()

    def _L0_xattn_setup():
        import jax, jax.numpy as jnp
        import numpy as np
        HEADS = 16
        EMBED = 128
        HEAD_DIM = EMBED // HEADS
        key = jax.random.key(seed)
        ks = jax.random.split(key, 7)
        B, S, E = (2, 256, EMBED)
        scale = 1.0 / np.sqrt(E)
        return {'query': jax.random.normal(ks[0], (B, S, E), dtype=jnp.float32), 'key': jax.random.normal(ks[1], (B, S, E), dtype=jnp.float32), 'value': jax.random.normal(ks[2], (B, S, E), dtype=jnp.float32), 'Wq': jax.random.normal(ks[3], (E, E), dtype=jnp.float32) * scale, 'Wk': jax.random.normal(ks[4], (E, E), dtype=jnp.float32) * scale, 'Wv': jax.random.normal(ks[5], (E, E), dtype=jnp.float32) * scale, 'Wo': jax.random.normal(ks[6], (E, E), dtype=jnp.float32) * scale}
    _L0_xattn_all = _L0_xattn_setup()
    _L0_xattn_in = {k: v for k, v in _L0_xattn_all.items() if k in ('Wq', 'Wk', 'Wv', 'Wo')}
    del _L0_xattn_all

    def _L0_ffn_setup():
        import jax, jax.numpy as jnp
        import numpy as np
        B, T, D = (2, 256, 128)
        E, DFF, TOPK = (8, 512, 2)
        TEMPERATURE = 1.0
        key = jax.random.key(seed)
        k_x, k_w1, k_w2, k_r = jax.random.split(key, 4)
        x = jax.random.normal(k_x, (B, T, D), dtype=jnp.float32)
        W1 = jax.random.normal(k_w1, (E, DFF, D), dtype=jnp.float32) * 0.02
        W2 = jax.random.normal(k_w2, (E, D, DFF), dtype=jnp.float32) * 0.02
        Wr = jax.random.normal(k_r, (E, D), dtype=jnp.float32) * 0.02
        return {'x': x, 'W1': W1, 'W2': W2, 'Wr': Wr}
    _L0_ffn_all = _L0_ffn_setup()
    _L0_ffn_in = {k: v for k, v in _L0_ffn_all.items() if k in ('W1', 'W2', 'Wr')}
    del _L0_ffn_all

    def _L1_xattn_setup():
        import jax, jax.numpy as jnp
        import numpy as np
        NUM_HEADS, NUM_KV, HEAD_DIM, WIDTH = (4, 1, 32, 128)
        MASK_FILL = -2.3819763e+38

        def _apply_rope(x, positions, max_wavelength=10000.0):
            d = x.shape[-1]
            freq_exp = 2.0 / d * jnp.arange(d // 2, dtype=jnp.float32)
            timescale = max_wavelength ** freq_exp
            radians = positions[..., None].astype(jnp.float32) / timescale
            radians = radians[..., None, :]
            sin, cos = (jnp.sin(radians), jnp.cos(radians))
            x1, x2 = jnp.split(x, 2, axis=-1)
            out = jnp.concatenate([x1 * cos - x2 * sin, x2 * cos + x1 * sin], axis=-1)
            return out.astype(x.dtype)

        def _rmsnorm(x, scale):
            var = jnp.mean(jnp.square(x.astype(jnp.float32)), axis=-1, keepdims=True)
            normed = x * jax.lax.rsqrt(var + 1e-06)
            return (normed * (1 + scale)).astype(x.dtype)
        key = jax.random.key(seed)
        ks = jax.random.split(key, 7)
        B, T, S = (8, 64, 256)
        return {'x': jax.random.normal(ks[0], (B, T, WIDTH), jnp.float32), 'mem_seq': jax.random.normal(ks[1], (B, S, WIDTH), jnp.float32), 'mem_mask': jax.random.randint(ks[2], (B, S), 0, 2).astype(bool), 'rms_scale': jax.random.normal(ks[3], (WIDTH,), jnp.float32) * 0.02, 'q_w': jax.random.normal(ks[4], (NUM_HEADS, WIDTH, HEAD_DIM), jnp.float32) / np.sqrt(WIDTH), 'kv_w': jax.random.normal(ks[5], (2, NUM_KV, WIDTH, HEAD_DIM), jnp.float32) / np.sqrt(WIDTH), 'out_w': jax.random.normal(ks[6], (NUM_HEADS, HEAD_DIM, WIDTH), jnp.float32) / np.sqrt(NUM_HEADS * HEAD_DIM)}
    _L1_xattn_all = _L1_xattn_setup()
    _L1_xattn_in = {k: v for k, v in _L1_xattn_all.items() if k in ('rms_scale', 'q_w', 'kv_w', 'out_w')}
    del _L1_xattn_all

    def _L1_ffn_setup():
        import jax, jax.numpy as jnp
        import numpy as np
        B, C, D, O = (4, 512, 128, 128)
        PROJ = 32
        RANKS = [1, 2, 4, 8]
        E = len(RANKS)
        CLAMP_MAX = float(np.log(1.0 / 0.01))

        def _l2norm(v, axis):
            return v / jnp.maximum(jnp.linalg.norm(v, axis=axis, keepdims=True), 1e-12)
        key = jax.random.key(seed)
        ks = jax.random.split(key, 16)
        inp = {'x': jax.random.normal(ks[0], (B, C, D), dtype=jnp.float32), 'W': jax.random.normal(ks[1], (O, D), dtype=jnp.float32) / np.sqrt(D), 'Wp': jax.random.normal(ks[2], (PROJ, D), dtype=jnp.float32) / np.sqrt(D), 'bp': jnp.zeros((PROJ,), dtype=jnp.float32), 'sim': jax.random.normal(ks[3], (PROJ, E), dtype=jnp.float32) * 0.01, 'temp': jnp.full((1,), np.log(1.0 / 0.5), dtype=jnp.float32)}
        for i, r in enumerate(RANKS):
            inp[f'Wd{i}'] = jax.random.normal(ks[4 + 2 * i], (r, D), dtype=jnp.float32) / r
            inp[f'Wu{i}'] = jax.random.normal(ks[5 + 2 * i], (O, r), dtype=jnp.float32) * 0.01
        return inp
    _L1_ffn_all = _L1_ffn_setup()
    _L1_ffn_in = {k: v for k, v in _L1_ffn_all.items() if k in ('W', 'Wp', 'bp', 'sim', 'temp', 'Wd0', 'Wu0', 'Wd1', 'Wu1', 'Wd2', 'Wu2', 'Wd3', 'Wu3')}
    del _L1_ffn_all
    return {'x': x, 'ctx_1024': ctx_1024, 'mask_BxS2_bk0': mask_BxS2_bk0, 'L0_xattn_Wq': _L0_xattn_in['Wq'], 'L0_xattn_Wk': _L0_xattn_in['Wk'], 'L0_xattn_Wv': _L0_xattn_in['Wv'], 'L0_xattn_Wo': _L0_xattn_in['Wo'], 'L0_ffn_W1': _L0_ffn_in['W1'], 'L0_ffn_W2': _L0_ffn_in['W2'], 'L0_ffn_Wr': _L0_ffn_in['Wr'], 'L1_xattn_rms_scale': _L1_xattn_in['rms_scale'], 'L1_xattn_q_w': _L1_xattn_in['q_w'], 'L1_xattn_kv_w': _L1_xattn_in['kv_w'], 'L1_xattn_out_w': _L1_xattn_in['out_w'], 'L1_ffn_W': _L1_ffn_in['W'], 'L1_ffn_Wp': _L1_ffn_in['Wp'], 'L1_ffn_bp': _L1_ffn_in['bp'], 'L1_ffn_sim': _L1_ffn_in['sim'], 'L1_ffn_temp': _L1_ffn_in['temp'], 'L1_ffn_Wd0': _L1_ffn_in['Wd0'], 'L1_ffn_Wu0': _L1_ffn_in['Wu0'], 'L1_ffn_Wd1': _L1_ffn_in['Wd1'], 'L1_ffn_Wu1': _L1_ffn_in['Wu1'], 'L1_ffn_Wd2': _L1_ffn_in['Wd2'], 'L1_ffn_Wu2': _L1_ffn_in['Wu2'], 'L1_ffn_Wd3': _L1_ffn_in['Wd3'], 'L1_ffn_Wu3': _L1_ffn_in['Wu3']}

def reference(x, ctx_1024, mask_BxS2_bk0, L0_xattn_Wq, L0_xattn_Wk, L0_xattn_Wv, L0_xattn_Wo, L0_ffn_W1, L0_ffn_W2, L0_ffn_Wr, L1_xattn_rms_scale, L1_xattn_q_w, L1_xattn_kv_w, L1_xattn_out_w, L1_ffn_W, L1_ffn_Wp, L1_ffn_bp, L1_ffn_sim, L1_ffn_temp, L1_ffn_Wd0, L1_ffn_Wu0, L1_ffn_Wd1, L1_ffn_Wu1, L1_ffn_Wd2, L1_ffn_Wu2, L1_ffn_Wd3, L1_ffn_Wu3):
    import jax
    import jax.numpy as jnp

    def _L0_xattn_ref(query, key, value, Wq, Wk, Wv, Wo):
        import jax, jax.numpy as jnp
        import numpy as np
        HEADS = 16
        EMBED = 128
        HEAD_DIM = EMBED // HEADS
        B, S, E = query.shape
        H, D = (HEADS, HEAD_DIM)

        def split_heads(x, W):
            return (x @ W.T).reshape(B, -1, H, D).transpose(0, 2, 1, 3)
        q = split_heads(query, Wq)
        k = split_heads(key, Wk)
        v = split_heads(value, Wv)
        scores = jnp.einsum('bhqd,bhkd->bhqk', q, k) / jnp.sqrt(jnp.float32(D))
        attn = jax.nn.softmax(scores, axis=-1)
        x = jnp.einsum('bhqk,bhkd->bhqd', attn, v)
        x = x.transpose(0, 2, 1, 3).reshape(B, -1, H * D)
        return x @ Wo.T

    def _L0_ffn_ref(x, W1, W2, Wr):
        import jax, jax.numpy as jnp
        import numpy as np
        B, T, D = (2, 256, 128)
        E, DFF, TOPK = (8, 512, 2)
        TEMPERATURE = 1.0
        logits = jnp.einsum('btd,ed->bte', x, Wr)
        probs = jax.nn.softmax(logits / TEMPERATURE, axis=-1)
        topk_vals, topk_idx = jax.lax.top_k(probs, TOPK)
        router_weights = topk_vals / topk_vals.sum(-1, keepdims=True)
        one_hot = jax.nn.one_hot(topk_idx, E, dtype=x.dtype)
        gate = jnp.einsum('btk,btke->bte', router_weights, one_hot)
        h = jax.nn.silu(jnp.einsum('btd,efd->btef', x, W1))
        y = jnp.einsum('btef,edf->bted', h, W2)
        out = jnp.einsum('bte,bted->btd', gate, y)
        return out

    def _L1_xattn_ref(x, mem_seq, mem_mask, rms_scale, q_w, kv_w, out_w):
        import jax, jax.numpy as jnp
        import numpy as np
        NUM_HEADS, NUM_KV, HEAD_DIM, WIDTH = (4, 1, 32, 128)
        MASK_FILL = -2.3819763e+38

        def _apply_rope(x, positions, max_wavelength=10000.0):
            d = x.shape[-1]
            freq_exp = 2.0 / d * jnp.arange(d // 2, dtype=jnp.float32)
            timescale = max_wavelength ** freq_exp
            radians = positions[..., None].astype(jnp.float32) / timescale
            radians = radians[..., None, :]
            sin, cos = (jnp.sin(radians), jnp.cos(radians))
            x1, x2 = jnp.split(x, 2, axis=-1)
            out = jnp.concatenate([x1 * cos - x2 * sin, x2 * cos + x1 * sin], axis=-1)
            return out.astype(x.dtype)

        def _rmsnorm(x, scale):
            var = jnp.mean(jnp.square(x.astype(jnp.float32)), axis=-1, keepdims=True)
            normed = x * jax.lax.rsqrt(var + 1e-06)
            return (normed * (1 + scale)).astype(x.dtype)
        B, S, _ = mem_seq.shape
        T = x.shape[1]
        G = NUM_HEADS // NUM_KV
        xn = _rmsnorm(x, rms_scale)
        mn = _rmsnorm(mem_seq, rms_scale)
        q = jnp.einsum('BTD,NDH->BTNH', xn, q_w)
        kv = jnp.einsum('BSD,cKDH->cBSKH', mn, kv_w)
        k, v = (kv[0], kv[1])
        q_pos = jnp.broadcast_to(jnp.arange(S, T + S), (B, T))
        k_pos = jnp.broadcast_to(jnp.arange(S), (B, S))
        q = _apply_rope(q, q_pos) * HEAD_DIM ** (-0.5)
        k = _apply_rope(k, k_pos)
        q = q.reshape(B, T, NUM_KV, G, HEAD_DIM)
        logits = jnp.einsum('BTKGH,BSKH->BKGTS', q, k, preferred_element_type=jnp.float32)
        masked = jnp.where(mem_mask[:, None, None, None, :], logits, MASK_FILL)
        probs = jax.nn.softmax(masked, axis=-1).astype(x.dtype)
        enc = jnp.einsum('BKGTS,BSKH->BTKGH', probs, v).reshape(B, T, NUM_HEADS, HEAD_DIM)
        return jnp.einsum('BTNH,NHD->BTD', enc, out_w)

    def _L1_ffn_ref(x, W, Wp, bp, sim, temp, Wd0, Wu0, Wd1, Wu1, Wd2, Wu2, Wd3, Wu3):
        import jax, jax.numpy as jnp
        import numpy as np
        B, C, D, O = (4, 512, 128, 128)
        PROJ = 32
        RANKS = [1, 2, 4, 8]
        E = len(RANKS)
        CLAMP_MAX = float(np.log(1.0 / 0.01))

        def _l2norm(v, axis):
            return v / jnp.maximum(jnp.linalg.norm(v, axis=axis, keepdims=True), 1e-12)
        base = jnp.einsum('bcd,od->bco', x, W)
        xf = x.reshape(-1, x.shape[-1])
        proj = _l2norm(xf @ Wp.T + bp, axis=1)
        simn = _l2norm(sim, axis=0)
        scale = jnp.exp(jnp.minimum(temp, CLAMP_MAX))
        logits = proj @ simn * scale
        lw = jax.nn.softmax(logits, axis=1)
        top1 = jnp.argmax(lw, axis=1)
        ret = jnp.where(jnp.arange(E)[None, :] == top1[:, None], lw, 0.0)
        ret = ret.reshape(x.shape[0], x.shape[1], E)
        downs = (Wd0, Wd1, Wd2, Wd3)
        ups = (Wu0, Wu1, Wu2, Wu3)
        l = jnp.stack([jnp.einsum('bcr,or->bco', jnp.einsum('bcd,rd->bcr', x, d), u) for d, u in zip(downs, ups)], axis=2)
        res = jnp.sum(ret[..., None] * l, axis=2)
        return base + res
    x = x + _L0_xattn_ref(_layernorm(x, axis=-1), ctx_1024, ctx_1024, L0_xattn_Wq, L0_xattn_Wk, L0_xattn_Wv, L0_xattn_Wo)
    x = x + _L0_ffn_ref(_layernorm(x, axis=-1), L0_ffn_W1, L0_ffn_W2, L0_ffn_Wr)
    x = x + _L1_xattn_ref(_layernorm(x, axis=-1), ctx_1024, mask_BxS2_bk0, L1_xattn_rms_scale, L1_xattn_q_w, L1_xattn_kv_w, L1_xattn_out_w)
    x = x + _L1_ffn_ref(_layernorm(x, axis=-1), L1_ffn_W, L1_ffn_Wp, L1_ffn_bp, L1_ffn_sim, L1_ffn_temp, L1_ffn_Wd0, L1_ffn_Wu0, L1_ffn_Wd1, L1_ffn_Wu1, L1_ffn_Wd2, L1_ffn_Wu2, L1_ffn_Wd3, L1_ffn_Wu3)
    return x

_drawn_inputs = setup_inputs


def setup_inputs(seed=0):
    import zlib

    import numpy as np

    out = dict(_drawn_inputs(seed))
    spreads = {'L1_ffn_bp': (0.0, 0.8)}
    factors = {'L1_xattn_rms_scale': 4.163,
     'L1_ffn_Wp': 2.977,
     'L1_ffn_sim': 3.046,
     'L1_ffn_Wd1': 8.0,
     'L1_ffn_Wu1': 8.0,
     'L1_ffn_Wd2': 8.0,
     'L1_ffn_Wu2': 8.0,
     'L1_ffn_Wd3': 8.0,
     'L1_ffn_Wu3': 8.0,
     'L1_ffn_Wd0': 2.754,
     'L1_ffn_Wu0': 2.847}
    for name, (base, spread) in spreads.items():
        noise = np.random.default_rng([zlib.crc32(name.encode()), seed]).standard_normal(out[name].shape)
        drawn = base * np.exp(spread * noise) if base else spread * noise
        out[name] = jnp.asarray(drawn.astype(out[name].dtype))
    for name, factor in factors.items():
        out[name] = (out[name] * factor).astype(out[name].dtype)
    return out
```

```python
import concourse.bass as bass
from concourse import mybir
from contextlib import ExitStack
import numpy as np

P = 128
B, S, D = 2, 512, 128
NT = S // P
TILES = B * NT
KC = 77
KCP = 80
H0, HD0 = 16, 8
GH = 4
G0 = H0 // GH
SH = H0 // 2
H1, HD1 = 4, 32
E, F = 8, 512
FC = F // P
E1 = 4
RANKS = [1, 2, 4, 8]
RSUM = sum(RANKS)
PROJ = 32
LAG = 4
NH = 2 * LAG
UE = B * FC
US = 2 * UE
PAIRS = E // 2
NEVER = -(2.0 ** 100)
CLAMP = 4.605170185988091

def columns(*widths):
    out, at = {}, 0
    for name, n in widths:
        out[name] = slice(at, at + n)
        at += n
    return out, at

C0, C0W = columns(("ident", P), ("block", GH * KC), ("ones", GH * KC), ("vpat", 2 * 640))
W0, W0W = columns(("k", G0 * 96), ("q", G0 * 96), ("v", D), ("o", D))
C1, C1W = columns(("qcos", S), ("qsin", S), ("kcos", KC), ("ksin", KC), ("block", H1 * KC), ("vpat", 264),
                  ("selm", H1 * KC), ("gsel", E * P), ("tie8", E), ("tie4", E1))
W1, W1W = columns(("r", E), ("q", D), ("qrot", D), ("k", D), ("krot", D), ("v", HD1), ("o", D), ("rms", 1),
                  ("pd", PROJ + RSUM), ("base", D), ("up", D), ("bp", PROJ), ("sim", E1 * PROJ), ("temp", 1))


def fused_layers(nc, x, ctx_nat, ctx_t, mask, c0, w0, c1, w1, moe, out):
    fp32 = mybir.dt.float32
    f32r = mybir.dt.float32r
    u8 = mybir.dt.uint8
    ALU = mybir.AluOpType
    ACT = mybir.ActivationFunctionType
    AX = mybir.AxisListType

    with ExitStack() as ctx:
        def sb(name, shape, dt=fp32):
            return ctx.enter_context(nc.sbuf_tensor(name, shape, dt))

        def sem(name):
            return ctx.enter_context(nc.semaphore(name))

        PS = ctx.enter_context(nc.psum_tensor("PS", [P, 8, 512], fp32))

        C0s = sb("C0s", [P, C0W]); W0s = sb("W0s", [P, W0W])
        C1s = sb("C1s", [P, C1W]); W1s = sb("W1s", [P, W1W])
        ident = C0s[:, C0["ident"]]
        identr = sb("identr", [P, P], f32r)
        X = sb("X", [P, TILES, D])
        Z = sb("Z", [P, TILES, D])
        stats = sb("stats", [P, TILES, 6]); mv = sb("mv", [P, TILES, 2])
        rstd = sb("rstd", [P, TILES]); mhalf = sb("mhalf", [P, TILES]); ve = sb("ve", [P, TILES]); one = sb("one", [P, 1])
        ZT = sb("ZT", [P, B * S])
        ctxT = sb("ctxT", [P, B * KC])
        shared = sb("shared", [P, 2464 + 2560 + 3072 + 1024])
        Kf = shared[0:96, 0:2464].rearrange("p (g b i k) -> p g b i k", g=G0, b=B, i=GH)
        Vaug = shared[:, 2464:5024].rearrange("p (b s n) -> p b s n", b=B, s=2)
        PT = shared[:, 5024:8096].rearrange("p (u j n) -> p u j n", u=3, j=2)
        Osb = shared[0:72, 8096:9120].rearrange("p (s n) -> p s n", s=2)
        Gbc = shared[:, 0:E * B * S].rearrange("p (e n) -> p e n", e=E)
        Kaug = sb("Kaug", [P, G0, B, GH * KC], f32r)
        Qaug = sb("Qaug", [P, B, G0, S], f32r)
        negm = sb("negm", [P, 2, G0, GH])
        mcat = sb("mcat", [P, B, NT, P], f32r)
        rs = sb("rs", [P, 2, NT, SH])
        On = sb("On", [P, NT, D])
        OnT = sb("OnT", [P, S])

        Zhi = sb("Zhi", [P, B * S], f32r); Zlo = sb("Zlo", [P, B * S], f32r)
        Wraw = sb("Wraw", [P, 2, 2 * F]); Whi = sb("Whi", [P, 2, 2 * F], f32r); Wlo = sb("Wlo", [P, 2, 2 * F], f32r)
        Sf = sb("Sf", [P, LAG, S])
        Hhi = Qaug[:, :, :, :].rearrange("p b g n -> p (b g) n")
        Hlo = sb("Hlo", [P, NH, S], f32r)
        Lg = sb("Lg", [P, TILES, E]); top = sb("top", [P, 2, TILES]); tie = sb("tie", [P, TILES, E]); tiem = sb("tiem", [P, TILES])
        pick = sb("pick", [P, 2, TILES, E]); gw = sb("gw", [P, 3, TILES]); gate = sb("gate", [P, TILES, E])
        gcat = sb("gcat", [P, TILES, 2 * E], f32r); gT = sb("gT", [2 * E, B * S], f32r)
        gsel = sb("gsel", [2 * E, E * P], f32r)
        Yg = sb("Yg", [P, S]); Yacc = sb("Yacc", [P, B * S])

        ctxn = sb("ctxn", [KC, B, D]); cstat = sb("cstat", [KC, B]); crms = sb("crms", [KC, B]); mn = sb("mn", [KC, B, D])
        mnT = sb("mnT", [P, B, KC]); Kr = sb("Kr", [P, 2, B, KC]); Kb = sb("Kb", [P, B, H1, KC])
        Kbhi = sb("Kbhi", [P, B, H1 * KC], f32r); Kblo = sb("Kblo", [P, B, H1 * KC], f32r)
        V1aug = sb("V1aug", [P, B, 2, 132])
        maskw = sb("maskw", [1, B * KCP // 4], mybir.dt.uint32); keep = sb("keep", [1, B, KC]); anyk = sb("anyk", [1, B])
        fill = sb("fill", [1, B, H1 * KC], f32r); onesf = sb("onesf", [1, P]); onesr = sb("onesr", [1, P], f32r)
        escale = sb("escale", [KC, B]); ebias = sb("ebias", [KC, B])
        selm = sb("selm", [2 * H1, H1 * KC], f32r)
        negm1 = sb("negm1", [P, B, NT, H1]); mcat1 = sb("mcat1", [P, B, NT, 2 * H1], f32r); M1T = sb("M1T", [2 * H1, B, S], f32r)
        Qr = Sf[:, :, :].rearrange("p (b n) s -> p b (n s)", b=B)
        Q1hi, Q1lo = Zhi, Zlo
        PT1 = Wraw
        Osb1 = shared[0:66, 0:2048].rearrange("p (b s n) -> p b s n", b=B, s=2)
        On1 = shared[:, 2048:3072].rearrange("p (b t n) -> p b t n", b=B, t=NT)
        OnT1 = shared[:, 3072:4096].rearrange("p (b n) -> p b n", b=B)
        rs1 = sb("rs1", [P, B, 2, NT, 2])
        at = 4096
        def view(*shape):
            nonlocal at
            n = int(np.prod(shape))
            names = " ".join("abcd"[:len(shape)])
            v = shared[:, at:at + n].rearrange(f"p ({names}) -> p {names}", **dict(zip("abcd", shape))) if len(shape) > 1 else shared[:, at:at + n]
            at += n
            return v
        pj = view(B, NT, PROJ); dn = view(B, NT, RSUM); sq = view(B, NT, E1, PROJ); ss = view(B, NT); rn = view(B, NT)
        lg = view(B, NT, E1); mx = view(B, NT); ex = view(B, NT, E1); lw = view(B, NT); eq = view(B, NT, E1); gdT = view(B, S)
        simn = sb("simn", [P, E1, PROJ]); simq = sb("simq", [P, E1, PROJ]); sims = sb("sims", [P, E1]); tscale = sb("tscale", [P, 1])

        ld_ctxn = sem("ld_ctxn"); ld_mask = sem("ld_mask"); ld_v1 = sem("ld_v1")
        c_ss = sem("c_ss"); c_rms = sem("c_rms"); mn_ok = sem("mn_ok"); mn_ps = sem("mn_ps"); mnt_ok = sem("mnt_ok")
        kv1_ps = sem("kv1_ps"); v1_ok = sem("v1_ok"); k1_ok = sem("k1_ok"); w1s_ok = sem("w1s_ok")
        keep_ok = sem("keep_ok"); keep_ps = sem("keep_ps"); emask_ok = sem("emask_ok"); selm_ok = sem("selm_ok")
        sim_ss = sem("sim_ss"); sim_rn = sem("sim_rn"); t_min = sem("t_min"); t_exp = sem("t_exp")
        var2_ok = sem("var2_ok"); rms_ok = sem("rms_ok")
        q1_ps = sem("q1_ps"); q1_rot = sem("q1_rot"); q1_hi = sem("q1_hi"); q1_ok = sem("q1_ok")
        nat1_ps = sem("nat1_ps"); nat1_max = sem("nat1_max"); m1_cat = sem("m1_cat"); m1_ps = sem("m1_ps"); m1_ok = sem("m1_ok")
        sc1_ps = sem("sc1_ps"); exp1_ok = sem("exp1_ok"); pv1_ok = sem("pv1_ok"); acc1_sb = sem("acc1_sb")
        on1_ps = sem("on1_ps"); on1_ok = sem("on1_ok"); ont1_ps = sem("ont1_ps"); ont1_ok = sem("ont1_ok"); proj1_ps = sem("proj1_ps")
        pd_ps = sem("pd_ps"); pss_ok = sem("pss_ok"); prn_ok = sem("prn_ok"); d_ok = sem("d_ok"); ex_ok = sem("ex_ok")
        gd_ok = sem("gd_ok"); gd_ps = sem("gd_ps"); gdt_ok = sem("gdt_ok"); f_ps = sem("f_ps")
        ld_moe = [sem(f"ld_moe{k}") for k in range(2)]
        w_hi = sem("w_hi"); w_ok = sem("w_ok"); z_hi = sem("z_hi"); zsplit_ok = sem("zsplit_ok")
        lg_ps = sem("lg_ps"); margin = sem("margin"); e_ok = sem("e_ok"); gcat_ok = sem("gcat_ok"); gt_ps = sem("gt_ps"); gt_ok = sem("gt_ok")
        gb_ps = sem("gb_ps"); gb_act = sem("gb_act"); gb_dve = sem("gb_dve"); gsel_ok = sem("gsel_ok")
        h_ps = sem("h_ps"); silu_ok = sem("silu_ok"); h_hi = sem("h_hi"); h_ok = sem("h_ok"); down_ok = sem("down_ok")
        y_used = sem("y_used"); y_added = sem("y_added"); y_ps = sem("y_ps")
        ld_x = [sem(f"ld_x{b}") for b in range(B)]
        ld_ctx = sem("ld_ctx"); ld_c0 = sem("ld_c0"); ld_w0 = sem("ld_w0"); ld_v = sem("ld_v")
        ld_c1 = sem("ld_c1"); ld_w1 = sem("ld_w1")
        consts = sem("consts"); kones = sem("kones"); dve_step = sem("dve_step"); pool_step = sem("pool_step")
        stats_ok = sem("stats_ok"); rstd_ok = sem("rstd_ok"); z_ok = sem("z_ok")
        zt_ps = sem("zt_ps"); zt_ok = sem("zt_ok")
        k_ps = sem("k_ps"); k_full = sem("k_full"); k_hi = sem("k_hi"); k_ok = sem("k_ok")
        v_ps = sem("v_ps"); v_ok = sem("v_ok")
        q_ps = sem("q_ps"); q_hi = sem("q_hi"); q_ok = sem("q_ok")
        nat_ps = sem("nat_ps"); nat_max = sem("nat_max"); m_cat = sem("m_cat"); m_ps = sem("m_ps"); m_ok = sem("m_ok")
        sc_ps = sem("sc_ps"); exp_ok = sem("exp_ok"); pv_ok = sem("pv_ok")
        acc_sb = sem("acc_sb"); on_ps = sem("on_ps"); on_ok = sem("on_ok")
        ont_ps = sem("ont_ps"); ont_ok = sem("ont_ok"); proj_ps = sem("proj_ps"); x_ok = sem("x_ok")
        stored = sem("stored")

        x_d = x.rearrange("b (t p) d -> p (b t) d", p=P)
        out_d = out.rearrange("b (t p) d -> p (b t) d", p=P)
        block = ctx.enter_context(nc.Block())

        def tiles(b):
            return slice(b * NT, (b + 1) * NT)

        @block.sync
        def _(sp):
            sp.dma_start(X[:, tiles(0), :], x_d[:, tiles(0), :]).then_inc(ld_x[0], 16)
            sp.dma_start(W0s[:, :], w0).then_inc(ld_w0, 16)
            sp.dma_start(X[:, tiles(1), :], x_d[:, tiles(1), :]).then_inc(ld_x[1], 16)
            for b in range(B):
                sp.dma_start(Vaug[:, b, :, :], c0[:, C0["vpat"]].rearrange("p (s n) -> p s n", s=2)).then_inc(ld_v, 16)
            sp.dma_start(C1s[:, :], c1).then_inc(ld_c1, 16)
            sp.dma_start(W1s[:, :], w1).then_inc(ld_w1, 16)
            sp.dma_start(ctxn[:, :, :], ctx_nat).then_inc(ld_ctxn, 16)
            sp.dma_start(maskw[:, :], mask).then_inc(ld_mask, 16)
            for b in range(B):
                sp.dma_start(V1aug[:, b, :, :], c1[:, C1["vpat"]].rearrange("p (s n) -> p s n", s=2)).then_inc(ld_v1, 16)
            for k in range(2):
                sp.dma_start(Wraw[:, k, :], moe[k]).then_inc(ld_moe[k], 16)
            with sp.Fori(1, PAIRS) as i:
                for k in range(2):
                    sp.wait_ge(w_ok, 2 * i + k - 1)
                    sp.dma_start(Wraw[:, k, :], moe[2 * i + k]).then_inc(ld_moe[k], 16)
            for b in range(B):
                sp.wait_ge(x_ok, 7 + b)
                sp.dma_start(out_d[:, tiles(b), :], X[:, tiles(b), :]).then_inc(stored, 16)
            sp.wait_ge(stored, 16 * B)

        @block.gpsimd
        def _(pool):
            def link(ins, count=[0]):
                count[0] += 1
                ins.then_inc(pool_step, 1)
                pool.wait_ge(pool_step, count[0])

            link(nc.gpsimd.memset(mhalf[:, :], -0.5))
            link(nc.gpsimd.memset(one[:, :], 1.0))
            link(nc.gpsimd.memset(PT[:, :, :, :], 0.0))
            nc.gpsimd.memset(mcat[:, :, :, :].bitcast(fp32), 0.0).then_inc(consts, 1)
            pool.wait_ge(ld_c0, 16)
            pool.wait_ge(consts, 1)
            nc.gpsimd.tensor_copy(identr[:, :], ident).then_inc(consts, 1)
            pool.wait_ge(consts, 2)
            for b in range(B):
                pool.wait_ge(stats_ok, b + 1)
                if b:
                    pool.wait_ge(rstd_ok, b)
                nc.gpsimd.tensor_tensor(rstd[:, tiles(b)], ve[:, tiles(b)], mhalf[:, tiles(b)], ALU.pow).then_inc(rstd_ok, 1)
            pool.wait_ge(rstd_ok, B)
            for b in range(B):
                if b:
                    pool.wait_ge(kones, b)
                nc.gpsimd.tensor_copy(Kaug[96:P, :, b, :],
                                      C0s[96:P, C0["ones"]].unsqueeze(1).broadcast_to([32, G0, GH * KC])).then_inc(kones, 1)

            pool.wait_ge(kones, B)
            pool.wait_ge(ld_c1, 16)
            nc.gpsimd.tensor_copy(gsel[:, :], C1s[0:2 * E, C1["gsel"]]).then_inc(gsel_ok, 1)
            pool.wait_ge(gsel_ok, 1)

            def split_weights(i, k, first):
                pool.wait_ge(ld_moe[k], 16 * i + 16)
                if not first:
                    pool.wait_ge(down_ok, US * i + UE * (k - 1))
                nc.gpsimd.tensor_tensor(Whi[:, k, :], Wraw[:, k, :], one[:, :].broadcast_to([P, 2 * F]), ALU.mult).then_inc(w_hi, 1)
                pool.wait_ge(w_hi, 2 * i + k + 1)
                nc.gpsimd.tensor_tensor(Wlo[:, k, :], Wraw[:, k, :], Whi[:, k, :].bitcast(fp32), ALU.subtract).then_inc(w_ok, 1)
                pool.wait_ge(w_ok, 2 * i + k + 1)

            nc.gpsimd.tensor_copy(selm[:, :], C1s[0:2 * H1, C1["selm"]]).then_inc(selm_ok, 1)
            pool.wait_ge(selm_ok, 1)
            for k in range(2):
                split_weights(0, k, True)
            pool.wait_ge(c_ss, 1)
            nc.gpsimd.tensor_tensor(crms[:, :], cstat[:, :], mhalf[0:KC, 0:B], ALU.pow).then_inc(c_rms, 1)
            pool.wait_ge(c_rms, 1)
            pool.wait_ge(sim_ss, 1)
            nc.gpsimd.tensor_tensor(sims[:, :], sims[:, :], mhalf[:, 0:E1], ALU.pow).then_inc(sim_rn, 1)
            pool.wait_ge(sim_rn, 1)
            for b in range(B):
                pool.wait_ge(stats_ok, B + b + 1)
                nc.gpsimd.tensor_tensor(rstd[:, tiles(b)], ve[:, tiles(b)], mhalf[:, tiles(b)], ALU.pow).then_inc(rstd_ok, 1)
                pool.wait_ge(rstd_ok, B + b + 1)
            with pool.Fori(1, PAIRS) as i:
                for k in range(2):
                    split_weights(i, k, False)
            for b in range(B):
                pool.wait_ge(stats_ok, 2 * B + b + 1)
                nc.gpsimd.tensor_tensor(rstd[:, tiles(b)], ve[:, tiles(b)], mhalf[:, tiles(b)], ALU.pow).then_inc(rstd_ok, 1)
                pool.wait_ge(rstd_ok, 2 * B + b + 1)
            for b in range(B):
                pool.wait_ge(var2_ok, b + 1)
                nc.gpsimd.tensor_tensor(ve[:, tiles(b)], ve[:, tiles(b)], mhalf[:, tiles(b)], ALU.pow).then_inc(rms_ok, 1)
                pool.wait_ge(rms_ok, b + 1)
            for b in range(B):
                pool.wait_ge(stats_ok, 3 * B + b + 1)
                nc.gpsimd.tensor_tensor(rstd[:, tiles(b)], ve[:, tiles(b)], mhalf[:, tiles(b)], ALU.pow).then_inc(rstd_ok, 1)
                pool.wait_ge(rstd_ok, 3 * B + b + 1)
            for b in range(B):
                pool.wait_ge(pss_ok, b + 1)
                nc.gpsimd.tensor_tensor(rn[:, b, :], ss[:, b, :], mhalf[:, 0:NT], ALU.pow).then_inc(prn_ok, 1)
                pool.wait_ge(prn_ok, b + 1)

        @block.scalar
        def _(act):
            act.dma_start(ctxT[:, :], ctx_t).then_inc(ld_ctx, 16)
            act.dma_start(C0s[:, :], c0).then_inc(ld_c0, 16)

            def zt_copy(b, n):
                act.wait_ge(zt_ps, n)
                nc.scalar.activation(ZT[:, b * S:(b + 1) * S], PS[:, 0, :], ACT.Copy).then_inc(zt_ok, 1)

            def q_high(b, g):
                act.wait_ge(q_ps, G0 * b + g + 1)
                nc.scalar.activation(Qaug[0:96, b, g, :], PS[0:96, (1, 2, 3, 0)[g], :], ACT.Copy).then_inc(q_hi, 1)

            def m_rows(b):
                act.wait_ge(m_ps, b + 1)
                for g in range(G0):
                    nc.scalar.activation(Qaug[96:P, b, g, :], PS[32 * g:32 * g + 32, 4, :], ACT.Copy).then_inc(m_ok, 1)

            def exps(b, hp):
                u = 8 * b + hp
                act.wait_ge(sc_ps, u + 1)
                if u >= 3:
                    act.wait_ge(pv_ok, u - 2)
                bank = 2 * (u % 2)
                nc.scalar.activation(PT[0:KC, u % 3, :, :], PS[0:KC, bank:bank + 2, :], ACT.Exp,
                                     scale=float(HD0) ** -0.5).then_inc(exp_ok, 1)

            def acc_copy(b, s):
                act.wait_ge(pv_ok, 8 * b + 4 * (s + 1))
                if b:
                    act.wait_ge(on_ps, 2 * (b - 1) + s + 1)
                nc.scalar.activation(Osb[:, s, :], PS[0:72, 6 + s, :], ACT.Copy).then_inc(acc_sb, 1)

            def z_split(b):
                act.wait_ge(zt_ps, B + b + 1)
                nc.scalar.activation(Zhi[:, b * S:(b + 1) * S], PS[:, 4 + b, :], ACT.Copy).then_inc(z_hi, 1)
                nc.scalar.activation(ZT[:, b * S:(b + 1) * S], PS[:, 4 + b, :], ACT.Copy).then_inc(zt_ok, 1)

            def finish_attention(b):
                act.wait_ge(ont_ps, b + 1)
                nc.scalar.activation(OnT[:, :], PS[:, 5, :], ACT.Copy).then_inc(ont_ok, 1)

            zt_copy(0, 1)
            for b in range(B):
                act.wait_ge(v_ps, 1)
                if b == 0:
                    act.wait_ge(ld_v, 16 * B)
                nc.scalar.activation(Vaug[0:KC, b, :, :].rearrange("p s (h c) -> p s h c", c=80)[:, :, :, 0:HD0],
                                     PS[0:KC, 5, b * D:(b + 1) * D].rearrange("p (s h c) -> p s h c", s=2, c=HD0),
                                     ACT.Copy).then_inc(v_ok, 1)
            for g in range(G0):
                q_high(0, g)
            act.wait_ge(k_full, G0)
            nc.scalar.activation(Kaug[0:96, :, :, :], Kf[:, :, :, :, :].rearrange("p g b i k -> p g b (i k)"), ACT.Copy).then_inc(k_hi, 1)
            zt_copy(1, 2)
            for g in range(G0):
                q_high(1, g)
            m_rows(0)
            for hp in range(8):
                exps(0, hp)
                if hp == 5:
                    acc_copy(0, 0)
            acc_copy(0, 1)
            m_rows(1)
            for hp in range(8):
                exps(1, hp)
                if hp == 3:
                    finish_attention(0)
                if hp == 5:
                    acc_copy(1, 0)
                if hp == 6:
                    z_split(0)
            acc_copy(1, 1)
            act.wait_ge(mn_ps, 1)
            nc.scalar.activation(mnT[:, :, :], PS[:, 0, 0:B * KC].rearrange("p (b k) -> p b k", b=B), ACT.Copy).then_inc(mnt_ok, 1)
            finish_attention(1)
            act.wait_ge(kv1_ps, 1)
            act.wait_ge(ld_v1, 16 * B)
            for b in range(B):
                nc.scalar.activation(V1aug[0:KC, b, :, :].rearrange("p s (j c) -> p s j c", j=2)[:, :, 0, 0:HD1],
                                     PS[0:KC, 2, b * HD1:(b + 1) * HD1].unsqueeze(1).broadcast_to([KC, 2, HD1]), ACT.Copy).then_inc(v1_ok, 1)
                nc.scalar.activation(V1aug[0:KC, b, :, :].rearrange("p s (j c) -> p s j c", j=2)[:, :, 1, HD1:2 * HD1],
                                     PS[0:KC, 2, b * HD1:(b + 1) * HD1].unsqueeze(1).broadcast_to([KC, 2, HD1]), ACT.Copy).then_inc(v1_ok, 1)
            act.wait_ge(t_min, 1)
            nc.scalar.activation(tscale[:, :], tscale[:, :], ACT.Exp).then_inc(t_exp, 1)
            z_split(1)
            act.wait_ge(margin, 1)
            nc.scalar.activation(gw[:, 0, :], gw[:, 0, :], ACT.Exp).then_inc(e_ok, 1)
            act.wait_ge(gt_ps, 1)
            nc.scalar.activation(gT[:, :].rearrange("p (b n) -> p b n", b=B), PS[0:2 * E, 6:8, :], ACT.Copy).then_inc(gt_ok, 1)
            for e in range(0, E, 2):
                act.wait_ge(gb_ps, e + 1)
                nc.scalar.activation(Gbc[:, e, :].rearrange("p (b n) -> p b n", b=B), PS[:, 6:8, :], ACT.Copy).then_inc(gb_act, 1)

            def hidden(i, j, first=False):
                act.wait_ge(h_ps, US * i + j + 1)
                if not (first and j < LAG):
                    act.wait_ge(h_ok, US * i + j - LAG + 1)
                nc.scalar.activation(Sf[:, j % LAG, :], PS[:, j % LAG, :], ACT.Silu).then_inc(silu_ok, 1)
                act.wait_ge(silu_ok, US * i + j + 1)
                if not (first and j < NH):
                    act.wait_ge(down_ok, US * i + j - NH + 1)
                nc.scalar.activation(Hhi[:, j % NH, :], Sf[:, j % LAG, :], ACT.Copy).then_inc(h_hi, 1)

            for j in range(US):
                hidden(0, j, True)
            with act.Fori(1, PAIRS) as i:
                for j in range(US):
                    hidden(i, j)

            for b in range(B):
                act.wait_ge(zt_ps, 2 * B + b + 1)
                nc.scalar.activation(ZT[:, b * S:(b + 1) * S], PS[:, 4 * b, :], ACT.Copy).then_inc(zt_ok, 1)
            for b in range(B):
                act.wait_ge(q1_rot, b + 1)
                nc.scalar.activation(Q1hi[:, b * S:(b + 1) * S], Qr[:, b, 0:S], ACT.Copy).then_inc(q1_hi, 1)
            for b in range(B):
                act.wait_ge(m1_ps, b + 1)
                nc.scalar.activation(M1T[:, b, :], PS[0:2 * H1, 4 * b + 1, :], ACT.Copy).then_inc(m1_ok, 1)
            act.wait_ge(emask_ok, 1)
            act.wait_ge(w_ok, E)
            for s in range(2):
                for b in range(B):
                    u = 2 * s + b
                    bank = 4 * b + 2 - 2 * s
                    act.wait_ge(sc1_ps, u + 1)
                    if s:
                        act.wait_ge(pv1_ok, u - 1)
                    nc.scalar.activation(PT1[0:KC, b, :].rearrange("p (j n) -> p j n", j=2), PS[0:KC, bank:bank + 2, :], ACT.Exp,
                                         bias=ebias[:, b:b + 1], scale=escale[:, b:b + 1]).then_inc(exp1_ok, 1)
            for s in range(2):
                for b in range(B):
                    act.wait_ge(pv1_ok, 2 * s + b + 1)
                    nc.scalar.activation(Osb1[:, b, s, :], PS[0:66, 4 * b + 2 - 2 * s, :], ACT.Copy).then_inc(acc1_sb, 1)
            for b in range(B):
                act.wait_ge(ont1_ps, b + 1)
                nc.scalar.activation(OnT1[:, b, :], PS[:, 4 * b + 1, :], ACT.Copy).then_inc(ont1_ok, 1)
            for b in range(B):
                act.wait_ge(zt_ps, 3 * B + b + 1)
                nc.scalar.activation(ZT[:, b * S:(b + 1) * S], PS[:, 4 * b, :], ACT.Copy).then_inc(zt_ok, 1)
            for b in range(B):
                act.wait_ge(d_ok, b + 1)
                nc.scalar.activation(ex[:, b, :, :], ex[:, b, :, :], ACT.Exp).then_inc(ex_ok, 1)
            for b in range(B):
                act.wait_ge(gd_ps, b + 1)
                nc.scalar.activation(gdT[0:RSUM, b, :], PS[0:RSUM, 4 * b + 2, :], ACT.Copy).then_inc(gdt_ok, 1)

        @block.vector
        def _(dve):
            def link(ins, count=[0]):
                count[0] += 1
                ins.then_inc(dve_step, 1)
                dve.wait_ge(dve_step, count[0])

            def norm_stats(b):
                for t in range(b * NT, (b + 1) * NT):
                    last = nc.vector.bn_stats(stats[:, t, :], X[:, t, :])
                link(last)
                for t in range(b * NT, (b + 1) * NT):
                    last = nc.vector.bn_aggr(mv[:, t, :], stats[:, t, :])
                link(last)
                nc.vector.tensor_scalar_add(ve[:, tiles(b)], mv[:, tiles(b), 1], 1e-5).then_inc(stats_ok, 1)

            def norm_apply(b, n):
                dve.wait_ge(rstd_ok, n)
                for t in range(b * NT, (b + 1) * NT):
                    last = nc.vector.tensor_scalar(Z[:, t, :], X[:, t, :], mv[:, t, 0:1], rstd[:, t:t + 1],
                                                   ALU.subtract, ALU.mult)
                last.then_inc(z_ok, 1)

            def q_low(b, g):
                dve.wait_ge(q_hi, G0 * b + g + 1)
                lo = Qaug[32:64, b, g, :]
                nc.vector.tensor_tensor(lo, PS[32:64, (1, 2, 3, 0)[g], :], lo.bitcast(fp32), ALU.subtract).then_inc(q_ok, 1)

            def nat(b, n):
                u = 8 * b + n
                t, gp = n // 2, n % 2
                bank = (4, 6)[n % 2] if b == 0 else 4
                dve.wait_ge(nat_ps, u + 1)
                nc.vector.tensor_reduce(negm[:, b, 2 * gp:2 * gp + 2, :],
                                        PS[:, bank:bank + 2, 0:GH * KC].rearrange("p g (i k) -> p g i k", i=GH),
                                        AX.X, ALU.max, negate=True).then_inc(nat_max, 1)
                if gp:
                    dve.wait_ge(nat_max, u + 1)
                    if u == 1:
                        dve.wait_ge(consts, 2)
                    parts = mcat[:, b, t, :].rearrange("p (g c) -> p g c", g=G0)
                    link(nc.vector.tensor_copy(parts[:, :, 0:GH], negm[:, b, :, :]))
                    ins = nc.vector.tensor_tensor(parts[:, :, GH:2 * GH], negm[:, b, :, :],
                                                  parts[:, :, 0:GH].bitcast(fp32), ALU.subtract)
                    link(ins)

            def normalise(b, s):
                dve.wait_ge(on_ps, 2 * b + s + 1)
                got = PS[:, 5, 0:NT * 72].rearrange("p (t c) -> p t c", c=72)
                link(nc.vector.reciprocal(rs[:, s, :, :], got[:, :, 64:72]))
                if b and not s:
                    dve.wait_ge(ont_ps, b)
                nc.vector.tensor_tensor(On[:, :, 64 * s:64 * s + 64].rearrange("p t (h d) -> p t h d", d=HD0),
                                        got[:, :, 0:64].rearrange("p t (h d) -> p t h d", d=HD0),
                                        rs[:, s, :, :].unsqueeze(3).broadcast_to([P, NT, SH, HD0]), ALU.mult).then_inc(on_ok, 1)

            def z_low(b):
                dve.wait_ge(z_hi, b + 1)
                dve.wait_ge(zt_ok, B + b + 1)
                nc.vector.tensor_tensor(Zlo[:, b * S:(b + 1) * S], PS[:, 4 + b, :], Zhi[:, b * S:(b + 1) * S].bitcast(fp32),
                                        ALU.subtract).then_inc(zsplit_ok, 1)

            def residual(b):
                dve.wait_ge(proj_ps, b + 1)
                nc.vector.tensor_tensor(X[:, tiles(b), :], PS[:, 4, :].rearrange("p (t d) -> p t d", d=D),
                                        X[:, tiles(b), :], ALU.add).then_inc(x_ok, 1)

            def prepare_second():
                dve.wait_ge(ld_ctxn, 16)
                link(nc.vector.tensor_tensor(mn[:, :, :], ctxn[:, :, :], ctxn[:, :, :], ALU.mult))
                link(nc.vector.reduce_sum(cstat[:, :], mn[:, :, :], AX.X))
                nc.vector.tensor_scalar(cstat[:, :], cstat[:, :], 1.0 / D, 1e-6, ALU.mult, ALU.add).then_inc(c_ss, 1)
                dve.wait_ge(ld_w1, 16)
                sim = W1s[:, W1["sim"]].rearrange("p (e n) -> p e n", e=E1)
                link(nc.vector.tensor_tensor(simq[:, :, :], sim, sim, ALU.mult))
                link(nc.vector.reduce_sum(sims[:, :], simq[:, :, :], AX.X))
                nc.vector.tensor_scalar_max(sims[:, :], sims[:, :], 1e-24).then_inc(sim_ss, 1)
                nc.vector.tensor_scalar_min(tscale[:, :], W1s[:, W1["temp"]], CLAMP).then_inc(t_min, 1)
                link(nc.vector.tensor_scalar_add(W1s[:, W1["rms"]], W1s[:, W1["rms"]], 1.0))
                scaled = W1s[:, W1["q"].start:W1["v"].stop]
                nc.vector.tensor_scalar(scaled, scaled, W1s[:, W1["rms"]], None, ALU.mult).then_inc(w1s_ok, 1)
                dve.wait_ge(ld_mask, 16)
                link(nc.vector.tensor_copy(keep[:, :, :], maskw[:, :].bitcast(u8).rearrange("p (b k) -> p b k", b=B)[:, :, 0:KC]))
                link(nc.vector.memset(onesf[:, :], 1.0))
                link(nc.vector.tensor_copy(onesr[:, :], onesf[:, :]))
                link(nc.vector.tensor_scalar(fill[:, :, :].rearrange("p b (i k) -> p b i k", i=H1), keep[:, :, :].unsqueeze(2).broadcast_to([1, B, H1, KC]),
                                             -1.0, -NEVER, ALU.add, ALU.mult))
                nc.vector.reduce_max(anyk[:, :], keep[:, :, :], AX.X).then_inc(keep_ok, 1)
                dve.wait_ge(c_rms, 1)
                for b in range(B):
                    last = nc.vector.tensor_scalar(mn[:, b, :], ctxn[:, b, :], crms[:, b:b + 1], None, ALU.mult)
                last.then_inc(mn_ok, 1)

            def prepare_keys():
                dve.wait_ge(kv1_ps, 1)
                dve.wait_ge(ld_c1, 16)
                for n, table in enumerate(("kcos", "ksin")):
                    last = nc.vector.tensor_tensor(Kr[:, n, :, :], PS[:, 1, n * B * KC:(n + 1) * B * KC].rearrange("p (b k) -> p b k", b=B),
                                                   C1s[:, C1[table]].unsqueeze(1).broadcast_to([P, B, KC]), ALU.mult)
                link(last)
                link(nc.vector.tensor_tensor(Kr[:, 0, :, :], Kr[:, 0, :, :], Kr[:, 1, :, :], ALU.add))
                link(nc.vector.tensor_tensor(Kb[:, :, :, :], Kr[:, 0, :, :].unsqueeze(2).broadcast_to([P, B, H1, KC]),
                                             C1s[:, C1["block"]].rearrange("p (i k) -> p i k", i=H1).unsqueeze(1).broadcast_to([P, B, H1, KC]), ALU.mult))
                whole = Kb[:, :, :, :].rearrange("p b i k -> p b (i k)")
                link(nc.vector.tensor_copy(Kbhi[:, :, :], whole))
                nc.vector.tensor_tensor(Kblo[:, :, :], whole, Kbhi[:, :, :].bitcast(fp32), ALU.subtract).then_inc(k1_ok, 1)
                link(nc.vector.tensor_copy(escale[:, :], PS[0:KC, 3, 0:B]))
                link(nc.vector.tensor_tensor(ebias[:, :], escale[:, :], PS[0:KC, 3, B:2 * B], ALU.subtract))
                link(nc.vector.tensor_scalar(ebias[:, :], ebias[:, :], -NEVER, None, ALU.mult))
                nc.vector.tensor_scalar(escale[:, :], escale[:, :], float(HD1) ** -0.5, None, ALU.mult).then_inc(emask_ok, 1)
                dve.wait_ge(sim_rn, 1)
                dve.wait_ge(t_exp, 1)
                link(nc.vector.tensor_scalar(sims[:, :], sims[:, :], tscale[:, :], None, ALU.mult))
                link(nc.vector.tensor_tensor(simn[:, :, :], W1s[:, W1["sim"]].rearrange("p (e n) -> p e n", e=E1),
                                             sims[:, :].unsqueeze(2).broadcast_to([P, E1, PROJ]), ALU.mult))

            dve.wait_ge(ld_x[0], 16)
            norm_stats(0)
            norm_apply(0, 1)
            for g in range(G0):
                dve.wait_ge(k_ps, g // 2 + 1)
                if g == 0:
                    dve.wait_ge(ld_c0, 16)
                src = PS[0:96, 6 + g // 2, (g % 2) * B * KC:(g % 2 + 1) * B * KC].rearrange("p (b k) -> p b k", b=B)
                nc.vector.tensor_tensor(Kf[:, g, :, :, :], src.unsqueeze(2).broadcast_to([96, B, GH, KC]),
                                        C0s[0:96, C0["block"]].rearrange("p (i k) -> p i k", i=GH).unsqueeze(1)
                                        .broadcast_to([96, B, GH, KC]), ALU.mult).then_inc(k_full, 1)
            dve.wait_ge(ld_x[1], 16)
            norm_stats(1)
            norm_apply(1, 2)
            for g in range(G0):
                q_low(0, g)
            dve.wait_ge(k_hi, 1)
            lo = Kaug[64:96, :, :, :]
            dve.wait_ge(k_full, G0)
            nc.vector.tensor_tensor(lo, Kf[64:96, :, :, :, :].rearrange("p g b i k -> p g b (i k)"), lo.bitcast(fp32), ALU.subtract).then_inc(k_ok, 1)
            for n in range(8):
                nat(0, n)
                if n % 2:
                    q_low(1, n // 2)
            nc.vector.tensor_copy(stats[:, 0, 0:1], mhalf[:, 0:1]).then_inc(m_cat, 1)
            for n in range(8):
                nat(1, n)
            nc.vector.tensor_copy(stats[:, 0, 1:2], mhalf[:, 0:1]).then_inc(m_cat, 1)
            prepare_second()
            normalise(0, 0)
            normalise(0, 1)
            residual(0)
            dve.wait_ge(x_ok, 1)
            norm_stats(0)
            norm_apply(0, 3)
            normalise(1, 0)
            z_low(0)
            normalise(1, 1)
            residual(1)
            prepare_keys()
            dve.wait_ge(x_ok, 2)
            norm_stats(1)
            norm_apply(1, 4)
            z_low(1)

            def bc(ap):
                return ap.unsqueeze(2).broadcast_to([P, TILES, E])

            dve.wait_ge(lg_ps, 2)
            dve.wait_ge(ld_c1, 16)
            link(nc.vector.tensor_copy(Lg[:, :, :], PS[:, 6, 0:TILES * E].rearrange("p (t e) -> p t e", e=E)))
            for n in range(2):
                link(nc.vector.tensor_reduce(top[:, n, :], Lg[:, :, :], AX.X, ALU.max))
                link(nc.vector.tensor_tensor(tie[:, :, :], Lg[:, :, :], bc(top[:, n, :]), ALU.is_equal))
                link(nc.vector.tensor_tensor(tie[:, :, :], tie[:, :, :], C1s[:, C1["tie8"]].unsqueeze(1).broadcast_to([P, TILES, E]), ALU.mult))
                link(nc.vector.tensor_reduce(tiem[:, :], tie[:, :, :], AX.X, ALU.max))
                link(nc.vector.tensor_tensor(pick[:, n, :, :], tie[:, :, :], bc(tiem[:, :]), ALU.is_equal))
                if n == 0:
                    link(nc.vector.scalar_tensor_tensor(Lg[:, :, :], pick[:, 0, :, :], -3.0e38, Lg[:, :, :], ALU.mult, ALU.add))
            nc.vector.tensor_tensor(gw[:, 0, :], top[:, 1, :], top[:, 0, :], ALU.subtract).then_inc(margin, 1)
            dve.wait_ge(e_ok, 1)
            link(nc.vector.tensor_scalar_add(gw[:, 1, :], gw[:, 0, :], 1.0))
            link(nc.vector.reciprocal(gw[:, 1, :], gw[:, 1, :]))
            link(nc.vector.tensor_tensor(gw[:, 2, :], gw[:, 0, :], gw[:, 1, :], ALU.mult))
            link(nc.vector.tensor_tensor(gate[:, :, :], pick[:, 0, :, :], bc(gw[:, 1, :]), ALU.mult))
            link(nc.vector.tensor_tensor(tie[:, :, :], pick[:, 1, :, :], bc(gw[:, 2, :]), ALU.mult))
            link(nc.vector.tensor_tensor(gate[:, :, :], gate[:, :, :], tie[:, :, :], ALU.add))
            link(nc.vector.tensor_copy(gcat[:, :, 0:E], gate[:, :, :]))
            nc.vector.tensor_tensor(gcat[:, :, E:2 * E], gate[:, :, :], gcat[:, :, 0:E].bitcast(fp32), ALU.subtract).then_inc(gcat_ok, 1)
            for e in range(1, E, 2):
                dve.wait_ge(gb_ps, e + 1)
                nc.vector.tensor_copy(Gbc[:, e, :].rearrange("p (b n) -> p b n", b=B), PS[:, 6:8, :]).then_inc(gb_dve, 1)
            dve.wait_ge(gb_act, E // 2)
            dve.wait_ge(gb_dve, E // 2)
            nc.vector.memset(Yacc[:, :], 0.0).then_inc(y_used, 2)
            dve.wait_ge(y_used, 2)

            def hidden_low(i, j):
                dve.wait_ge(h_hi, US * i + j + 1)
                nc.vector.tensor_tensor(Hlo[:, j % NH, :], Sf[:, j % LAG, :], Hhi[:, j % NH, :].bitcast(fp32), ALU.subtract).then_inc(h_ok, 1)

            def gated(i, k, b):
                n = 2 * (2 * i + k) + b
                dve.wait_ge(down_ok, US * i + UE * k + FC * (b + 1))
                nc.vector.tensor_tensor(Yg[:, :], PS[:, 4 + b, :], Gbc[:, 2 * i + k, b * S:(b + 1) * S], ALU.mult).then_inc(y_used, 1)
                dve.wait_ge(y_used, n + 3)
                acc = Yacc[:, b * S:(b + 1) * S]
                nc.vector.tensor_tensor(acc, acc, Yg[:, :], ALU.add).then_inc(y_added, 1)
                dve.wait_ge(y_added, n + 1)

            def steps(i, last=False):
                for j in range(US):
                    if not (last and j + LAG >= US):
                        hidden_low(i, j + LAG)
                    if j % FC == FC - 1:
                        gated(i, j // UE, j // FC % B)

            for j in range(LAG):
                hidden_low(0, j)
            with dve.Fori(0, PAIRS - 1) as i:
                steps(i)
            steps(PAIRS - 1, True)
            for b in range(B):
                dve.wait_ge(y_ps, b + 1)
                nc.vector.tensor_tensor(X[:, tiles(b), :], PS[:, 4 * b, :].rearrange("p (t d) -> p t d", d=D),
                                        X[:, tiles(b), :], ALU.add).then_inc(x_ok, 1)

            for b in range(B):
                dve.wait_ge(x_ok, 3 + b)
                norm_stats(b)
            for b in range(B):
                dve.wait_ge(rstd_ok, 2 * B + b + 1)
                link(nc.vector.tensor_tensor(ve[:, tiles(b)], mv[:, tiles(b), 1], rstd[:, tiles(b)], ALU.mult))
                link(nc.vector.tensor_tensor(ve[:, tiles(b)], ve[:, tiles(b)], rstd[:, tiles(b)], ALU.mult))
                nc.vector.tensor_scalar_add(ve[:, tiles(b)], ve[:, tiles(b)], 1e-6).then_inc(var2_ok, 1)
            for b in range(B):
                dve.wait_ge(rms_ok, b + 1)
                link(nc.vector.tensor_tensor(rstd[:, tiles(b)], rstd[:, tiles(b)], ve[:, tiles(b)], ALU.mult))
                norm_apply(b, 2 * B + b + 1)
            for b in range(B):
                dve.wait_ge(q1_ps, b + 1)
                for n, table in enumerate(("qcos", "qsin")):
                    last = nc.vector.tensor_tensor(Qr[:, b, n * S:(n + 1) * S], PS[:, 4 * b + 1 + n, :], C1s[:, C1[table]], ALU.mult)
                link(last)
                nc.vector.tensor_tensor(Qr[:, b, 0:S], Qr[:, b, 0:S], Qr[:, b, S:2 * S], ALU.add).then_inc(q1_rot, 1)
            for b in range(B):
                dve.wait_ge(q1_hi, b + 1)
                nc.vector.tensor_tensor(Q1lo[:, b * S:(b + 1) * S], Qr[:, b, 0:S], Q1hi[:, b * S:(b + 1) * S].bitcast(fp32), ALU.subtract).then_inc(q1_ok, 1)
            for t in range(NT):
                for b in range(B):
                    u = 2 * t + b
                    dve.wait_ge(nat1_ps, u + 1)
                    nc.vector.tensor_reduce(negm1[:, b, t, :], PS[:, 4 * b + (3, 0)[t % 2], 0:H1 * KC].rearrange("p (i k) -> p i k", i=H1),
                                            AX.X, ALU.max, negate=True).then_inc(nat1_max, 1)
            for b in range(B):
                dve.wait_ge(nat1_max, 2 * NT)
                link(nc.vector.tensor_copy(mcat1[:, b, :, 0:H1], negm1[:, b, :, :]))
                nc.vector.tensor_tensor(mcat1[:, b, :, H1:2 * H1], negm1[:, b, :, :], mcat1[:, b, :, 0:H1].bitcast(fp32), ALU.subtract).then_inc(m1_cat, 1)
            for s in range(2):
                for b in range(B):
                    dve.wait_ge(on1_ps, 2 * s + b + 1)
                    got = PS[:, 4 * b + 3, 0:NT * 66].rearrange("p (t c) -> p t c", c=66)
                    link(nc.vector.reciprocal(rs1[:, b, s, :, :], got[:, :, 64:66]))
                    nc.vector.tensor_tensor(On1[:, b, :, 64 * s:64 * s + 64].rearrange("p t (h d) -> p t h d", d=HD1),
                                            got[:, :, 0:64].rearrange("p t (h d) -> p t h d", d=HD1),
                                            rs1[:, b, s, :, :].unsqueeze(3).broadcast_to([P, NT, 2, HD1]), ALU.mult).then_inc(on1_ok, 1)
            for b in range(B):
                dve.wait_ge(proj1_ps, b + 1)
                nc.vector.tensor_tensor(X[:, tiles(b), :], PS[:, 4 * b + 3, :].rearrange("p (t d) -> p t d", d=D),
                                        X[:, tiles(b), :], ALU.add).then_inc(x_ok, 1)
            for b in range(B):
                dve.wait_ge(x_ok, 5 + b)
                norm_stats(b)
            for b in range(B):
                norm_apply(b, 3 * B + b + 1)
            def bc4(ap):
                return ap.unsqueeze(2).broadcast_to([P, NT, E1])
            for b in range(B):
                dve.wait_ge(pd_ps, b + 1)
                got = PS[:, 4 * b + 1, 0:NT * (PROJ + RSUM)].rearrange("p (t c) -> p t c", t=NT)
                nc.vector.tensor_copy(dn[:, b, :, :], got[:, :, PROJ:PROJ + RSUM])
                link(nc.vector.tensor_tensor(pj[:, b, :, :], got[:, :, 0:PROJ], W1s[:, W1["bp"]].unsqueeze(1).broadcast_to([P, NT, PROJ]), ALU.add))
                link(nc.vector.tensor_tensor(sq[:, b, :, 0, :], pj[:, b, :, :], pj[:, b, :, :], ALU.mult))
                link(nc.vector.reduce_sum(ss[:, b, :], sq[:, b, :, 0, :], AX.X))
                nc.vector.tensor_scalar_max(ss[:, b, :], ss[:, b, :], 1e-24).then_inc(pss_ok, 1)
                link(nc.vector.tensor_tensor(sq[:, b, :, :, :], pj[:, b, :, :].unsqueeze(2).broadcast_to([P, NT, E1, PROJ]),
                                             simn[:, :, :].unsqueeze(1).broadcast_to([P, NT, E1, PROJ]), ALU.mult))
                link(nc.vector.reduce_sum(lg[:, b, :, :], sq[:, b, :, :, :], AX.X))
            for b in range(B):
                dve.wait_ge(prn_ok, b + 1)
                link(nc.vector.tensor_tensor(lg[:, b, :, :], lg[:, b, :, :], bc4(rn[:, b, :]), ALU.mult))
                link(nc.vector.reduce_max(mx[:, b, :], lg[:, b, :, :], AX.X))
                nc.vector.tensor_tensor(ex[:, b, :, :], lg[:, b, :, :], bc4(mx[:, b, :]), ALU.subtract).then_inc(d_ok, 1)
                link(nc.vector.tensor_tensor(eq[:, b, :, :], lg[:, b, :, :], bc4(mx[:, b, :]), ALU.is_equal))
                link(nc.vector.tensor_tensor(eq[:, b, :, :], eq[:, b, :, :], C1s[:, C1["tie4"]].unsqueeze(1).broadcast_to([P, NT, E1]), ALU.mult))
                link(nc.vector.reduce_max(mx[:, b, :], eq[:, b, :, :], AX.X))
                link(nc.vector.tensor_tensor(eq[:, b, :, :], eq[:, b, :, :], bc4(mx[:, b, :]), ALU.is_equal))
            for b in range(B):
                dve.wait_ge(ex_ok, b + 1)
                link(nc.vector.reduce_sum(lw[:, b, :], ex[:, b, :, :], AX.X))
                link(nc.vector.reciprocal(lw[:, b, :], lw[:, b, :]))
                link(nc.vector.tensor_tensor(eq[:, b, :, :], eq[:, b, :, :], bc4(lw[:, b, :]), ALU.mult))
                c = 0
                for e, r in enumerate(RANKS):
                    part = dn[:, b, :, c:c + r]
                    last = nc.vector.tensor_tensor(part, part, eq[:, b, :, e:e + 1].broadcast_to([P, NT, r]), ALU.mult)
                    c += r
                last.then_inc(gd_ok, 1)
            for b in range(B):
                dve.wait_ge(f_ps, b + 1)
                nc.vector.tensor_tensor(X[:, tiles(b), :], PS[:, 4 * b + 3, :].rearrange("p (t d) -> p t d", d=D),
                                        X[:, tiles(b), :], ALU.add).then_inc(x_ok, 1)

        @block.tensor
        def _(pe):
            def z_transposes(b, n, bank):
                pe.wait_ge(z_ok, n)
                for t in range(NT):
                    last = nc.tensor.transpose(PS[:, bank, t * P:(t + 1) * P], Z[:, b * NT + t, :], ident)
                last.then_inc(zt_ps, 1)

            def q_proj(b, g):
                pe.wait_ge(zt_ok, b + 1)
                if b:
                    pe.wait_ge(q_ok, g + 1)
                nc.tensor.matmul(PS[0:96, (1, 2, 3, 0)[g], :], W0s[:, W0["q"]][:, 96 * g:96 * g + 96],
                                 ZT[:, b * S:(b + 1) * S], start=True, stop=True).then_inc(q_ps, 1)

            def nat(b, n):
                u = 8 * b + n
                t, gp = n // 2, n % 2
                if b == 0:
                    bank = (4, 6)[n % 2]
                    if n >= 2:
                        pe.wait_ge(nat_max, n - 1)
                else:
                    bank = 4
                    pe.wait_ge(nat_max, u)
                for g in (2 * gp, 2 * gp + 1):
                    last = nc.tensor.matmul(PS[:, bank + g % 2, 0:GH * KC], Qaug[0:96, b, g, t * P:(t + 1) * P],
                                            Kaug[0:96, g, b, :], start=True, stop=True)
                last.then_inc(nat_ps, 1)

            def m_transposes(b):
                pe.wait_ge(m_cat, b + 1)
                for t in range(NT):
                    last = nc.tensor.matmul(PS[:, 4, t * P:(t + 1) * P], mcat[:, b, t, :], identr[:, :], start=True, stop=True)
                last.then_inc(m_ps, 1)

            def scores(b, hp):
                u = 8 * b + hp
                if hp % 2 == 0:
                    pe.wait_ge(m_ok, G0 * b + hp // 2 + 1)
                if u >= 2:
                    pe.wait_ge(exp_ok, u - 1)
                for j in range(2):
                    h = 2 * hp + j
                    g, i = h // GH, h % GH
                    last = nc.tensor.matmul(PS[0:KC, 2 * (u % 2) + j, :], Kaug[:, g, b, i * KC:(i + 1) * KC],
                                            Qaug[:, b, g, :], start=True, stop=True)
                last.then_inc(sc_ps, 1)

            def values(b, hp):
                u = 8 * b + hp
                s = hp // 4
                pe.wait_ge(exp_ok, u + 1)
                if b and hp % 4 == 0:
                    pe.wait_ge(acc_sb, 2 * (b - 1) + s + 1)
                for j in range(2):
                    h = 2 * (hp % 4) + j
                    last = nc.tensor.matmul(PS[0:72, 6 + s, :], Vaug[:, b, s, 72 * h:72 * h + 72], PT[:, u % 3, j, :],
                                            start=(h == 0), stop=(h == SH - 1))
                last.then_inc(pv_ok, 1)

            def out_transposes(b, s):
                pe.wait_ge(acc_sb, 2 * b + s + 1)
                if 2 * b + s:
                    pe.wait_ge(on_ok, 2 * b + s)
                    if b and not s:
                        pe.wait_ge(ont_ok, b)
                for t in range(NT):
                    last = nc.tensor.transpose(PS[:, 5, 72 * t:72 * t + 72], Osb[:, s, t * P:(t + 1) * P], ident[0:72, 0:72])
                last.then_inc(on_ps, 1)

            def out_back(b):
                pe.wait_ge(on_ok, 2 * b + 2)
                for t in range(NT):
                    last = nc.tensor.transpose(PS[:, 5, t * P:(t + 1) * P], On[:, t, :], ident)
                last.then_inc(ont_ps, 1)

            def out_proj(b):
                pe.wait_ge(ont_ok, b + 1)
                for t in range(NT):
                    last = nc.tensor.matmul(PS[:, 4, t * P:(t + 1) * P], OnT[:, t * P:(t + 1) * P], W0s[:, W0["o"]],
                                            start=True, stop=True)
                last.then_inc(proj_ps, 1)

            pe.wait_ge(ld_w0, 16)
            pe.wait_ge(ld_ctx, 16)
            for g in range(G0):
                last = nc.tensor.matmul(PS[0:96, 6 + g // 2, (g % 2) * B * KC:(g % 2 + 1) * B * KC],
                                        W0s[:, W0["k"]][:, 96 * g:96 * g + 96], ctxT[:, :], start=True, stop=True)
                if g % 2:
                    last.then_inc(k_ps, 1)
            for b in range(B):
                last = nc.tensor.matmul(PS[0:KC, 5, b * D:(b + 1) * D], ctxT[:, b * KC:(b + 1) * KC], W0s[:, W0["v"]],
                                        start=True, stop=True)
            last.then_inc(v_ps, 1)
            pe.wait_ge(ld_c0, 16)
            z_transposes(0, 1, 0)
            for g in range(G0):
                q_proj(0, g)
            pe.wait_ge(q_ok, G0)
            z_transposes(1, 2, 0)
            pe.wait_ge(k_ok, 1)
            pe.wait_ge(v_ok, B)
            for n in range(8):
                nat(0, n)
                if n % 2:
                    q_proj(1, n // 2)
            m_transposes(0)
            pe.wait_ge(q_ok, 2 * G0)
            pe.wait_ge(kones, B)
            for hp in range(8):
                scores(0, hp)
                if hp == 0:
                    pe.wait_ge(m_ok, G0)
                nat(1, hp)
                if hp:
                    values(0, hp - 1)
            values(0, 7)
            m_transposes(1)
            for hp in range(8):
                scores(1, hp)
                if hp:
                    values(1, hp - 1)
                if hp == 0:
                    out_transposes(0, 0)
                if hp == 1:
                    out_transposes(0, 1)
                if hp == 2:
                    out_back(0)
                if hp == 3:
                    pe.wait_ge(m_ok, 2 * G0)
                    out_proj(0)
                if hp == 6:
                    pe.wait_ge(x_ok, 1)
                    z_transposes(0, 3, 4)
            values(1, 7)
            pe.wait_ge(mn_ok, 1)
            pe.wait_ge(exp_ok, 16)
            for b in range(B):
                last = nc.tensor.transpose(PS[:, 0, b * KC:(b + 1) * KC], mn[:, b, :], ident[0:KC, 0:KC])
            last.then_inc(mn_ps, 1)
            out_transposes(1, 0)
            out_transposes(1, 1)
            pe.wait_ge(keep_ok, 1)
            for b in range(B):
                nc.tensor.matmul(PS[0:KC, 3, b:b + 1], keep[:, b, :], onesf[:, 0:1], start=True, stop=True)
            nc.tensor.matmul(PS[0:KC, 3, B:2 * B], onesf[:, 0:KC], anyk[:, :], start=True, stop=True)
            pe.wait_ge(w1s_ok, 1)
            pe.wait_ge(mnt_ok, 1)
            for n, name in enumerate(("k", "krot")):
                nc.tensor.matmul(PS[:, 1, n * B * KC:(n + 1) * B * KC], W1s[:, W1[name]], mnT[:, :, :].rearrange("p b k -> p (b k)"), start=True, stop=True)
            for b in range(B):
                last = nc.tensor.matmul(PS[0:KC, 2, b * HD1:(b + 1) * HD1], mnT[:, b, :], W1s[:, W1["v"]], start=True, stop=True)
            last.then_inc(kv1_ps, 1)
            out_back(1)
            pe.wait_ge(zsplit_ok, 1)
            out_proj(1)
            pe.wait_ge(ont_ok, 2)
            z_transposes(1, 4, 5)

            def router(b):
                pe.wait_ge(zt_ok, B + b + 1)
                for t in range(b * NT, (b + 1) * NT):
                    last = nc.tensor.matmul(PS[:, 6, t * E:(t + 1) * E], ZT[:, t * P:(t + 1) * P], W1s[:, W1["r"]], start=True, stop=True)
                last.then_inc(lg_ps, 1)

            pe.wait_ge(acc_sb, 4)
            router(0)
            router(1)
            pe.wait_ge(gcat_ok, 1)
            for t in range(TILES):
                last = nc.tensor.matmul(PS[0:2 * E, 6 + t // NT, t % NT * P:(t % NT + 1) * P], gcat[:, t, :], identr[:, :], start=True, stop=True)
            last.then_inc(gt_ps, 1)
            pe.wait_ge(gt_ok, 1)
            pe.wait_ge(gsel_ok, 1)
            for e in range(E):
                if e:
                    pe.wait_ge(gb_dve if e % 2 == 0 else gb_act, (e + 1) // 2)
                for b in range(B):
                    last = nc.tensor.matmul(PS[:, 6 + b, :], gsel[:, e * P:(e + 1) * P], gT[:, b * S:(b + 1) * S], start=True, stop=True)
                last.then_inc(gb_ps, 1)

            def three(to, w, c, right_hi, right_lo, start, stop):
                hi, lo = Whi[:, w, c * P:(c + 1) * P], Wlo[:, w, c * P:(c + 1) * P]
                nc.tensor.matmul(to, hi, right_hi, start=start, stop=False)
                nc.tensor.matmul(to, lo, right_hi, start=False, stop=False)
                return nc.tensor.matmul(to, hi, right_lo, start=False, stop=stop)

            def up(i, j, first=False):
                k, b, c = j // UE % 2, j // FC % B, j % FC
                if j % UE == 0:
                    pe.wait_ge(w_ok, 2 * i + j // UE + 1)
                if not first:
                    pe.wait_ge(silu_ok, US * i + j - LAG + 1)
                three(PS[:, j % LAG, :], k, c, Zhi[:, b * S:(b + 1) * S], Zlo[:, b * S:(b + 1) * S], True, True).then_inc(h_ps, 1)

            def down(i, j):
                k, b, c = j // UE, j // FC % B, j % FC
                pe.wait_ge(h_ok, US * i + j + 1)
                if c == 0:
                    pe.wait_ge(y_used, 2 * (2 * i + k) + b + 1)
                three(PS[:, 4 + b, :], k, FC + c, Hhi[:, j % NH, :], Hlo[:, j % NH, :], c == 0, c == FC - 1).then_inc(down_ok, 1)

            pe.wait_ge(zsplit_ok, 2)
            pe.wait_ge(emask_ok, 1)
            pe.wait_ge(v1_ok, 2 * B)
            for j in range(LAG):
                up(0, j, True)
            with pe.Fori(0, PAIRS - 1) as i:
                for j in range(US):
                    down(i, j)
                    up(i, j + LAG)
            for j in range(US):
                down(PAIRS - 1, j)
                if j + LAG < US:
                    up(PAIRS - 1, j + LAG)
            for b in range(B):
                pe.wait_ge(y_added, 2 * E - 1 + b)
                for t in range(NT):
                    last = nc.tensor.transpose(PS[:, 4 * b, t * P:(t + 1) * P], Yacc[:, b * S + t * P:b * S + (t + 1) * P], ident)
                last.then_inc(y_ps, 1)

            for b in range(B):
                pe.wait_ge(x_ok, 3 + b)
                z_transposes(b, 2 * B + b + 1, 4 * b)
            for b in range(B):
                pe.wait_ge(zt_ok, 2 * B + b + 1)
                for n, name in enumerate(("q", "qrot")):
                    last = nc.tensor.matmul(PS[:, 4 * b + 1 + n, :], W1s[:, W1[name]], ZT[:, b * S:(b + 1) * S], start=True, stop=True)
                last.then_inc(q1_ps, 1)
            pe.wait_ge(k1_ok, 1)
            for t in range(NT):
                for b in range(B):
                    if t == 0:
                        pe.wait_ge(q1_ok, b + 1)
                    if t >= 2:
                        pe.wait_ge(nat1_max, 2 * (t - 2) + b + 1)
                    to = PS[:, 4 * b + (3, 0)[t % 2], 0:H1 * KC]
                    at = slice(b * S + t * P, b * S + (t + 1) * P)
                    nc.tensor.matmul(to, Q1hi[:, at], Kbhi[:, b, :], start=True, stop=False)
                    nc.tensor.matmul(to, Q1lo[:, at], Kbhi[:, b, :], start=False, stop=False)
                    nc.tensor.matmul(to, Q1hi[:, at], Kblo[:, b, :], start=False, stop=False)
                    nc.tensor.matmul(to, onesr[:, :], fill[:, b, :], start=False, stop=True).then_inc(nat1_ps, 1)
            for b in range(B):
                pe.wait_ge(m1_cat, b + 1)
                for t in range(NT):
                    last = nc.tensor.matmul(PS[0:2 * H1, 4 * b + 1, t * P:(t + 1) * P], mcat1[:, b, t, :], identr[:, :], start=True, stop=True)
                last.then_inc(m1_ps, 1)
            pe.wait_ge(selm_ok, 1)
            for s in range(2):
                for b in range(B):
                    if s == 0:
                        pe.wait_ge(m1_ok, b + 1)
                    for j in range(2):
                        h = 2 * s + j
                        to = PS[0:KC, 4 * b + 2 - 2 * s + j, :]
                        at, cols = slice(b * S, (b + 1) * S), slice(h * KC, (h + 1) * KC)
                        nc.tensor.matmul(to, Kbhi[:, b, cols], Q1hi[:, at], start=True, stop=False)
                        nc.tensor.matmul(to, Kblo[:, b, cols], Q1hi[:, at], start=False, stop=False)
                        nc.tensor.matmul(to, Kbhi[:, b, cols], Q1lo[:, at], start=False, stop=False)
                        last = nc.tensor.matmul(to, selm[:, cols], M1T[:, b, :], start=False, stop=True)
                    last.then_inc(sc1_ps, 1)
            for s in range(2):
                for b in range(B):
                    pe.wait_ge(exp1_ok, 2 * s + b + 1)
                    for j in range(2):
                        last = nc.tensor.matmul(PS[0:66, 4 * b + 2 - 2 * s, :], V1aug[:, b, s, 66 * j:66 * j + 66],
                                                PT1[:, b, j * S:(j + 1) * S], start=(j == 0), stop=(j == 1))
                    last.then_inc(pv1_ok, 1)
            for s in range(2):
                for b in range(B):
                    pe.wait_ge(acc1_sb, 2 * s + b + 1)
                    if s:
                        pe.wait_ge(on1_ok, b + 1)
                    for t in range(NT):
                        last = nc.tensor.transpose(PS[:, 4 * b + 3, 66 * t:66 * t + 66], Osb1[:, b, s, t * P:(t + 1) * P], ident[0:66, 0:66])
                    last.then_inc(on1_ps, 1)
            for b in range(B):
                pe.wait_ge(on1_ok, B + b + 1)
                for t in range(NT):
                    last = nc.tensor.transpose(PS[:, 4 * b + 1, t * P:(t + 1) * P], On1[:, b, t, :], ident)
                last.then_inc(ont1_ps, 1)
            for b in range(B):
                pe.wait_ge(ont1_ok, b + 1)
                for t in range(NT):
                    last = nc.tensor.matmul(PS[:, 4 * b + 3, t * P:(t + 1) * P], OnT1[:, b, t * P:(t + 1) * P], W1s[:, W1["o"]], start=True, stop=True)
                last.then_inc(proj1_ps, 1)
            for b in range(B):
                z_transposes(b, 3 * B + b + 1, 4 * b)
            for b in range(B):
                pe.wait_ge(zt_ok, 3 * B + b + 1)
                w = PROJ + RSUM
                for t in range(NT):
                    last = nc.tensor.matmul(PS[:, 4 * b + 1, t * w:(t + 1) * w], ZT[:, b * S + t * P:b * S + (t + 1) * P], W1s[:, W1["pd"]], start=True, stop=True)
                last.then_inc(pd_ps, 1)
            for b in range(B):
                pe.wait_ge(gd_ok, b + 1)
                for t in range(NT):
                    last = nc.tensor.transpose(PS[0:RSUM, 4 * b + 2, t * P:(t + 1) * P], dn[:, b, t, :], ident)
                last.then_inc(gd_ps, 1)
            for b in range(B):
                pe.wait_ge(gdt_ok, b + 1)
                for t in range(NT):
                    to = PS[:, 4 * b + 3, t * P:(t + 1) * P]
                    nc.tensor.matmul(to, ZT[:, b * S + t * P:b * S + (t + 1) * P], W1s[:, W1["base"]], start=True, stop=False)
                    last = nc.tensor.matmul(to, gdT[0:RSUM, b, t * P:(t + 1) * P], W1s[0:RSUM, W1["up"]], start=False, stop=True)
                last.then_inc(f_ps, 1)


def kernel(**inputs):
    import numpy as np
    import concourse.bacc as bacc
    from concourse.bass_utils import run_bass_kernel_spmd as run

    a = {k: np.asarray(v) for k, v in inputs.items()}
    f4 = np.float32

    def pack(cols, width, **parts):
        out = np.zeros((P, width), f4)
        for name, (row, part) in parts.items():
            out[row:row + part.shape[0], cols[name]] = part
        return out

    row = np.arange(P)
    def block_mask(rows, per, heads):
        m = np.zeros((rows, heads, KC), f4)
        m[np.arange(rows), (np.arange(rows) // per) % heads, :] = 1
        return m.reshape(rows, -1)
    ones = np.zeros((32, GH, KC), f4)
    for i in range(GH):
        ones[i, i] = 1
        ones[GH + i, i] = 1
    vpat = np.zeros((KC, 2, 640), f4)
    for h in range(SH):
        vpat[:, :, 72 * h + 64 + h] = 1
    c0 = pack(C0, C0W, ident=(0, np.eye(P, dtype=f4)), block=(0, block_mask(96, HD0, GH)),
              ones=(96, ones.reshape(32, -1)), vpat=(0, vpat.reshape(KC, -1)))
    half = HD1 // 2
    timescale = np.power(f4(10000.0), f4(2.0 / HD1) * np.arange(half, dtype=f4)).astype(f4)
    def rope(pos):
        rad = pos.astype(f4)[None, :] / timescale[:, None]
        sin, cos = np.sin(rad), np.cos(rad)
        return np.tile(np.concatenate([cos, cos]), (H1, 1)), np.tile(np.concatenate([-sin, sin]), (H1, 1))
    qcos, qsin = rope(np.arange(KC, KC + S))
    kcos, ksin = rope(np.arange(KC))
    v1pat = np.zeros((KC, 2, 2, 66), f4)
    selm = np.zeros((8, H1, KC), f4)
    for i in range(H1):
        v1pat[:, :, i % 2, 64 + i % 2] = 1
        selm[i, i] = 1
        selm[H1 + i, i] = 1
    gsel = np.zeros((2 * E, E, P), f4)
    for e in range(E):
        gsel[e, e] = 1
        gsel[E + e, e] = 1
    c1 = pack(C1, C1W, qcos=(0, qcos), qsin=(0, qsin), kcos=(0, kcos), ksin=(0, ksin), block=(0, block_mask(P, HD1, H1)),
              vpat=(0, v1pat.reshape(KC, -1)), selm=(0, selm.reshape(8, -1)), gsel=(0, gsel.reshape(2 * E, -1)),
              tie8=(0, np.tile(np.arange(E, 0, -1, dtype=f4), (P, 1))), tie4=(0, np.tile(np.arange(E1, 0, -1, dtype=f4), (P, 1))))

    def thrice(w):
        w = w.T.reshape(D, G0, 1, GH * HD0)
        return np.broadcast_to(w, (D, G0, 3, GH * HD0)).reshape(D, -1)
    w0 = pack(W0, W0W, k=(0, thrice(a["L0_xattn_Wk"])), q=(0, thrice(a["L0_xattn_Wq"])),
              v=(0, a["L0_xattn_Wv"].T), o=(0, a["L0_xattn_Wo"].T))
    qw = a["L1_xattn_q_w"].transpose(1, 0, 2)
    swap = np.r_[half:HD1, 0:half]
    kw = a["L1_xattn_kv_w"][0, 0]
    downs = np.concatenate([a[f"L1_ffn_Wd{i}"] for i in range(E1)], 0).T
    ups = np.concatenate([a[f"L1_ffn_Wu{i}"] for i in range(E1)], 1).T
    w1 = pack(W1, W1W, r=(0, a["L0_ffn_Wr"].T), q=(0, qw.reshape(D, -1)), qrot=(0, qw[:, :, swap].reshape(D, -1)),
              k=(0, np.tile(kw, (1, H1))), krot=(0, np.tile(kw[:, swap], (1, H1))), v=(0, a["L1_xattn_kv_w"][1, 0]),
              o=(0, a["L1_xattn_out_w"].reshape(D, D)), rms=(0, a["L1_xattn_rms_scale"][:, None]),
              pd=(0, np.concatenate([a["L1_ffn_Wp"].T, downs], 1)), base=(0, a["L1_ffn_W"].T), up=(0, ups),
              bp=(0, np.tile(a["L1_ffn_bp"], (P, 1))), sim=(0, np.tile(a["L1_ffn_sim"].T.reshape(1, -1), (P, 1))),
              temp=(0, np.tile(a["L1_ffn_temp"], (P, 1))))
    up = a["L0_ffn_W1"].transpose(0, 2, 1)
    down = a["L0_ffn_W2"].reshape(E, D, FC, P).transpose(0, 3, 2, 1).reshape(E, P, FC * D)
    mask = np.zeros((B, KCP), np.bool_)
    mask[:, :KC] = a["mask_BxS2_bk0"]
    arrays = {
        "x": a["x"], "ctx_nat": a["ctx_1024"].transpose(1, 0, 2), "ctx_t": a["ctx_1024"].transpose(2, 0, 1).reshape(D, B * KC),
        "mask": mask.view(np.uint32).reshape(1, -1),
        "c0": c0, "w0": w0, "c1": c1, "w1": w1, "moe": np.concatenate([up, down], 2),
    }
    arrays = {k: np.ascontiguousarray(v) for k, v in arrays.items()}
    nc = bacc.Bacc("TRN2", target_bir_lowering=False, num_devices=1)
    args = [nc.dram_tensor(n, v.shape, mybir.dt.from_np(v.dtype), kind="ExternalInput").ap() for n, v in arrays.items()]
    args.append(nc.dram_tensor("out", (B, S, D), mybir.dt.float32, kind="ExternalOutput").ap())
    fused_layers(nc, *args)
    return run(nc, [arrays], core_ids=[0]).results[0]["out"]
```

```python
import concourse.bass as bass
from concourse import mybir
from contextlib import ExitStack

P = 128
B, S, D = 2, 512, 128
NT = S // P
TILES = B * NT
KC = 77
KCP = 80
H0, HD0 = 16, 8
GH = 4
G0 = H0 // GH
SH = H0 // 2
H1, HD1 = 4, 32
E, F = 8, 512
FC = F // P
E1 = 4
RANKS = [1, 2, 4, 8]
RSUM = sum(RANKS)
PROJ = 32
LAG = 4
NH = 2 * LAG
UE = B * FC
US = 2 * UE
PAIRS = E // 2
NEVER = -(2.0 ** 100)
CLAMP = 4.605170185988091

LAYERS = 4

def columns(*widths):
    out, at = {}, 0
    for name, n in widths:
        out[name] = slice(at, at + n)
        at += n
    return out, at

C0, C0W = columns(("ident", P), ("block", GH * KC), ("ones", GH * KC), ("vpat", 2 * 640))
W0, W0W = columns(("k", G0 * 96), ("q", G0 * 96), ("v", D), ("o", D))
C1, C1W = columns(("qcos", S), ("qsin", S), ("kcos", KC), ("ksin", KC), ("block", H1 * KC), 
                  ("gsel", E * P), ("tie8", E), ("tie4", E1))
W1, W1W = columns(("r", E), ("q", D), ("qrot", D), ("k", D), ("krot", D), ("v", HD1), ("o", D), ("rms", 1),
                  ("pd", PROJ + RSUM), ("base", D), ("up", D), ("bp", PROJ), ("sim", E1 * PROJ), ("temp", 1))


def fused_layers(nc, x, ctx_nat, ctx_t, mask, c0, w0, c1, w1, moe, out):
    fp32 = mybir.dt.float32
    f32r = mybir.dt.float32r
    u8 = mybir.dt.uint8
    ALU = mybir.AluOpType
    ACT = mybir.ActivationFunctionType
    AX = mybir.AxisListType

    with ExitStack() as ctx:
        def sb(name, shape, dt=fp32):
            return ctx.enter_context(nc.sbuf_tensor(name, shape, dt))

        def sem(name):
            return ctx.enter_context(nc.semaphore(name))

        def sems(name, n=B):
            return [sem(f"{name}{k}") for k in range(n)]

        PS = ctx.enter_context(nc.psum_tensor("PS", [P, 8, 512], fp32))

        C0s = sb("C0s", [P, C0["vpat"].start]); W0s = sb("W0s", [P, W0W])
        C1s = sb("C1s", [P, C1W]); W1s = sb("W1s", [P, W1W])
        ident = C0s[:, C0["ident"]]
        identr = sb("identr", [P, P], f32r)
        X = sb("X", [P, TILES, D])
        Z = sb("Z", [P, TILES, D])
        stats = sb("stats", [P, TILES, 6]); mv = sb("mv", [P, TILES, 2])
        rstd = sb("rstd", [P, TILES]); ve = sb("ve", [P, TILES]); mhalf = sb("mhalf", [P, TILES]); one = sb("one", [P, 1])
        ZT = sb("ZT", [P, B * S])
        ctxT = sb("ctxT", [P, B * KC])
        Kaug = sb("Kaug", [P, B, G0, GH * KC], f32r)
        Qaug = sb("Qaug", [P, B, G0, S], f32r)
        negm = sb("negm", [P, B, NT, G0, GH])
        mcat = sb("mcat", [P, B, NT, P], f32r)
        rs = sb("rs", [P, 2, NT, SH])
        On = sb("On", [P, NT, D])
        OnT = sb("OnT", [P, S])
        shared = sb("shared", [P, 2464 + 2560 + 3072 + 1024])
        Kf = shared[0:96, 0:2464].rearrange("p (b g i k) -> p b g i k", b=B, g=G0, i=GH)
        Vaug = shared[:, 2464:5024].rearrange("p (b s n) -> p b s n", b=B, s=2)
        PT = shared[:, 5024:8096].rearrange("p (u j n) -> p u j n", u=3, j=2)
        Osb = shared[0:72, 8096:9120].rearrange("p (s n) -> p s n", s=2)
        Zhi = sb("Zhi", [P, B * S], f32r); Zlo = sb("Zlo", [P, B * S], f32r)
        Wraw = sb("Wraw", [P, 2, 2, F]); Whi = sb("Whi", [P, 2, 2, F], f32r); Wlo = sb("Wlo", [P, 2, 2, F], f32r)
        Sf = sb("Sf", [P, LAG, S])
        Hhi = Qaug[:, :, :, :].rearrange("p b g n -> p (b g) n")
        Hlo = sb("Hlo", [P, NH, S], f32r)
        Lg = sb("Lg", [P, TILES, E]); top = sb("top", [P, B, 2, NT]); tie = sb("tie", [P, TILES, E]); tiem = sb("tiem", [P, TILES])
        pick = sb("pick", [P, B, 2, NT, E]); gw = sb("gw", [P, B, 2, NT]); gate = sb("gate", [P, TILES, E])
        gcat = sb("gcat", [P, TILES, 2 * E], f32r); gT = sb("gT", [2 * E, B * S], f32r)
        gsel = sb("gsel", [2 * E, 2, P], f32r)
        Gs = sb("Gs", [P, 2, S]); Yg = sb("Yg", [P, S]); Yacc = sb("Yacc", [P, B * S])
        ctxn = sb("ctxn", [KC, B, D]); cstat = sb("cstat", [KC, B]); crms = sb("crms", [KC, B]); mn = sb("mn", [KC, B, D])
        mnT = sb("mnT", [P, B, KC]); Kr = sb("Kr", [P, 2, B, KC]); Kb = sb("Kb", [P, B, H1, KC])
        Kbhi = sb("Kbhi", [P, B, H1 * KC], f32r); Kblo = sb("Kblo", [P, B, H1 * KC], f32r)
        V1 = sb("V1", [KC, B, HD1])
        maskw = sb("maskw", [1, B * KCP // 4], mybir.dt.uint32); keep = sb("keep", [1, B, KC])
        fill = sb("fill", [1, B, H1 * KC], f32r); onesf = sb("onesf", [1, P]); onesr = sb("onesr", [1, P], f32r)
        mx1 = sb("mx1", [P, B, NT, H1])
        Qr = Sf[:, :, :].rearrange("p (b n) s -> p b (n s)", b=B)
        Q1hi, Q1lo = Zhi, Zlo
        Pn1 = shared[:, 6144:6144 + B * NT * H1 * KC].rearrange("p (b t k) -> p b t k", b=B, t=NT)
        PT1 = shared[0:KC, 0:B * 2 * H1 * P].rearrange("p (b s n) -> p b s n", b=B, s=2)
        On1 = shared[:, 2048:3072].rearrange("p (b t n) -> p b t n", b=B, t=NT)
        OnT1 = shared[:, 3072:4096].rearrange("p (b n) -> p b n", b=B)
        gdT = shared[0:RSUM, 4096:4096 + B * S].rearrange("p (b n) -> p b n", b=B)
        sq = shared[:, 5120:5120 + B * NT * E1 * PROJ].rearrange("p (b t e j) -> p b t e j", b=B, t=NT, e=E1)
        rs1 = sb("rs1", [P, B, NT, H1])
        pj = sb("pj", [P, B, NT, PROJ]); dn = sb("dn", [P, B, NT, RSUM])
        ss = sb("ss", [P, B, NT]); rn = sb("rn", [P, B, NT]); lg = sb("lg", [P, B, NT, E1]); mx = sb("mx", [P, B, NT])
        ex = sb("ex", [P, B, NT, E1]); lw = sb("lw", [P, B, NT]); eq = sb("eq", [P, B, NT, E1])
        simn = sb("simn", [P, E1, PROJ]); simq = sb("simq", [P, E1, PROJ]); sims = sb("sims", [P, E1]); tscale = sb("tscale", [P, 1])

        ld_x = sems("ld_x"); ld_id = sem("ld_id"); ld_ctx = sem("ld_ctx"); ld_wk = sem("ld_wk"); ld_wq = sem("ld_wq"); ld_wvo = sem("ld_wvo")
        ld_c0 = sem("ld_c0"); ld_v = sem("ld_v"); ld_c1 = sem("ld_c1"); ld_w1 = sem("ld_w1"); ld_ctxn = sem("ld_ctxn")
        ld_mask = sem("ld_mask"); ld_moe = sems("ld_moe")
        dve_step = sem("dve_step"); pool_step = sem("pool_step")
        stats_ok = sems("stats_ok"); rstd_ok = sems("rstd_ok"); z_ok = sems("z_ok"); zt_ps = sems("zt_ps"); zt_ok = sems("zt_ok"); x_ok = sems("x_ok")
        consts = sem("consts"); idr_ok = sem("idr_ok"); kones = sem("kones"); gsel_ok = sem("gsel_ok")
        k_ps = sem("k_ps"); k_full = sem("k_full"); k_hi = sem("k_hi"); k_ok = sems("k_ok"); v_ps = sem("v_ps"); v_ok = sem("v_ok")
        q_ps = sem("q_ps"); q_hi = sem("q_hi"); q_ok = sem("q_ok")
        nat_ps = sem("nat_ps"); nat_max = sem("nat_max"); m_cat = sem("m_cat"); m_ps = sem("m_ps"); m_ok = sem("m_ok")
        sc_ps = sem("sc_ps"); exp_ok = sem("exp_ok"); pv_ok = sem("pv_ok"); acc_sb = sem("acc_sb")
        on_ps = sem("on_ps"); on_ok = sem("on_ok"); ont_ps = sem("ont_ps"); ont_ok = sem("ont_ok"); proj_ps = sem("proj_ps")
        w_hi = sem("w_hi"); w_up = sems("w_up"); w_down = sems("w_down"); z_hi = sem("z_hi"); zsplit_ok = sem("zsplit_ok")
        lg_ps = sem("lg_ps"); lg_read = sem("lg_read"); margin = sem("margin"); gw_ok = sem("gw_ok"); gcat_ok = sem("gcat_ok")
        gt_ps = sem("gt_ps"); gt_ok = sem("gt_ok"); gate_ps = sem("gate_ps"); gate_sb = sems("gate_sb")
        h_ps = sem("h_ps"); silu_ok = sem("silu_ok"); h_hi = sem("h_hi"); h_ok = sem("h_ok"); down_ok = sem("down_ok")
        y_used = sem("y_used"); y_added = sem("y_added"); y_ps = sem("y_ps")
        c_ss = sem("c_ss"); c_rms = sem("c_rms"); mn_ok = sem("mn_ok"); mn_ps = sem("mn_ps"); mnt_ok = sem("mnt_ok")
        kv1_ps = sem("kv1_ps"); k1_ok = sem("k1_ok"); w1s_ok = sem("w1s_ok"); fill_ok = sem("fill_ok")
        q1_ps = sem("q1_ps"); q1_rot = sem("q1_rot"); q1_hi = sem("q1_hi"); q1_ok = sem("q1_ok")
        nat1_ps = sems("nat1_ps"); sub1_ok = sems("sub1_ok"); exp1_ok = sems("exp1_ok")
        tr1_ps = sems("tr1_ps"); pt1_ok = sems("pt1_ok"); pv1_ok = sems("pv1_ok")
        on1_ok = sems("on1_ok"); ont1_ps = sem("ont1_ps"); ont1_ok = sem("ont1_ok"); proj1_ps = sem("proj1_ps")
        sim_ss = sem("sim_ss"); sim_rn = sem("sim_rn"); t_min = sem("t_min"); t_exp = sem("t_exp")
        pd_ps = sem("pd_ps"); pss_ok = sem("pss_ok"); prn_ok = sem("prn_ok"); d_ok = sem("d_ok"); ex_ok = sem("ex_ok")
        gd_ok = sem("gd_ok"); gd_ps = sem("gd_ps"); gdt_ok = sem("gdt_ok"); f_ps = sem("f_ps")
        stored = sem("stored")

        x_d = x.rearrange("b (t p) d -> p (b t) d", p=P)
        out_d = out.rearrange("b (t p) d -> p (b t) d", p=P)
        QBANK = (1, 2, 3, 0)
        QBANK1 = ((3, 2), (5, 4))
        BANKS = ((6, 7, 0, 1), (4, 5, 2, 3))

        def tiles(b):
            return slice(b * NT, (b + 1) * NT)

        def tokens(b):
            return slice(b * S, (b + 1) * S)

        block = ctx.enter_context(nc.Block())

        @block.sync
        def _(sp):
            def part(cols):
                return w0[:, cols]
            sp.dma_start(X[:, tiles(0), :], x_d[:, tiles(0), :]).then_inc(ld_x[0], 16)
            sp.dma_start(W0s[:, W0["q"]], part(W0["q"])).then_inc(ld_wq, 16)
            sp.dma_start(X[:, tiles(1), :], x_d[:, tiles(1), :]).then_inc(ld_x[1], 16)
            for b in range(B):
                sp.dma_start(Vaug[:, b, :, :], c0[:, C0["vpat"]].rearrange("p (s n) -> p s n", s=2)).then_inc(ld_v, 16)
            sp.dma_start(W0s[:, W0["v"].start:W0["o"].stop], part(slice(W0["v"].start, W0["o"].stop))).then_inc(ld_wvo, 16)
            sp.dma_start(C1s[:, :], c1).then_inc(ld_c1, 16)
            sp.dma_start(W1s[:, :], w1).then_inc(ld_w1, 16)
            sp.dma_start(ctxn[:, :, :], ctx_nat).then_inc(ld_ctxn, 16)
            sp.dma_start(maskw[:, :], mask).then_inc(ld_mask, 16)
            for k in range(2):
                sp.dma_start(Wraw[:, k, :, :], moe[k]).then_inc(ld_moe[k], 16)
            with sp.Fori(1, PAIRS) as i:
                for k in range(2):
                    sp.wait_ge(w_down[k], i)
                    sp.dma_start(Wraw[:, k, :, :], moe[2 * i + k]).then_inc(ld_moe[k], 16)
            for b in range(B):
                sp.wait_ge(x_ok[b], LAYERS)
                sp.dma_start(out_d[:, tiles(b), :], X[:, tiles(b), :]).then_inc(stored, 16)
            sp.wait_ge(stored, 16 * B)

        @block.gpsimd
        def _(pool):
            def link(ins, count=[0]):
                count[0] += 1
                ins.then_inc(pool_step, 1)
                pool.wait_ge(pool_step, count[0])

            def inverse_root(layer, b):
                pool.wait_ge(stats_ok[b], layer + 1)
                nc.gpsimd.tensor_tensor(rstd[:, tiles(b)], ve[:, tiles(b)], mhalf[:, tiles(b)], ALU.pow).then_inc(rstd_ok[b], 1)
                pool.wait_ge(rstd_ok[b], layer + 1)

            def split_weights(i, k, half, ready, n):
                pool.wait_ge(ld_moe[k], 16 * i + 16)
                if ready:
                    pool.wait_ge(*ready)
                hi, lo, raw = Whi[:, k, half, :], Wlo[:, k, half, :], Wraw[:, k, half, :]
                nc.gpsimd.tensor_tensor(hi, raw, one[:, :].broadcast_to([P, F]), ALU.mult).then_inc(w_hi, 1)
                pool.wait_ge(w_hi, 4 * i + n + 1)
                done = (w_up, w_down)[half][k]
                nc.gpsimd.tensor_tensor(lo, raw, hi.bitcast(fp32), ALU.subtract).then_inc(done, 1)
                pool.wait_ge(done, i + 1)

            link(nc.gpsimd.memset(mhalf[:, :], -0.5))
            link(nc.gpsimd.memset(one[:, :], 1.0))
            inverse_root(0, 0)
            pool.wait_ge(ld_id, 16)
            nc.gpsimd.tensor_copy(identr[:, :], ident).then_inc(idr_ok, 1)
            pool.wait_ge(idr_ok, 1)
            inverse_root(0, 1)
            nc.gpsimd.memset(mcat[:, :, :, :].bitcast(fp32), 0.0).then_inc(consts, 1)
            pool.wait_ge(consts, 1)
            nc.gpsimd.memset(PT[:, :, :, :], 0.0).then_inc(consts, 1)
            pool.wait_ge(consts, 2)
            pool.wait_ge(k_hi, 2)
            lo = Kaug[64:96, 1, :, :]
            nc.gpsimd.tensor_tensor(lo, Kf[64:96, 1, :, :, :].rearrange("p g i k -> p g (i k)"), lo.bitcast(fp32), ALU.subtract).then_inc(k_ok[1], 1)
            pool.wait_ge(k_ok[1], 1)
            for n in range(4):
                split_weights(0, n % 2, n // 2, None, n)
            pool.wait_ge(c_ss, 1)
            nc.gpsimd.tensor_tensor(crms[:, :], cstat[:, :], mhalf[0:KC, 0:B], ALU.pow).then_inc(c_rms, 1)
            pool.wait_ge(c_rms, 1)
            pool.wait_ge(sim_ss, 1)
            nc.gpsimd.tensor_tensor(sims[:, :], sims[:, :], mhalf[:, 0:E1], ALU.pow).then_inc(sim_rn, 1)
            pool.wait_ge(sim_rn, 1)
            pool.wait_ge(ld_c1, 16)

            def gate_picker(i, k, ready):
                if ready:
                    pool.wait_ge(*ready)
                nc.gpsimd.tensor_tensor(gsel[:, k, :], C1s[0:2 * E, bass.ds(C1["gsel"].start + (2 * i + k) * P, P)],
                                        one[0:2 * E, :].broadcast_to([2 * E, P]), ALU.mult).then_inc(gsel_ok, 1)
                pool.wait_ge(gsel_ok, 2 * i + k + 1)

            gate_picker(0, 0, None)
            gate_picker(0, 1, None)
            for b in range(B):
                inverse_root(1, b)
            with pool.Fori(1, PAIRS) as i:
                split_weights(i, 0, 0, (h_ps, US * i - FC), 0)
                gate_picker(i, 0, (gate_ps, 4 * i - 1))
                split_weights(i, 1, 0, (h_ps, US * i), 1)
                gate_picker(i, 1, (gate_ps, 4 * i))
                split_weights(i, 0, 1, (down_ok, US * i - FC), 2)
                split_weights(i, 1, 1, (down_ok, US * i), 3)
            inverse_root(2, 0)
            inverse_root(2, 1)

            def proj_norms(b):
                pool.wait_ge(pss_ok, b + 1)
                nc.gpsimd.tensor_tensor(rn[:, b, :], ss[:, b, :], mhalf[:, 0:NT], ALU.pow).then_inc(prn_ok, 1)
                pool.wait_ge(prn_ok, b + 1)

            inverse_root(3, 0)
            proj_norms(0)
            inverse_root(3, 1)
            proj_norms(1)

        @block.scalar
        def _(act):
            act.dma_start(C0s[:, C0["ident"]], c0[:, C0["ident"]]).then_inc(ld_id, 16)
            act.dma_start(ctxT[:, :], ctx_t).then_inc(ld_ctx, 16)
            act.dma_start(W0s[:, W0["k"]], w0[:, W0["k"]]).then_inc(ld_wk, 16)
            act.dma_start(C0s[:, C0["block"].start:C0["ones"].stop], c0[:, C0["block"].start:C0["ones"].stop]).then_inc(ld_c0, 16)

            def copy(to, source):
                return nc.scalar.activation(to, source, ACT.Copy)

            def zt_copy(layer, b, bank):
                act.wait_ge(zt_ps[b], layer + 1)
                copy(ZT[:, tokens(b)], PS[:, bank, :]).then_inc(zt_ok[b], 1)

            def q_high(b, g):
                act.wait_ge(q_ps, G0 * b + g + 1)
                copy(Qaug[0:96, b, g, :], PS[0:96, QBANK[g], :]).then_inc(q_hi, 1)

            def k_high(b):
                act.wait_ge(k_full, b + 1)
                copy(Kaug[0:96, b, :, :], Kf[:, b, :, :, :].rearrange("p g i k -> p g (i k)")).then_inc(k_hi, 1)

            def m_rows(b):
                act.wait_ge(m_ps, b + 1)
                for g in range(G0):
                    copy(Qaug[96:P, b, g, :], PS[32 * g:32 * g + 32, 4, :]).then_inc(m_ok, 1)

            def exps(b, hp):
                u = 8 * b + hp
                act.wait_ge(sc_ps, u + 1)
                if u >= 3:
                    act.wait_ge(pv_ok, u - 2)
                bank = 2 * (u % 2)
                nc.scalar.activation(PT[0:KC, u % 3, :, :], PS[0:KC, bank:bank + 2, :], ACT.Exp,
                                     scale=float(HD0) ** -0.5).then_inc(exp_ok, 1)

            def acc_copy(b, s):
                act.wait_ge(pv_ok, 8 * b + 4 * (s + 1))
                if b:
                    act.wait_ge(on_ps, s + 1)
                copy(Osb[:, s, :], PS[0:72, 6 + s, :]).then_inc(acc_sb, 1)

            def out_copy(b, bank):
                act.wait_ge(ont_ps, b + 1)
                copy(OnT[:, :], PS[:, bank, :]).then_inc(ont_ok, 1)

            def z_split(b, bank):
                act.wait_ge(zt_ps[b], 2)
                copy(ZT[:, tokens(b)], PS[:, bank, :]).then_inc(zt_ok[b], 1)
                copy(Zhi[:, tokens(b)], PS[:, bank, :]).then_inc(z_hi, 1)

            zt_copy(0, 0, 0)
            k_high(0)
            for g in range(G0):
                q_high(0, g)
            act.wait_ge(v_ps, 1)
            act.wait_ge(ld_v, 16 * B)
            for b in range(B):
                copy(Vaug[0:KC, b, :, :].rearrange("p s (h c) -> p s h c", c=80)[:, :, :, 0:HD0],
                     PS[0:KC, 5, b * D:(b + 1) * D].rearrange("p (s h c) -> p s h c", s=2, c=HD0)).then_inc(v_ok, 1)
            zt_copy(0, 1, 4)
            copy(Kaug[96:P, :, :, :].rearrange("p b g n -> p (b g) n"),
                 C0s[96:P, C0["ones"]].unsqueeze(1).broadcast_to([32, B * G0, GH * KC])).then_inc(kones, 1)
            k_high(1)
            for g in range(G0):
                q_high(1, g)
            m_rows(0)
            act.wait_ge(consts, 2)
            for hp in range(8):
                exps(0, hp)
                if hp == 5:
                    acc_copy(0, 0)
            acc_copy(0, 1)
            m_rows(1)
            for hp in range(8):
                exps(1, hp)
                if hp == 3:
                    out_copy(0, 5)
                if hp == 0:
                    act.wait_ge(mn_ps, 1)
                    copy(mnT[:, :, :], PS[:, 4, 0:B * KC].rearrange("p (b k) -> p b k", b=B)).then_inc(mnt_ok, 1)
                    act.wait_ge(t_min, 1)
                    nc.scalar.activation(tscale[:, :], tscale[:, :], ACT.Exp).then_inc(t_exp, 1)
                if hp == 5:
                    acc_copy(1, 0)
                if hp == 6:
                    z_split(0, 4)
            nc.scalar.preload_act_table(ACT.Silu)
            acc_copy(1, 1)

            def hidden(i, j, first=False):
                act.wait_ge(h_ps, US * i + j + 1)
                if not (first and j < LAG):
                    act.wait_ge(h_ok, US * i + j - LAG + 1)
                nc.scalar.activation(Sf[:, j % LAG, :], PS[:, j % LAG, :], ACT.Silu).then_inc(silu_ok, 1)
                act.wait_ge(silu_ok, US * i + j + 1)
                if not (first and j < NH):
                    act.wait_ge(down_ok, US * i + j - NH + 1)
                copy(Hhi[:, j % NH, :], Sf[:, j % LAG, :]).then_inc(h_hi, 1)

            def half_tanh(b):
                act.wait_ge(margin, b + 1)
                nc.scalar.activation(gw[:, b, 0, :], gw[:, b, 0, :], ACT.Tanh, scale=0.5).then_inc(gw_ok, 1)

            def gate_rows(b):
                act.wait_ge(gt_ps, b + 1)
                copy(gT[:, tokens(b)], PS[0:2 * E, 6, :]).then_inc(gt_ok, 1)

            def gate_copy(i, b):
                act.wait_ge(gate_ps, 4 * i + 2 * b + 1)
                act.wait_ge(y_used, 4 * i + 2 * b + 1)
                copy(Gs[:, 0, :], PS[:, 6, :]).then_inc(gate_sb[0], 1)

            half_tanh(0)
            for j in range(LAG):
                if j == 2:
                    out_copy(1, 6)
                hidden(0, j, True)
            for j in range(US):
                hidden(j + LAG >= US, (j + LAG) % US, j + LAG < US)
                if j == 2:
                    gate_rows(0)
                if j == 3:
                    gate_copy(0, 0)
                    z_split(1, 0)
                if j == 9:
                    half_tanh(1)
                if j == 12:
                    gate_rows(1)
                if j == 13:
                    gate_copy(0, 1)
            with act.Fori(1, PAIRS - 1) as i:
                for j in range(US):
                    hidden(i + (j + LAG) // US, (j + LAG) % US)
                    if j in (2, 10):
                        gate_copy(i, j // 8)
            for j in range(US - LAG):
                hidden(PAIRS - 1, j + LAG)
                if j in (2, 10):
                    gate_copy(PAIRS - 1, j // 8)
            nc.scalar.preload_act_table(ACT.Exp)

            def q1_high(b):
                act.wait_ge(q1_rot, b + 1)
                copy(Q1hi[:, tokens(b)], Qr[:, b, 0:S]).then_inc(q1_hi, 1)

            def exp1(b, t):
                act.wait_ge(sub1_ok[b], t + 1)
                nc.scalar.activation(Pn1[:, b, t, :], Pn1[:, b, t, :], ACT.Exp, scale=float(HD1) ** -0.5).then_inc(exp1_ok[b], 1)

            def turned_copy(b, t):
                act.wait_ge(tr1_ps[b], t + 1)
                if t >= 2:
                    act.wait_ge(pv1_ok[b], t - 1)
                copy(PT1[:, b, t % 2, :], PS[0:KC, BANKS[b][0], :]).then_inc(pt1_ok[b], 1)

            def out1_copy(b):
                act.wait_ge(ont1_ps, b + 1)
                copy(OnT1[:, b, :], PS[:, BANKS[b][3], :]).then_inc(ont1_ok, 1)

            def low_rank_exp(b):
                act.wait_ge(d_ok, b + 1)
                nc.scalar.activation(ex[:, b, :, :], ex[:, b, :, :], ACT.Exp).then_inc(ex_ok, 1)

            def gated_down_copy(b):
                act.wait_ge(gd_ps, b + 1)
                copy(gdT[:, b, :], PS[0:RSUM, BANKS[b][2], :]).then_inc(gdt_ok, 1)

            zt_copy(2, 0, 0)
            q1_high(0)
            exp1(0, 0)
            zt_copy(2, 1, BANKS[1][0])
            exp1(0, 1)
            turned_copy(0, 0)
            exp1(0, 2)
            turned_copy(0, 1)
            exp1(0, 3)
            turned_copy(0, 2)
            turned_copy(0, 3)
            q1_high(1)
            exp1(1, 0)
            out1_copy(0)
            exp1(1, 1)
            turned_copy(1, 0)
            exp1(1, 2)
            turned_copy(1, 1)
            exp1(1, 3)
            turned_copy(1, 2)
            zt_copy(3, 0, BANKS[0][0])
            turned_copy(1, 3)
            out1_copy(1)
            low_rank_exp(0)
            zt_copy(3, 1, BANKS[1][0])
            gated_down_copy(0)
            low_rank_exp(1)
            gated_down_copy(1)

        @block.vector
        def _(dve):
            def link(ins, count=[0]):
                count[0] += 1
                ins.then_inc(dve_step, 1)
                dve.wait_ge(dve_step, count[0])

            def norm_stats(layer, b):
                dve.wait_ge(ld_x[b], 16) if layer == 0 else dve.wait_ge(x_ok[b], layer)
                for t in range(b * NT, (b + 1) * NT):
                    last = nc.vector.bn_stats(stats[:, t, :], X[:, t, :])
                link(last)
                for t in range(b * NT, (b + 1) * NT):
                    last = nc.vector.bn_aggr(mv[:, t, :], stats[:, t, :])
                link(last)
                e1, e2 = 1e-5, 1e-6
                a, c = (1.0 + e2, e1 * e2) if layer == 2 else (1.0, e1)
                nc.vector.tensor_scalar(ve[:, tiles(b)], mv[:, tiles(b), 1], a, c, ALU.mult, ALU.add).then_inc(stats_ok[b], 1)

            def norm_apply(layer, b):
                dve.wait_ge(rstd_ok[b], layer + 1)
                for t in range(b * NT, (b + 1) * NT):
                    last = nc.vector.tensor_scalar(Z[:, t, :], X[:, t, :], mv[:, t, 0:1], rstd[:, t:t + 1],
                                                   ALU.subtract, ALU.mult)
                last.then_inc(z_ok[b], 1)

            def add_to_x(b, bank):
                nc.vector.tensor_tensor(X[:, tiles(b), :], PS[:, bank, :].rearrange("p (t d) -> p t d", d=D),
                                        X[:, tiles(b), :], ALU.add).then_inc(x_ok[b], 1)

            def k_block(b, g):
                dve.wait_ge(k_ps, g // 2 + 1)
                src = PS[0:96, 6 + g // 2, (g % 2) * B * KC + b * KC:(g % 2) * B * KC + (b + 1) * KC]
                ins = nc.vector.tensor_tensor(Kf[:, b, g, :, :], src.unsqueeze(1).broadcast_to([96, GH, KC]),
                                              C0s[0:96, C0["block"]].rearrange("p (i k) -> p i k", i=GH), ALU.mult)
                if g == G0 - 1:
                    ins.then_inc(k_full, 1)

            def k_low():
                dve.wait_ge(k_hi, 1)
                lo = Kaug[64:96, 0, :, :]
                nc.vector.tensor_tensor(lo, Kf[64:96, 0, :, :, :].rearrange("p g i k -> p g (i k)"), lo.bitcast(fp32), ALU.subtract).then_inc(k_ok[0], 1)

            def q_low(b, g):
                dve.wait_ge(q_hi, G0 * b + g + 1)
                lo = Qaug[32:64, b, g, :]
                nc.vector.tensor_tensor(lo, PS[32:64, QBANK[g], :], lo.bitcast(fp32), ALU.subtract).then_inc(q_ok, 1)

            def nat(b, n):
                u = 8 * b + n
                t, gp = n // 2, n % 2
                bank = (4, 6)[n % 2] if b == 0 else 4
                dve.wait_ge(nat_ps, u + 1)
                nc.vector.tensor_reduce(negm[:, b, t, 2 * gp:2 * gp + 2, :],
                                        PS[:, bank:bank + 2, 0:GH * KC].rearrange("p g (i k) -> p g i k", i=GH),
                                        AX.X, ALU.max, negate=True).then_inc(nat_max, 1)

            def max_parts(b):
                dve.wait_ge(nat_max, 8 * (b + 1))
                dve.wait_ge(consts, 1)
                parts = mcat[:, b, :, :].rearrange("p t (g c) -> p t g c", g=G0)
                for part in (0, 1):
                    for t in range(NT):
                        if part == 0:
                            ins = nc.vector.tensor_copy(parts[:, t, :, 0:GH], negm[:, b, t, :, :])
                        else:
                            ins = nc.vector.tensor_tensor(parts[:, t, :, GH:2 * GH], negm[:, b, t, :, :],
                                                          parts[:, t, :, 0:GH].bitcast(fp32), ALU.subtract)
                    if part == 0:
                        link(ins)
                ins.then_inc(m_cat, 1)

            def normalise(b, s, bank):
                dve.wait_ge(on_ps, 2 * b + s + 1)
                got = PS[:, bank, 0:NT * 72].rearrange("p (t c) -> p t c", c=72)
                link(nc.vector.reciprocal(rs[:, s, :, :], got[:, :, 64:72]))
                if b and not s:
                    dve.wait_ge(ont_ps, b)
                nc.vector.tensor_tensor(On[:, :, 64 * s:64 * s + 64].rearrange("p t (h d) -> p t h d", d=HD0),
                                        got[:, :, 0:64].rearrange("p t (h d) -> p t h d", d=HD0),
                                        rs[:, s, :, :].unsqueeze(3).broadcast_to([P, NT, SH, HD0]), ALU.mult).then_inc(on_ok, 1)

            def z_low(b, bank):
                dve.wait_ge(z_hi, b + 1)
                dve.wait_ge(zt_ok[b], 2)
                nc.vector.tensor_tensor(Zlo[:, tokens(b)], PS[:, bank, :], Zhi[:, tokens(b)].bitcast(fp32),
                                        ALU.subtract).then_inc(zsplit_ok, 1)

            def context_norms():
                dve.wait_ge(ld_ctxn, 16)
                link(nc.vector.tensor_tensor(mn[:, :, :], ctxn[:, :, :], ctxn[:, :, :], ALU.mult))
                link(nc.vector.reduce_sum(cstat[:, :], mn[:, :, :], AX.X))
                nc.vector.tensor_scalar(cstat[:, :], cstat[:, :], 1.0 / D, 1e-6, ALU.mult, ALU.add).then_inc(c_ss, 1)

            def weights_second():
                dve.wait_ge(ld_w1, 16)
                sim = W1s[:, W1["sim"]].rearrange("p (e n) -> p e n", e=E1)
                link(nc.vector.tensor_tensor(simq[:, :, :], sim, sim, ALU.mult))
                link(nc.vector.reduce_sum(sims[:, :], simq[:, :, :], AX.X))
                nc.vector.tensor_scalar_max(sims[:, :], sims[:, :], 1e-24).then_inc(sim_ss, 1)
                nc.vector.tensor_scalar_min(tscale[:, :], W1s[:, W1["temp"]], CLAMP).then_inc(t_min, 1)
                link(nc.vector.tensor_scalar_add(W1s[:, W1["rms"]], W1s[:, W1["rms"]], 1.0))
                scaled = W1s[:, W1["q"].start:W1["v"].stop]
                nc.vector.tensor_scalar(scaled, scaled, W1s[:, W1["rms"]], None, ALU.mult).then_inc(w1s_ok, 1)

            def mask_rows():
                dve.wait_ge(ld_mask, 16)
                link(nc.vector.tensor_copy(keep[:, :, :], maskw[:, :].bitcast(u8).rearrange("p (b k) -> p b k", b=B)[:, :, 0:KC]))
                link(nc.vector.memset(onesf[:, :], 1.0))
                link(nc.vector.tensor_copy(onesr[:, :], onesf[:, :]))
                nc.vector.tensor_scalar(fill[:, :, :].rearrange("p b (i k) -> p b i k", i=H1), keep[:, :, :].unsqueeze(2).broadcast_to([1, B, H1, KC]),
                                        -1.0, -NEVER, ALU.add, ALU.mult).then_inc(fill_ok, 1)

            def context_rows():
                dve.wait_ge(c_rms, 1)
                for b in range(B):
                    last = nc.vector.tensor_scalar(mn[:, b, :], ctxn[:, b, :], crms[:, b:b + 1], None, ALU.mult)
                last.then_inc(mn_ok, 1)

            def prepare_keys():
                dve.wait_ge(kv1_ps, 1)
                nc.vector.tensor_copy(V1[:, :, :], PS[0:KC, 4, 2 * B * KC:2 * B * KC + B * HD1].rearrange("p (b d) -> p b d", b=B))
                dve.wait_ge(ld_c1, 16)
                for n, table in enumerate(("kcos", "ksin")):
                    last = nc.vector.tensor_tensor(Kr[:, n, :, :], PS[:, 4, n * B * KC:(n + 1) * B * KC].rearrange("p (b k) -> p b k", b=B),
                                                   C1s[:, C1[table]].unsqueeze(1).broadcast_to([P, B, KC]), ALU.mult)
                link(last)
                link(nc.vector.tensor_tensor(Kr[:, 0, :, :], Kr[:, 0, :, :], Kr[:, 1, :, :], ALU.add))
                link(nc.vector.tensor_tensor(Kb[:, :, :, :], Kr[:, 0, :, :].unsqueeze(2).broadcast_to([P, B, H1, KC]),
                                             C1s[:, C1["block"]].rearrange("p (i k) -> p i k", i=H1).unsqueeze(1).broadcast_to([P, B, H1, KC]), ALU.mult))
                whole = Kb[:, :, :, :].rearrange("p b i k -> p b (i k)")
                link(nc.vector.tensor_copy(Kbhi[:, :, :], whole))
                nc.vector.tensor_tensor(Kblo[:, :, :], whole, Kbhi[:, :, :].bitcast(fp32), ALU.subtract).then_inc(k1_ok, 1)
                dve.wait_ge(sim_rn, 1)
                dve.wait_ge(t_exp, 1)
                link(nc.vector.tensor_scalar(sims[:, :], sims[:, :], tscale[:, :], None, ALU.mult))
                link(nc.vector.tensor_tensor(simn[:, :, :], W1s[:, W1["sim"]].rearrange("p (e n) -> p e n", e=E1),
                                             sims[:, :].unsqueeze(2).broadcast_to([P, E1, PROJ]), ALU.mult))

            nc.vector.memset(Yacc[:, :], 0.0).then_inc(y_used, 2)
            norm_stats(0, 0)
            norm_apply(0, 0)
            dve.wait_ge(ld_c0, 16)
            for g in range(G0):
                k_block(0, g)
            norm_stats(0, 1)
            k_low()
            norm_apply(0, 1)
            q_low(0, 0)
            k_block(1, 0)
            k_block(1, 1)
            q_low(0, 1)
            q_low(0, 2)
            k_block(1, 2)
            k_block(1, 3)
            q_low(0, 3)
            for n in range(8):
                nat(0, n)
                if n % 2 and n > 2:
                    q_low(1, n // 2 - 1)
            max_parts(0)
            q_low(1, 3)
            for n in range(8):
                nat(1, n)
                if n == 1:
                    context_norms()
                if n == 3:
                    weights_second()
                if n == 5:
                    mask_rows()
            max_parts(1)
            context_rows()
            normalise(0, 0, 5)
            normalise(0, 1, 5)
            prepare_keys()
            dve.wait_ge(proj_ps, 1)
            add_to_x(0, 4)
            norm_stats(1, 0)
            norm_apply(1, 0)
            z_low(0, 4)

            def logits_copy(b, bank):
                dve.wait_ge(lg_ps, b + 1)
                nc.vector.tensor_copy(Lg[:, tiles(b), :], PS[:, bank, 0:NT * E].rearrange("p (t e) -> p t e", e=E)).then_inc(lg_read, 1)
                dve.wait_ge(lg_read, b + 1)

            def choose(b):
                def bc(ap):
                    return ap.unsqueeze(2).broadcast_to([P, NT, E])
                row, tied = Lg[:, tiles(b), :], tie[:, tiles(b), :]
                for n in range(2):
                    link(nc.vector.tensor_reduce(top[:, b, n, :], row, AX.X, ALU.max))
                    if n == 1:
                        nc.vector.tensor_tensor(gw[:, b, 0, :], top[:, b, 0, :], top[:, b, 1, :], ALU.subtract).then_inc(margin, 1)
                    link(nc.vector.tensor_tensor(tied, row, bc(top[:, b, n, :]), ALU.is_equal))
                    link(nc.vector.tensor_tensor(tied, tied, C1s[:, C1["tie8"]].unsqueeze(1).broadcast_to([P, NT, E]), ALU.mult))
                    link(nc.vector.tensor_reduce(tiem[:, tiles(b)], tied, AX.X, ALU.max))
                    link(nc.vector.tensor_tensor(pick[:, b, n, :, :], tied, bc(tiem[:, tiles(b)]), ALU.is_equal))
                    if n == 0:
                        link(nc.vector.scalar_tensor_tensor(row, pick[:, b, 0, :, :], -3.0e38, row, ALU.mult, ALU.add))

            def weigh(b):
                def bc(ap):
                    return ap.unsqueeze(2).broadcast_to([P, NT, E])
                dve.wait_ge(gw_ok, b + 1)
                nc.vector.tensor_scalar(gw[:, b, 1, :], gw[:, b, 0, :], -0.5, 0.5, ALU.mult, ALU.add)
                link(nc.vector.tensor_scalar(gw[:, b, 0, :], gw[:, b, 0, :], 0.5, 0.5, ALU.mult, ALU.add))
                g = gate[:, tiles(b), :]
                nc.vector.tensor_tensor(g, pick[:, b, 0, :, :], bc(gw[:, b, 0, :]), ALU.mult)
                link(nc.vector.tensor_tensor(tie[:, tiles(b), :], pick[:, b, 1, :, :], bc(gw[:, b, 1, :]), ALU.mult))
                link(nc.vector.tensor_tensor(g, g, tie[:, tiles(b), :], ALU.add))
                link(nc.vector.tensor_copy(gcat[:, tiles(b), 0:E], g))
                nc.vector.tensor_tensor(gcat[:, tiles(b), E:2 * E], g, gcat[:, tiles(b), 0:E].bitcast(fp32), ALU.subtract).then_inc(gcat_ok, 1)

            def hidden_low(i, j):
                dve.wait_ge(h_hi, US * i + j + 1)
                nc.vector.tensor_tensor(Hlo[:, j % NH, :], Sf[:, j % LAG, :], Hhi[:, j % NH, :].bitcast(fp32), ALU.subtract).then_inc(h_ok, 1)

            def gated(i, n):
                b, k = n // 2, n % 2
                if k == 0:
                    dve.wait_ge(gate_sb[0], 2 * i + b + 1)
                else:
                    dve.wait_ge(gate_ps, 4 * i + n + 1)
                    nc.vector.tensor_copy(Gs[:, 1, :], PS[:, 7, :]).then_inc(gate_sb[1], 1)
                    dve.wait_ge(gate_sb[1], 2 * i + b + 1)
                dve.wait_ge(down_ok, US * i + FC * (n + 1))
                nc.vector.tensor_tensor(Yg[:, :], PS[:, 4 + k, :], Gs[:, k, :], ALU.mult).then_inc(y_used, 1)
                dve.wait_ge(y_used, 4 * i + n + 3)
                acc = Yacc[:, tokens(b)]
                nc.vector.tensor_tensor(acc, acc, Yg[:, :], ALU.add).then_inc(y_added, 1)
                dve.wait_ge(y_added, 4 * i + n + 1)

            logits_copy(0, 5)
            normalise(1, 0, 6)
            choose(0)
            normalise(1, 1, 7)
            hidden_low(0, 0)
            hidden_low(0, 1)
            weigh(0)
            hidden_low(0, 2)
            dve.wait_ge(proj_ps, 2)
            add_to_x(1, 7)
            norm_stats(1, 1)
            hidden_low(0, 3)
            for j in range(US):
                hidden_low(j + LAG >= US, (j + LAG) % US)
                if j == 0:
                    norm_apply(1, 1)
                if j == 3:
                    gated(0, 0)
                    z_low(1, 0)
                    logits_copy(1, 3)
                if j == 5:
                    gated(0, 1)
                if j == 8:
                    choose(1)
                if j == 10:
                    weigh(1)
                if j == 13:
                    gated(0, 2)
                if j == 15:
                    gated(0, 3)
            with dve.Fori(1, PAIRS - 1) as i:
                for j in range(US):
                    hidden_low(i + (j + LAG) // US, (j + LAG) % US)
                    if j % FC == FC - 1:
                        gated(i, j // FC)
            for j in range(US):
                if j + LAG < US:
                    hidden_low(PAIRS - 1, j + LAG)
                if j % FC == FC - 1:
                    gated(PAIRS - 1, j // FC)
                if j == 8:
                    dve.wait_ge(y_ps, 1)
                    add_to_x(0, BANKS[0][1])
                    norm_stats(2, 0)
                if j == 10:
                    norm_apply(2, 0)

            def rotate(b):
                for n, table in enumerate(("qcos", "qsin")):
                    dve.wait_ge(q1_ps, 2 * b + n + 1)
                    last = nc.vector.tensor_tensor(Qr[:, b, n * S:(n + 1) * S], PS[:, QBANK1[b][n], :], C1s[:, C1[table]], ALU.mult)
                link(last)
                nc.vector.tensor_tensor(Qr[:, b, 0:S], Qr[:, b, 0:S], Qr[:, b, S:2 * S], ALU.add).then_inc(q1_rot, 1)

            def q1_low(b):
                dve.wait_ge(q1_hi, b + 1)
                nc.vector.tensor_tensor(Q1lo[:, tokens(b)], Qr[:, b, 0:S], Q1hi[:, tokens(b)].bitcast(fp32), ALU.subtract).then_inc(q1_ok, 1)

            def subtract_max(b, t):
                dve.wait_ge(nat1_ps[b], t + 1)
                got = PS[:, BANKS[b][2 + t % 2], 0:H1 * KC].rearrange("p (i k) -> p i k", i=H1)
                link(nc.vector.tensor_reduce(mx1[:, b, t, :], got, AX.X, ALU.max))
                nc.vector.tensor_tensor(Pn1[:, b, t, :].rearrange("p (i k) -> p i k", i=H1), got,
                                        mx1[:, b, t, :].unsqueeze(2).broadcast_to([P, H1, KC]), ALU.subtract).then_inc(sub1_ok[b], 1)

            def sums(b, t):
                dve.wait_ge(exp1_ok[b], t + 1)
                return nc.vector.reduce_sum(rs1[:, b, t, :], Pn1[:, b, t, :].rearrange("p (i k) -> p i k", i=H1), AX.X)

            def reciprocals(b):
                link(sums(b, NT - 1))
                link(nc.vector.reciprocal(rs1[:, b, :, :], rs1[:, b, :, :]))

            def normalise1(b):
                dve.wait_ge(pv1_ok[b], NT)
                nc.vector.tensor_tensor(On1[:, b, :, :].rearrange("p t (h d) -> p t h d", d=HD1),
                                        PS[:, BANKS[b][1], :].rearrange("p (t h d) -> p t h d", t=NT, h=H1),
                                        rs1[:, b, :, :].unsqueeze(3).broadcast_to([P, NT, H1, HD1]), ALU.mult).then_inc(on1_ok[b], 1)

            def residual1(b):
                dve.wait_ge(proj1_ps, b + 1)
                add_to_x(b, BANKS[b][1])

            def bc4(ap):
                return ap.unsqueeze(2).broadcast_to([P, NT, E1])

            def project(b):
                dve.wait_ge(pd_ps, b + 1)
                got = PS[:, BANKS[b][3], 0:NT * (PROJ + RSUM)].rearrange("p (t c) -> p t c", t=NT)
                link(nc.vector.tensor_tensor(pj[:, b, :, :], got[:, :, 0:PROJ], W1s[:, W1["bp"]].unsqueeze(1).broadcast_to([P, NT, PROJ]), ALU.add))
                link(nc.vector.tensor_tensor(sq[:, b, :, 0, :], pj[:, b, :, :], pj[:, b, :, :], ALU.mult))
                link(nc.vector.reduce_sum(ss[:, b, :], sq[:, b, :, 0, :], AX.X))
                nc.vector.tensor_scalar_max(ss[:, b, :], ss[:, b, :], 1e-24).then_inc(pss_ok, 1)
                nc.vector.tensor_copy(dn[:, b, :, :], got[:, :, PROJ:PROJ + RSUM])

            def match(b):
                link(nc.vector.tensor_tensor(sq[:, b, :, :, :], pj[:, b, :, :].unsqueeze(2).broadcast_to([P, NT, E1, PROJ]),
                                             simn[:, :, :].unsqueeze(1).broadcast_to([P, NT, E1, PROJ]), ALU.mult))
                link(nc.vector.reduce_sum(lg[:, b, :, :], sq[:, b, :, :, :], AX.X))

            def margins(b):
                dve.wait_ge(prn_ok, b + 1)
                link(nc.vector.tensor_tensor(lg[:, b, :, :], lg[:, b, :, :], bc4(rn[:, b, :]), ALU.mult))
                link(nc.vector.reduce_max(mx[:, b, :], lg[:, b, :, :], AX.X))
                nc.vector.tensor_tensor(ex[:, b, :, :], lg[:, b, :, :], bc4(mx[:, b, :]), ALU.subtract).then_inc(d_ok, 1)

            def choose_one(b):
                link(nc.vector.tensor_tensor(eq[:, b, :, :], lg[:, b, :, :], bc4(mx[:, b, :]), ALU.is_equal))
                link(nc.vector.tensor_tensor(eq[:, b, :, :], eq[:, b, :, :], C1s[:, C1["tie4"]].unsqueeze(1).broadcast_to([P, NT, E1]), ALU.mult))
                link(nc.vector.reduce_max(mx[:, b, :], eq[:, b, :, :], AX.X))
                link(nc.vector.tensor_tensor(eq[:, b, :, :], eq[:, b, :, :], bc4(mx[:, b, :]), ALU.is_equal))
                dve.wait_ge(ex_ok, b + 1)
                link(nc.vector.reduce_sum(lw[:, b, :], ex[:, b, :, :], AX.X))
                link(nc.vector.reciprocal(lw[:, b, :], lw[:, b, :]))
                link(nc.vector.tensor_tensor(eq[:, b, :, :], eq[:, b, :, :], bc4(lw[:, b, :]), ALU.mult))
                c = 0
                for e, r in enumerate(RANKS):
                    part = dn[:, b, :, c:c + r]
                    last = nc.vector.tensor_tensor(part, part, eq[:, b, :, e:e + 1].broadcast_to([P, NT, r]), ALU.mult)
                    c += r
                last.then_inc(gd_ok, 1)

            def finish(b):
                dve.wait_ge(f_ps, b + 1)
                add_to_x(b, BANKS[b][1])

            def second_residual():
                dve.wait_ge(y_ps, 2)
                add_to_x(1, BANKS[1][1])
                norm_stats(2, 1)

            rotate(0)
            second_residual()
            q1_low(0)
            norm_apply(2, 1)
            subtract_max(0, 0)
            subtract_max(0, 1)
            sums(0, 0)
            subtract_max(0, 2)
            sums(0, 1)
            subtract_max(0, 3)
            sums(0, 2)
            reciprocals(0)
            rotate(1)
            q1_low(1)
            normalise1(0)
            subtract_max(1, 0)
            sums(1, 0)
            subtract_max(1, 1)
            residual1(0)
            norm_stats(3, 0)
            subtract_max(1, 2)
            sums(1, 1)
            subtract_max(1, 3)
            norm_apply(3, 0)
            sums(1, 2)
            reciprocals(1)
            normalise1(1)
            project(0)
            residual1(1)
            norm_stats(3, 1)
            match(0)
            margins(0)
            norm_apply(3, 1)
            choose_one(0)
            project(1)
            match(1)
            finish(0)
            margins(1)
            choose_one(1)
            finish(1)

        @block.tensor
        def _(pe):
            def transposes(layer, b, bank):
                pe.wait_ge(z_ok[b], layer + 1)
                for t in range(NT):
                    last = nc.tensor.transpose(PS[:, bank, t * P:(t + 1) * P], Z[:, b * NT + t, :], ident)
                last.then_inc(zt_ps[b], 1)

            def q_proj(b, g):
                pe.wait_ge(zt_ok[b], 1)
                if b:
                    pe.wait_ge(q_ok, g + 1)
                nc.tensor.matmul(PS[0:96, QBANK[g], :], W0s[:, W0["q"]][:, 96 * g:96 * g + 96],
                                 ZT[:, tokens(b)], start=True, stop=True).then_inc(q_ps, 1)

            def nat(b, n):
                t, gp = n // 2, n % 2
                if b == 0:
                    bank = (4, 6)[n % 2]
                    if n < 2:
                        pe.wait_ge(q_ok, 2 * n + 2)
                    if n >= 2:
                        pe.wait_ge(nat_max, n - 1)
                else:
                    bank = 4
                    pe.wait_ge(nat_max, 8 + n)
                for g in (2 * gp, 2 * gp + 1):
                    last = nc.tensor.matmul(PS[:, bank + g % 2, 0:GH * KC], Qaug[0:96, b, g, t * P:(t + 1) * P],
                                            Kaug[0:96, b, g, :], start=True, stop=True)
                last.then_inc(nat_ps, 1)

            def max_rows(b):
                pe.wait_ge(m_cat, b + 1)
                pe.wait_ge(idr_ok, 1)
                for t in range(NT):
                    last = nc.tensor.matmul(PS[:, 4, t * P:(t + 1) * P], mcat[:, b, t, :], identr[:, :], start=True, stop=True)
                last.then_inc(m_ps, 1)

            def scores(b, hp):
                u = 8 * b + hp
                if hp % 2 == 0:
                    pe.wait_ge(m_ok, G0 * b + hp // 2 + 1)
                if u >= 2:
                    pe.wait_ge(exp_ok, u - 1)
                for j in range(2):
                    g, i = (2 * hp + j) // GH, (2 * hp + j) % GH
                    last = nc.tensor.matmul(PS[0:KC, 2 * (u % 2) + j, :], Kaug[:, b, g, i * KC:(i + 1) * KC],
                                            Qaug[:, b, g, :], start=True, stop=True)
                last.then_inc(sc_ps, 1)

            def values(b, hp):
                u, s = 8 * b + hp, hp // 4
                pe.wait_ge(exp_ok, u + 1)
                if b and hp % 4 == 0:
                    pe.wait_ge(acc_sb, s + 1)
                for j in range(2):
                    h = 2 * (hp % 4) + j
                    last = nc.tensor.matmul(PS[0:72, 6 + s, :], Vaug[:, b, s, 72 * h:72 * h + 72], PT[:, u % 3, j, :],
                                            start=(h == 0), stop=(h == SH - 1))
                last.then_inc(pv_ok, 1)

            def out_transposes(b, s, bank):
                pe.wait_ge(acc_sb, 2 * b + s + 1)
                if s and not b:
                    pe.wait_ge(on_ok, 1)
                for t in range(NT):
                    last = nc.tensor.transpose(PS[:, bank, 72 * t:72 * t + 72], Osb[:, s, t * P:(t + 1) * P], ident[0:72, 0:72])
                last.then_inc(on_ps, 1)

            def out_back(b, bank):
                pe.wait_ge(on_ok, 2 * b + 2)
                for t in range(NT):
                    last = nc.tensor.transpose(PS[:, bank, t * P:(t + 1) * P], On[:, t, :], ident)
                last.then_inc(ont_ps, 1)

            def out_proj(b, bank):
                pe.wait_ge(ont_ok, b + 1)
                for t in range(NT):
                    last = nc.tensor.matmul(PS[:, bank, t * P:(t + 1) * P], OnT[:, t * P:(t + 1) * P], W0s[:, W0["o"]],
                                            start=True, stop=True)
                last.then_inc(proj_ps, 1)

            def router(b, bank):
                pe.wait_ge(zt_ok[b], 2)
                for t in range(NT):
                    last = nc.tensor.matmul(PS[:, bank, t * E:(t + 1) * E], ZT[:, b * S + t * P:b * S + (t + 1) * P], W1s[:, W1["r"]], start=True, stop=True)
                last.then_inc(lg_ps, 1)

            pe.wait_ge(ld_wk, 16)
            pe.wait_ge(ld_ctx, 16)
            for g in range(G0):
                last = nc.tensor.matmul(PS[0:96, 6 + g // 2, (g % 2) * B * KC:(g % 2 + 1) * B * KC],
                                        W0s[:, W0["k"]][:, 96 * g:96 * g + 96], ctxT[:, :], start=True, stop=True)
                if g % 2:
                    last.then_inc(k_ps, 1)
            pe.wait_ge(ld_id, 16)
            transposes(0, 0, 0)
            pe.wait_ge(ld_wq, 16)
            for g in range(G0):
                q_proj(0, g)
            pe.wait_ge(ld_wvo, 16)
            for b in range(B):
                last = nc.tensor.matmul(PS[0:KC, 5, b * D:(b + 1) * D], ctxT[:, b * KC:(b + 1) * KC], W0s[:, W0["v"]],
                                        start=True, stop=True)
            last.then_inc(v_ps, 1)
            transposes(0, 1, 4)
            pe.wait_ge(k_ok[0], 1)
            pe.wait_ge(zt_ok[1], 1)
            pe.wait_ge(v_ok, B)
            for n in range(8):
                if n == 1:
                    pe.wait_ge(k_full, 2)
                nat(0, n)
                if n % 2:
                    q_proj(1, n // 2)
            max_rows(0)
            pe.wait_ge(q_ok, 2 * G0)
            pe.wait_ge(kones, 1)
            pe.wait_ge(k_ok[1], 1)
            for hp in range(8):
                scores(0, hp)
                if hp == 0:
                    pe.wait_ge(m_ok, G0)
                nat(1, hp)
                if hp:
                    values(0, hp - 1)
            values(0, 7)
            max_rows(1)
            for hp in range(8):
                scores(1, hp)
                if hp:
                    values(1, hp - 1)
                if hp == 0:
                    out_transposes(0, 0, 5)
                if hp == 1:
                    out_transposes(0, 1, 5)
                if hp == 2:
                    out_back(0, 5)
                if hp == 0:
                    pe.wait_ge(m_ok, 2 * G0)
                    pe.wait_ge(mn_ok, 1)
                    for b in range(B):
                        last = nc.tensor.transpose(PS[:, 4, b * KC:(b + 1) * KC], mn[:, b, :], ident[0:KC, 0:KC])
                    last.then_inc(mn_ps, 1)
                if hp == 1:
                    pe.wait_ge(w1s_ok, 1)
                    pe.wait_ge(mnt_ok, 1)
                    for n, name in enumerate(("k", "krot")):
                        nc.tensor.matmul(PS[:, 4, n * B * KC:(n + 1) * B * KC], W1s[:, W1[name]], mnT[:, :, :].rearrange("p b k -> p (b k)"), start=True, stop=True)
                    at = 2 * B * KC
                    for b in range(B):
                        last = nc.tensor.matmul(PS[0:KC, 4, at + b * HD1:at + (b + 1) * HD1], mnT[:, b, :], W1s[:, W1["v"]], start=True, stop=True)
                    last.then_inc(kv1_ps, 1)
                if hp == 3:
                    pe.wait_ge(k1_ok, 1)
                    out_proj(0, 4)
                if hp == 6:
                    pe.wait_ge(x_ok[0], 1)
                    transposes(1, 0, 4)
                if hp == 7:
                    out_transposes(1, 0, 6)
                    router(0, 5)
            values(1, 7)

            def gate_rows(b):
                pe.wait_ge(gcat_ok, b + 1)
                for t in range(NT):
                    last = nc.tensor.matmul(PS[0:2 * E, 6, t * P:(t + 1) * P], gcat[:, b * NT + t, :], identr[:, :], start=True, stop=True)
                last.then_inc(gt_ps, 1)

            def gate_spread(i, n):
                b, k = n // 2, n % 2
                if b == 0:
                    pe.wait_ge(gsel_ok, 2 * i + k + 1)
                nc.tensor.matmul(PS[:, 6 + k, :], gsel[:, k, :], gT[:, tokens(b)], start=True, stop=True).then_inc(gate_ps, 1)

            def three(to, half, k, c, right_hi, right_lo, start, stop):
                hi, lo = Whi[:, k, half, c * P:(c + 1) * P], Wlo[:, k, half, c * P:(c + 1) * P]
                nc.tensor.matmul(to, hi, right_hi, start=start, stop=False)
                nc.tensor.matmul(to, lo, right_hi, start=False, stop=False)
                return nc.tensor.matmul(to, hi, right_lo, start=False, stop=stop)

            def up(i, j, first=False):
                b, k, c = j // (2 * FC), j // FC % 2, j % FC
                if b == 0 and c == 0:
                    pe.wait_ge(w_up[k], i + 1)
                if not first:
                    pe.wait_ge(silu_ok, US * i + j - LAG + 1)
                three(PS[:, j % LAG, :], 0, k, c, Zhi[:, tokens(b)], Zlo[:, tokens(b)], True, True).then_inc(h_ps, 1)

            def down(i, j):
                b, k, c = j // (2 * FC), j // FC % 2, j % FC
                if b == 0 and c == 0:
                    pe.wait_ge(w_down[k], i + 1)
                pe.wait_ge(h_ok, US * i + j + 1)
                if c == 0:
                    pe.wait_ge(y_used, 4 * i + j // FC + 1)
                three(PS[:, 4 + k, :], 1, k, c, Hhi[:, j % NH, :], Hlo[:, j % NH, :], c == 0, c == FC - 1).then_inc(down_ok, 1)

            pe.wait_ge(zsplit_ok, 1)
            pe.wait_ge(exp_ok, 16)
            up(0, 0, True)
            up(0, 1, True)
            out_transposes(1, 1, 7)
            up(0, 2, True)
            up(0, 3, True)
            out_back(1, 6)
            pe.wait_ge(lg_read, 1)
            down(0, 0)
            out_proj(1, 7)
            for j in range(US):
                if j:
                    down(0, j)
                if j == 7:
                    pe.wait_ge(silu_ok, 2 * FC)
                    router(1, 3)
                    pe.wait_ge(zsplit_ok, 2)
                    for n in range(2 * FC, 2 * FC + LAG):
                        if n % LAG == 3:
                            pe.wait_ge(lg_read, 2)
                        up(0, n)
                elif not LAG <= j < 2 * FC:
                    up(j + LAG >= US, (j + LAG) % US)
                if j == 2:
                    gate_rows(0)
                if j == 4:
                    pe.wait_ge(gt_ok, 1)
                    gate_spread(0, 0)
                if j == 5:
                    pe.wait_ge(silu_ok, LAG + 1)
                    transposes(1, 1, 0)
                if j == 6:
                    pe.wait_ge(x_ok[1], 1)
                    gate_spread(0, 1)
                if j == 12:
                    gate_rows(1)
                if j == 13:
                    pe.wait_ge(gt_ok, 2)
                    gate_spread(0, 2)
                if j == 14:
                    gate_spread(0, 3)
            with pe.Fori(1, PAIRS - 1) as i:
                for j in range(US):
                    down(i, j)
                    up(i + (j + LAG) // US, (j + LAG) % US)
                    if j % FC == 1:
                        gate_spread(i, j // FC)

            def y_back(b, bank):
                pe.wait_ge(y_added, 4 * PAIRS - 2 * (1 - b))
                for t in range(NT):
                    last = nc.tensor.transpose(PS[:, bank, t * P:(t + 1) * P], Yacc[:, b * S + t * P:b * S + (t + 1) * P], ident)
                last.then_inc(y_ps, 1)

            for j in range(US):
                down(PAIRS - 1, j)
                if j + LAG < US:
                    up(PAIRS - 1, j + LAG)
                if j % FC == 1 and j < 13:
                    gate_spread(PAIRS - 1, j // FC)
                if j == 8:
                    y_back(0, BANKS[0][1])
                if j == 13:
                    pe.wait_ge(x_ok[0], 2)
                    gate_spread(PAIRS - 1, 3)
                if j == 14:
                    pe.wait_ge(silu_ok, PAIRS * US - FC + 1)
                    transposes(2, 0, 0)

            def q1_proj(b, n):
                pe.wait_ge(zt_ok[b], 3)
                pe.wait_ge(x_ok[b], 2)
                nc.tensor.matmul(PS[:, QBANK1[b][n], :], W1s[:, W1[("q", "qrot")[n]]], ZT[:, tokens(b)], start=True, stop=True).then_inc(q1_ps, 1)

            def nat1(b, t):
                if t == 0:
                    pe.wait_ge(q1_ok, b + 1)
                    pe.wait_ge(fill_ok, 1)
                    if b:
                        pe.wait_ge(q1_rot, 1)
                if t >= 2:
                    pe.wait_ge(sub1_ok[b], t - 1)
                to = PS[:, BANKS[b][2 + t % 2], 0:H1 * KC]
                at = slice(b * S + t * P, b * S + (t + 1) * P)
                nc.tensor.matmul(to, Q1hi[:, at], Kbhi[:, b, :], start=True, stop=False)
                nc.tensor.matmul(to, Q1hi[:, at], Kblo[:, b, :], start=False, stop=False)
                nc.tensor.matmul(to, Q1lo[:, at], Kbhi[:, b, :], start=False, stop=False)
                nc.tensor.matmul(to, onesr[:, :], fill[:, b, :], start=False, stop=True).then_inc(nat1_ps[b], 1)

            def turn(b, t):
                pe.wait_ge(exp1_ok[b], t + 1)
                if t:
                    pe.wait_ge(pt1_ok[b], t)
                elif b == 0:
                    pe.wait_ge(y_used, 4 * PAIRS + 2)
                for h in range(H1):
                    last = nc.tensor.transpose(PS[0:KC, BANKS[b][0], h * P:(h + 1) * P], Pn1[:, b, t, h * KC:(h + 1) * KC], ident)
                last.then_inc(tr1_ps[b], 1)

            def values1(b, t):
                pe.wait_ge(pt1_ok[b], t + 1)
                for h in range(H1):
                    at = t * P + h * HD1
                    last = nc.tensor.matmul(PS[:, BANKS[b][1], at:at + HD1], PT1[:, b, t % 2, h * P:(h + 1) * P],
                                            V1[:, b, :], start=True, stop=True)
                last.then_inc(pv1_ok[b], 1)

            def out1_back(b):
                pe.wait_ge(on1_ok[b], 1)
                for t in range(NT):
                    last = nc.tensor.transpose(PS[:, BANKS[b][3], t * P:(t + 1) * P], On1[:, b, t, :], ident)
                last.then_inc(ont1_ps, 1)

            def out1_proj(b):
                pe.wait_ge(ont1_ok, b + 1)
                for t in range(NT):
                    last = nc.tensor.matmul(PS[:, BANKS[b][1], t * P:(t + 1) * P], OnT1[:, b, t * P:(t + 1) * P], W1s[:, W1["o"]], start=True, stop=True)
                last.then_inc(proj1_ps, 1)

            def projections(b):
                pe.wait_ge(zt_ok[b], 4)
                w = PROJ + RSUM
                for t in range(NT):
                    last = nc.tensor.matmul(PS[:, BANKS[b][3], t * w:(t + 1) * w], ZT[:, b * S + t * P:b * S + (t + 1) * P], W1s[:, W1["pd"]], start=True, stop=True)
                last.then_inc(pd_ps, 1)

            def gated_down_rows(b):
                pe.wait_ge(gd_ok, b + 1)
                for t in range(NT):
                    last = nc.tensor.transpose(PS[0:RSUM, BANKS[b][2], t * P:(t + 1) * P], dn[:, b, t, :], ident)
                last.then_inc(gd_ps, 1)

            def base_product(b):
                pe.wait_ge(x_ok[b], 3)
                for t in range(NT):
                    nc.tensor.matmul(PS[:, BANKS[b][1], t * P:(t + 1) * P], ZT[:, b * S + t * P:b * S + (t + 1) * P], W1s[:, W1["base"]], start=(t == 0), stop=False)

            def last_product(b):
                pe.wait_ge(gdt_ok, b + 1)
                for t in range(NT):
                    last = nc.tensor.matmul(PS[:, BANKS[b][1], t * P:(t + 1) * P], gdT[:, b, t * P:(t + 1) * P], W1s[0:RSUM, W1["up"]], start=False, stop=(t == NT - 1))
                last.then_inc(f_ps, 1)

            pe.wait_ge(silu_ok, PAIRS * US)
            q1_proj(0, 0)
            q1_proj(0, 1)
            y_back(1, BANKS[1][1])
            nat1(0, 0)
            nat1(0, 1)
            transposes(2, 1, BANKS[1][0])
            nat1(0, 2)
            turn(0, 0)
            nat1(0, 3)
            q1_proj(1, 0)
            turn(0, 1)
            values1(0, 0)
            q1_proj(1, 1)
            turn(0, 2)
            values1(0, 1)
            turn(0, 3)
            values1(0, 2)
            values1(0, 3)
            nat1(1, 0)
            out1_back(0)
            nat1(1, 1)
            out1_proj(0)
            turn(1, 0)
            nat1(1, 2)
            turn(1, 1)
            values1(1, 0)
            nat1(1, 3)
            turn(1, 2)
            values1(1, 1)
            transposes(3, 0, BANKS[0][0])
            turn(1, 3)
            values1(1, 2)
            values1(1, 3)
            out1_back(1)
            projections(0)
            out1_proj(1)
            base_product(0)
            transposes(3, 1, BANKS[1][0])
            gated_down_rows(0)
            projections(1)
            last_product(0)
            base_product(1)
            gated_down_rows(1)
            last_product(1)


def kernel(**inputs):
    import numpy as np
    import concourse.bacc as bacc
    from concourse.bass_utils import run_bass_kernel_spmd as run

    a = {k: np.asarray(v) for k, v in inputs.items()}
    f4 = np.float32

    def pack(cols, width, **parts):
        out = np.zeros((P, width), f4)
        for name, (row, part) in parts.items():
            out[row:row + part.shape[0], cols[name]] = part
        return out

    row = np.arange(P)
    def block_mask(rows, per, heads):
        m = np.zeros((rows, heads, KC), f4)
        m[np.arange(rows), (np.arange(rows) // per) % heads, :] = 1
        return m.reshape(rows, -1)
    ones = np.zeros((32, GH, KC), f4)
    for i in range(GH):
        ones[i, i] = 1
        ones[GH + i, i] = 1
    vpat = np.zeros((KC, 2, 640), f4)
    for h in range(SH):
        vpat[:, :, 72 * h + 64 + h] = 1
    c0 = pack(C0, C0W, ident=(0, np.eye(P, dtype=f4)), block=(0, block_mask(96, HD0, GH)),
              ones=(96, ones.reshape(32, -1)), vpat=(0, vpat.reshape(KC, -1)))
    half = HD1 // 2
    timescale = np.power(f4(10000.0), f4(2.0 / HD1) * np.arange(half, dtype=f4)).astype(f4)
    def rope(pos):
        rad = pos.astype(f4)[None, :] / timescale[:, None]
        sin, cos = np.sin(rad), np.cos(rad)
        return np.tile(np.concatenate([cos, cos]), (H1, 1)), np.tile(np.concatenate([-sin, sin]), (H1, 1))
    qcos, qsin = rope(np.arange(KC, KC + S))
    kcos, ksin = rope(np.arange(KC))
    gsel = np.zeros((2 * E, E, P), f4)
    for e in range(E):
        gsel[e, e] = 1
        gsel[E + e, e] = 1
    c1 = pack(C1, C1W, qcos=(0, qcos), qsin=(0, qsin), kcos=(0, kcos), ksin=(0, ksin), block=(0, block_mask(P, HD1, H1)),
              gsel=(0, gsel.reshape(2 * E, -1)),
              tie8=(0, np.tile(np.arange(E, 0, -1, dtype=f4), (P, 1))), tie4=(0, np.tile(np.arange(E1, 0, -1, dtype=f4), (P, 1))))

    def thrice(w):
        w = w.T.reshape(D, G0, 1, GH * HD0)
        return np.broadcast_to(w, (D, G0, 3, GH * HD0)).reshape(D, -1)
    w0 = pack(W0, W0W, k=(0, thrice(a["L0_xattn_Wk"])), q=(0, thrice(a["L0_xattn_Wq"])),
              v=(0, a["L0_xattn_Wv"].T), o=(0, a["L0_xattn_Wo"].T))
    qw = a["L1_xattn_q_w"].transpose(1, 0, 2)
    swap = np.r_[half:HD1, 0:half]
    kw = a["L1_xattn_kv_w"][0, 0]
    downs = np.concatenate([a[f"L1_ffn_Wd{i}"] for i in range(E1)], 0).T
    ups = np.concatenate([a[f"L1_ffn_Wu{i}"] for i in range(E1)], 1).T
    w1 = pack(W1, W1W, r=(0, a["L0_ffn_Wr"].T), q=(0, qw.reshape(D, -1)), qrot=(0, qw[:, :, swap].reshape(D, -1)),
              k=(0, np.tile(kw, (1, H1))), krot=(0, np.tile(kw[:, swap], (1, H1))), v=(0, a["L1_xattn_kv_w"][1, 0]),
              o=(0, a["L1_xattn_out_w"].reshape(D, D)), rms=(0, a["L1_xattn_rms_scale"][:, None]),
              pd=(0, np.concatenate([a["L1_ffn_Wp"].T, downs], 1)), base=(0, a["L1_ffn_W"].T), up=(0, ups),
              bp=(0, np.tile(a["L1_ffn_bp"], (P, 1))), sim=(0, np.tile(a["L1_ffn_sim"].T.reshape(1, -1), (P, 1))),
              temp=(0, np.tile(a["L1_ffn_temp"], (P, 1))))
    up = a["L0_ffn_W1"].transpose(0, 2, 1)
    down = a["L0_ffn_W2"].reshape(E, D, FC, P).transpose(0, 3, 2, 1).reshape(E, P, FC * D)
    mask = np.zeros((B, KCP), np.bool_)
    mask[:, :KC] = a["mask_BxS2_bk0"]
    arrays = {
        "x": a["x"], "ctx_nat": a["ctx_1024"].transpose(1, 0, 2), "ctx_t": a["ctx_1024"].transpose(2, 0, 1).reshape(D, B * KC),
        "mask": mask.view(np.uint32).reshape(1, -1),
        "c0": c0, "w0": w0, "c1": c1, "w1": w1, "moe": np.concatenate([up, down], 2),
    }
    arrays = {k: np.ascontiguousarray(v) for k, v in arrays.items()}
    nc = bacc.Bacc("TRN2", target_bir_lowering=False, num_devices=1)
    args = [nc.dram_tensor(n, v.shape, mybir.dt.from_np(v.dtype), kind="ExternalInput").ap() for n, v in arrays.items()]
    args.append(nc.dram_tensor("out", (B, S, D), mybir.dt.float32, kind="ExternalOutput").ap())
    fused_layers(nc, *args)
    return run(nc, [arrays], core_ids=[0]).results[0]["out"]
```

```python
import concourse.bass as bass
from concourse import mybir
from contextlib import ExitStack

P = 128
B, S, D = 2, 512, 128
NT = S // P
TILES = B * NT
KC = 77
KCP = 80
H0, HD0 = 16, 8
GH = 4
G0 = H0 // GH
SETS = H0 // GH
VS = GH * HD0
VM = VS + GH + VS
VW = GH * (VM + HD0)
H1, HD1 = 4, 32
E, F = 8, 512
FC = F // P
E1 = 4
RANKS = [1, 2, 4, 8]
RSUM = sum(RANKS)
PROJ = 32
LAG = 4
NH = 2 * LAG
UE = B * FC
US = 2 * UE
PAIRS = E // 2
NEVER = -(2.0 ** 100)
CLAMP = 4.605170185988091

LAYERS = 4

def columns(*widths):
    out, at = {}, 0
    for name, n in widths:
        out[name] = slice(at, at + n)
        at += n
    return out, at

C0, C0W = columns(("ident", P), ("block", GH * KC), ("ones", GH * KC), ("fold", VS + GH))
W0, W0W = columns(("k", G0 * 96), ("q", G0 * 96), ("v", D), ("o", D))
C1, C1W = columns(("qcos", S), ("qsin", S), ("kcos", KC), ("ksin", KC), ("block", H1 * KC), 
                  ("gsel", E * P), ("tie8", E), ("tie4", E1))
W1, W1W = columns(("r", E), ("q", D), ("qrot", D), ("k", D), ("krot", D), ("v", HD1), ("o", D), ("rms", 1),
                  ("pd", PROJ + RSUM), ("base", D), ("up", D), ("bp", PROJ), ("sim", E1 * PROJ), ("temp", 1))


def fused_layers(nc, x, ctx_nat, ctx_t, mask, c0, w0, c1, w1, moe, out):
    fp32 = mybir.dt.float32
    f32r = mybir.dt.float32r
    u8 = mybir.dt.uint8
    ALU = mybir.AluOpType
    ACT = mybir.ActivationFunctionType
    AX = mybir.AxisListType

    with ExitStack() as ctx:
        def sb(name, shape, dt=fp32):
            return ctx.enter_context(nc.sbuf_tensor(name, shape, dt))

        def sem(name):
            return ctx.enter_context(nc.semaphore(name))

        def sems(name, n=B):
            return [sem(f"{name}{k}") for k in range(n)]

        PS = ctx.enter_context(nc.psum_tensor("PS", [P, 8, 512], fp32))

        C0s = sb("C0s", [P, C0W]); W0s = sb("W0s", [P, W0W])
        C1s = sb("C1s", [P, C1W]); W1s = sb("W1s", [P, W1W])
        ident = C0s[:, C0["ident"]]
        identr = sb("identr", [P, P], f32r)
        X = sb("X", [P, TILES, D])
        Z = sb("Z", [P, TILES, D])
        stats = sb("stats", [P, TILES, 6]); mv = sb("mv", [P, TILES, 2])
        rstd = sb("rstd", [P, TILES]); ve = sb("ve", [P, TILES]); mhalf = sb("mhalf", [P, TILES]); one = sb("one", [P, 1])
        ZT = sb("ZT", [P, B * S])
        ctxT = sb("ctxT", [P, B * KC])
        Kaug = sb("Kaug", [P, B, G0, GH * KC], f32r)
        Qaug = sb("Qaug", [P, B, G0, S], f32r)
        negm = sb("negm", [P, B, NT, G0, GH])
        mcat = sb("mcat", [P, B, NT, P], f32r)
        rs = sb("rs", [P, SETS, NT, GH])
        On = sb("On", [P, NT, D])
        OnT = sb("OnT", [P, S])
        shared = sb("shared", [P, 2464 + 3072 + 2048])
        Kf = shared[0:96, 0:2464].rearrange("p (b g i k) -> p b g i k", b=B, g=G0, i=GH)
        PT = shared[0:KC, 2464:5536].rearrange("p (u j n) -> p u j n", u=3, j=2)
        Osb = shared[0:VM, 5536:7584].rearrange("p (s n) -> p s n", s=SETS)
        Vp = sb("Vp", [P, B, SETS, VW], f32r)
        Zhi = sb("Zhi", [P, B * S], f32r); Zlo = sb("Zlo", [P, B * S], f32r)
        Wraw = sb("Wraw", [P, 2, 2, F]); Whi = sb("Whi", [P, 2, 2, F], f32r); Wlo = sb("Wlo", [P, 2, 2, F], f32r)
        Sf = sb("Sf", [P, LAG, S])
        Hhi = Qaug[:, :, :, :].rearrange("p b g n -> p (b g) n")
        Hlo = sb("Hlo", [P, NH, S], f32r)
        more_parts = sb("more_parts", [P, 4, S], f32r)
        PThi = [Hlo[:, 0:2, :], Hlo[:, 2:4, :], more_parts[:, 0:2, :]]
        PTlo = [Hlo[:, 4:6, :], Hlo[:, 6:8, :], more_parts[:, 2:4, :]]
        Lg = sb("Lg", [P, TILES, E]); top = sb("top", [P, B, 2, NT]); tie = sb("tie", [P, TILES, E]); tiem = sb("tiem", [P, TILES])
        pick = sb("pick", [P, B, 2, NT, E]); gw = sb("gw", [P, B, 2, NT]); gate = sb("gate", [P, TILES, E])
        gcat = sb("gcat", [P, TILES, 2 * E], f32r); gT = sb("gT", [2 * E, B * S], f32r)
        gsel = sb("gsel", [2 * E, 2, P], f32r)
        Gs = sb("Gs", [P, 2, S]); Yg = sb("Yg", [P, S]); Yacc = sb("Yacc", [P, B * S])
        ctxn = sb("ctxn", [KC, B, D]); cstat = sb("cstat", [KC, B]); crms = sb("crms", [KC, B]); mn = sb("mn", [KC, B, D])
        mnT = sb("mnT", [P, B, KC]); Kr = sb("Kr", [P, 2, B, KC]); Kb = sb("Kb", [P, B, H1, KC])
        Kbhi = sb("Kbhi", [P, B, H1 * KC], f32r); Kblo = sb("Kblo", [P, B, H1 * KC], f32r)
        V1 = sb("V1", [KC, B, HD1])
        maskw = sb("maskw", [1, B * KCP // 4], mybir.dt.uint32); keep = sb("keep", [1, B, KC])
        fill = sb("fill", [1, B, H1 * KC], f32r); onesf = sb("onesf", [1, P]); onesr = sb("onesr", [1, P], f32r)
        mx1 = sb("mx1", [P, B, NT, H1])
        Qr = Sf[:, :, :].rearrange("p (b n) s -> p b (n s)", b=B)
        Q1hi, Q1lo = Zhi, Zlo
        Pn1 = shared[:, 0:B * NT * H1 * KC].rearrange("p (b t k) -> p b t k", b=B, t=NT)
        PT1 = Wraw[0:KC, :, :, :]
        On1 = shared[:, 2464:3488].rearrange("p (b t n) -> p b t n", b=B, t=NT)
        OnT1 = shared[:, 3488:4512].rearrange("p (b n) -> p b n", b=B)
        gdT = shared[0:RSUM, 4512:4512 + B * S].rearrange("p (b n) -> p b n", b=B)
        sq = shared[:, 5536:5536 + B * NT * E1 * PROJ].rearrange("p (b t e j) -> p b t e j", b=B, t=NT, e=E1)
        rs1 = sb("rs1", [P, B, NT, H1])
        pj = sb("pj", [P, B, NT, PROJ]); dn = sb("dn", [P, B, NT, RSUM])
        ss = sb("ss", [P, B, NT]); rn = sb("rn", [P, B, NT]); lg = sb("lg", [P, B, NT, E1]); mx = sb("mx", [P, B, NT])
        ex = sb("ex", [P, B, NT, E1]); lw = sb("lw", [P, B, NT]); eq = sb("eq", [P, B, NT, E1])
        simq = Yg[:, 0:E1 * PROJ].rearrange("p (e n) -> p e n", e=E1)
        simn = sb("simn", [P, E1, PROJ]); sims = sb("sims", [P, E1]); tscale = sb("tscale", [P, 1])

        ld_x = sems("ld_x"); ld_id = sem("ld_id"); ld_ctx = sem("ld_ctx"); ld_wk = sem("ld_wk"); ld_wq = sem("ld_wq"); ld_wvo = sem("ld_wvo")
        ld_c0 = sem("ld_c0"); ld_c1 = sem("ld_c1"); ld_w1 = sem("ld_w1"); ld_ctxn = sem("ld_ctxn")
        ld_mask = sem("ld_mask"); ld_moe = sems("ld_moe")
        dve_step = sem("dve_step"); pool_step = sem("pool_step")
        stats_ok = sems("stats_ok"); rstd_ok = sems("rstd_ok"); z_ok = sems("z_ok"); zt_ps = sems("zt_ps"); zt_ok = sems("zt_ok"); x_ok = sems("x_ok")
        consts = sem("consts"); idr_ok = sem("idr_ok"); kones = sem("kones"); gsel_ok = sem("gsel_ok")
        k_ps = sem("k_ps"); k_full = sem("k_full"); k_hi = sem("k_hi"); k_ok = sems("k_ok"); v_ps = sem("v_ps"); v_clear = sem("v_clear"); v_hi = sem("v_hi"); v_ok = sem("v_ok")
        q_ps = sem("q_ps"); q_hi = sem("q_hi"); q_ok = sem("q_ok")
        nat_ps = sem("nat_ps"); nat_max = sem("nat_max"); m_cat = sem("m_cat"); m_ps = sem("m_ps"); m_ok = sem("m_ok")
        sc_ps = sem("sc_ps"); exp_ok = sem("exp_ok"); pt_hi = sems("pt_hi"); pt_lo = sems("pt_lo"); pv_ok = sem("pv_ok"); acc_sb = sem("acc_sb")
        on_ps = sem("on_ps"); on_ok = sem("on_ok"); ont_ps = sem("ont_ps"); ont_ok = sem("ont_ok"); proj_ps = sem("proj_ps")
        w_hi = sem("w_hi"); w_up = sems("w_up"); w_down = sems("w_down"); z_hi = sem("z_hi"); zsplit_ok = sem("zsplit_ok")
        lg_ps = sem("lg_ps"); lg_read = sem("lg_read"); margin = sem("margin"); gw_ok = sem("gw_ok"); gcat_ok = sem("gcat_ok")
        gt_ps = sem("gt_ps"); gt_ok = sem("gt_ok"); gate_ps = sem("gate_ps"); gate_sb = sems("gate_sb")
        h_ps = sem("h_ps"); silu_ok = sem("silu_ok"); h_hi = sem("h_hi"); h_ok = sem("h_ok"); down_ok = sem("down_ok")
        y_used = sem("y_used"); y_added = sem("y_added"); y_ps = sem("y_ps")
        c_ss = sem("c_ss"); c_rms = sem("c_rms"); mn_ok = sem("mn_ok"); mn_ps = sem("mn_ps"); mnt_ok = sem("mnt_ok")
        kv1_ps = sem("kv1_ps"); kv1_read = sem("kv1_read"); k1_ok = sem("k1_ok"); w1s_ok = sem("w1s_ok"); fill_ok = sem("fill_ok")
        q1_ps = sem("q1_ps"); q1_rot = sem("q1_rot"); q1_hi = sem("q1_hi"); q1_ok = sem("q1_ok")
        nat1_ps = sems("nat1_ps"); sub1_ok = sems("sub1_ok"); exp1_ok = sems("exp1_ok")
        tr1_ps = sems("tr1_ps"); pt1_ok = sems("pt1_ok"); pv1_ok = sems("pv1_ok")
        on1_ok = sems("on1_ok"); ont1_ps = sem("ont1_ps"); ont1_ok = sem("ont1_ok"); proj1_ps = sem("proj1_ps")
        sim_ss = sem("sim_ss"); sim_rn = sem("sim_rn"); t_min = sem("t_min"); t_exp = sem("t_exp")
        pd_ps = sem("pd_ps"); pss_ok = sem("pss_ok"); prn_ok = sem("prn_ok"); d_ok = sem("d_ok"); ex_ok = sem("ex_ok")
        gd_ok = sem("gd_ok"); gd_ps = sem("gd_ps"); gdt_ok = sem("gdt_ok"); f_ps = sem("f_ps")
        stored = sem("stored")

        x_d = x.rearrange("b (t p) d -> p (b t) d", p=P)
        out_d = out.rearrange("b (t p) d -> p (b t) d", p=P)
        QBANK = (1, 2, 3, 0)
        QBANK1 = ((3, 2), (5, 4))
        BANKS = ((6, 7, 0, 1), (4, 5, 2, 3))

        def tiles(b):
            return slice(b * NT, (b + 1) * NT)

        def tokens(b):
            return slice(b * S, (b + 1) * S)

        block = ctx.enter_context(nc.Block())

        @block.sync
        def _(sp):
            def part(cols):
                return w0[:, cols]
            sp.dma_start(X[:, tiles(0), :], x_d[:, tiles(0), :]).then_inc(ld_x[0], 16)
            sp.dma_start(W0s[:, W0["q"]], part(W0["q"])).then_inc(ld_wq, 16)
            sp.dma_start(X[:, tiles(1), :], x_d[:, tiles(1), :]).then_inc(ld_x[1], 16)
            sp.dma_start(W0s[:, W0["v"].start:W0["o"].stop], part(slice(W0["v"].start, W0["o"].stop))).then_inc(ld_wvo, 16)
            sp.dma_start(C1s[:, :], c1).then_inc(ld_c1, 16)
            sp.dma_start(W1s[:, :], w1).then_inc(ld_w1, 16)
            sp.dma_start(ctxn[:, :, :], ctx_nat).then_inc(ld_ctxn, 16)
            sp.dma_start(maskw[:, :], mask).then_inc(ld_mask, 16)
            for k in range(2):
                sp.dma_start(Wraw[:, k, :, :], moe[k]).then_inc(ld_moe[k], 16)
            with sp.Fori(1, PAIRS) as i:
                for k in range(2):
                    sp.wait_ge(w_down[k], i)
                    sp.dma_start(Wraw[:, k, :, :], moe[2 * i + k]).then_inc(ld_moe[k], 16)
            for b in range(B):
                sp.wait_ge(x_ok[b], LAYERS)
                sp.dma_start(out_d[:, tiles(b), :], X[:, tiles(b), :]).then_inc(stored, 16)
            sp.wait_ge(stored, 16 * B)

        @block.gpsimd
        def _(pool):
            def link(ins, count=[0]):
                count[0] += 1
                ins.then_inc(pool_step, 1)
                pool.wait_ge(pool_step, count[0])

            def inverse_root(layer, b):
                pool.wait_ge(stats_ok[b], layer + 1)
                nc.gpsimd.tensor_tensor(rstd[:, tiles(b)], ve[:, tiles(b)], mhalf[:, tiles(b)], ALU.pow).then_inc(rstd_ok[b], 1)
                pool.wait_ge(rstd_ok[b], layer + 1)

            def split_weights(i, k, half, ready, n):
                pool.wait_ge(ld_moe[k], 16 * i + 16)
                if ready:
                    pool.wait_ge(*ready)
                hi, lo, raw = Whi[:, k, half, :], Wlo[:, k, half, :], Wraw[:, k, half, :]
                nc.gpsimd.tensor_tensor(hi, raw, one[:, :].broadcast_to([P, F]), ALU.mult).then_inc(w_hi, 1)
                pool.wait_ge(w_hi, 4 * i + n + 1)
                done = (w_up, w_down)[half][k]
                nc.gpsimd.tensor_tensor(lo, raw, hi.bitcast(fp32), ALU.subtract).then_inc(done, 1)
                pool.wait_ge(done, i + 1)

            link(nc.gpsimd.memset(mhalf[:, :], -0.5))
            link(nc.gpsimd.memset(one[:, :], 1.0))
            link(nc.gpsimd.memset(Vp[:, :, :, :].bitcast(fp32), 0.0))
            for i in range(GH):
                last = nc.gpsimd.memset(Vp[0:KC, :, :, VM * i + VS + i:VM * i + VS + i + 1].bitcast(fp32), 1.0)
            last.then_inc(v_clear, 1)
            inverse_root(0, 0)
            pool.wait_ge(ld_id, 16)
            nc.gpsimd.tensor_copy(identr[:, :], ident).then_inc(idr_ok, 1)
            pool.wait_ge(idr_ok, 1)
            inverse_root(0, 1)
            nc.gpsimd.memset(mcat[:, :, :, :].bitcast(fp32), 0.0).then_inc(consts, 1)
            pool.wait_ge(consts, 1)
            nc.gpsimd.memset(Hlo[:, :, :].bitcast(fp32), 0.0).then_inc(consts, 1)
            pool.wait_ge(consts, 2)
            nc.gpsimd.memset(more_parts[:, :, :].bitcast(fp32), 0.0).then_inc(consts, 1)
            pool.wait_ge(consts, 3)
            split_weights(0, 0, 0, None, 0)
            split_weights(0, 1, 0, None, 1)
            pool.wait_ge(k_hi, 2)
            lo = Kaug[64:96, 1, :, :]
            nc.gpsimd.tensor_tensor(lo, Kf[64:96, 1, :, :, :].rearrange("p g i k -> p g (i k)"), lo.bitcast(fp32), ALU.subtract).then_inc(k_ok[1], 1)
            pool.wait_ge(k_ok[1], 1)
            split_weights(0, 0, 1, None, 2)
            split_weights(0, 1, 1, None, 3)

            def probs_low(u):
                pool.wait_ge(pt_hi[0], u + 1)
                nc.gpsimd.tensor_tensor(PTlo[u % 3][0:KC, 0, :], PT[:, u % 3, 0, :], PThi[u % 3][0:KC, 0, :].bitcast(fp32), ALU.subtract).then_inc(pt_lo[0], 1)
                pool.wait_ge(pt_lo[0], u + 1)

            pool.wait_ge(c_ss, 1)
            nc.gpsimd.tensor_tensor(crms[:, :], cstat[:, :], mhalf[0:KC, 0:B], ALU.pow).then_inc(c_rms, 1)
            pool.wait_ge(c_rms, 1)
            probs_low(0)
            pool.wait_ge(sim_ss, 1)
            nc.gpsimd.tensor_tensor(sims[:, :], sims[:, :], mhalf[:, 0:E1], ALU.pow).then_inc(sim_rn, 1)
            pool.wait_ge(sim_rn, 1)
            for u in range(1, 6):
                probs_low(u)
            probs_low(6)
            probs_low(7)
            pool.wait_ge(ld_c1, 16)

            def gate_picker(i, k, ready):
                if ready:
                    pool.wait_ge(*ready)
                nc.gpsimd.tensor_tensor(gsel[:, k, :], C1s[0:2 * E, bass.ds(C1["gsel"].start + (2 * i + k) * P, P)],
                                        one[0:2 * E, :].broadcast_to([2 * E, P]), ALU.mult).then_inc(gsel_ok, 1)
                pool.wait_ge(gsel_ok, 2 * i + k + 1)

            gate_picker(0, 0, None)
            gate_picker(0, 1, None)
            for u in range(8, 13):
                probs_low(u)
            inverse_root(1, 0)
            for u in range(13, 16):
                probs_low(u)
            inverse_root(1, 1)
            with pool.Fori(1, PAIRS) as i:
                split_weights(i, 0, 0, (h_ps, US * i - FC), 0)
                split_weights(i, 1, 0, (h_ps, US * i), 1)
                split_weights(i, 0, 1, (down_ok, US * i - FC), 2)
                gate_picker(i, 0, (gate_ps, 4 * i - 1))
                split_weights(i, 1, 1, (down_ok, US * i), 3)
                gate_picker(i, 1, (gate_ps, 4 * i))
            inverse_root(2, 0)
            inverse_root(2, 1)

            def proj_norms(b):
                pool.wait_ge(pss_ok, b + 1)
                nc.gpsimd.tensor_tensor(rn[:, b, :], ss[:, b, :], mhalf[:, 0:NT], ALU.pow).then_inc(prn_ok, 1)
                pool.wait_ge(prn_ok, b + 1)

            inverse_root(3, 0)
            proj_norms(0)
            inverse_root(3, 1)
            proj_norms(1)

        @block.scalar
        def _(act):
            act.dma_start(C0s[:, C0["ident"]], c0[:, C0["ident"]]).then_inc(ld_id, 16)
            act.dma_start(ctxT[:, :], ctx_t).then_inc(ld_ctx, 16)
            act.dma_start(W0s[:, W0["k"]], w0[:, W0["k"]]).then_inc(ld_wk, 16)
            act.dma_start(C0s[:, C0["block"].start:C0["fold"].stop], c0[:, C0["block"].start:C0["fold"].stop]).then_inc(ld_c0, 16)

            def copy(to, source):
                return nc.scalar.activation(to, source, ACT.Copy)

            def zt_copy(layer, b, bank):
                act.wait_ge(zt_ps[b], layer + 1)
                copy(ZT[:, tokens(b)], PS[:, bank, :]).then_inc(zt_ok[b], 1)

            def q_high(b, g):
                act.wait_ge(q_ps, G0 * b + g + 1)
                copy(Qaug[0:96, b, g, :], PS[0:96, QBANK[g], :]).then_inc(q_hi, 1)

            def k_high(b):
                act.wait_ge(k_full, b + 1)
                copy(Kaug[0:96, b, :, :], Kf[:, b, :, :, :].rearrange("p g i k -> p g (i k)")).then_inc(k_hi, 1)

            def m_rows(b):
                act.wait_ge(m_ps, b + 1)
                for g in range(G0):
                    copy(Qaug[96:P, b, g, :], PS[32 * g:32 * g + 32, 4, :]).then_inc(m_ok, 1)

            def exps(b, hp):
                u = 8 * b + hp
                act.wait_ge(sc_ps, u + 1)
                if u >= 3:
                    act.wait_ge(pt_lo[0], u - 2)
                    act.wait_ge(pt_lo[1], u - 2)
                bank = 2 * (u % 2)
                nc.scalar.activation(PT[:, u % 3, :, :], PS[0:KC, bank:bank + 2, :], ACT.Exp,
                                     scale=float(HD0) ** -0.5).then_inc(exp_ok, 1)
                act.wait_ge(exp_ok, u + 1)
                if u >= 3:
                    act.wait_ge(pv_ok, u - 2)
                copy(PThi[u % 3][0:KC, 0, :], PT[:, u % 3, 0, :]).then_inc(pt_hi[0], 1)

            def acc_copy(b, s):
                act.wait_ge(pv_ok, 8 * b + 2 * (s + 1))
                if b:
                    act.wait_ge(on_ps, s + 1)
                copy(Osb[:, s, :], PS[0:VM, 6 + s % 2, :]).then_inc(acc_sb, 1)

            def out_copy(b, bank):
                act.wait_ge(ont_ps, b + 1)
                copy(OnT[:, :], PS[:, bank, :]).then_inc(ont_ok, 1)

            def z_split(b, bank):
                act.wait_ge(zt_ps[b], 2)
                copy(ZT[:, tokens(b)], PS[:, bank, :]).then_inc(zt_ok[b], 1)
                copy(Zhi[:, tokens(b)], PS[:, bank, :]).then_inc(z_hi, 1)

            zt_copy(0, 0, 0)
            k_high(0)
            for g in range(G0):
                q_high(0, g)
            act.wait_ge(v_ps, 1)
            act.wait_ge(v_clear, 1)
            for b in range(B):
                copy(Vp[0:KC, b, :, :].rearrange("p s (i c) -> p s i c", i=GH)[:, :, :, 0:HD0],
                     PS[0:KC, 5, b * D:(b + 1) * D].rearrange("p (s i c) -> p s i c", s=SETS, c=HD0)).then_inc(v_hi, 1)
            zt_copy(0, 1, 4)
            copy(Kaug[96:P, :, :, :].rearrange("p b g n -> p (b g) n"),
                 C0s[96:P, C0["ones"]].unsqueeze(1).broadcast_to([32, B * G0, GH * KC])).then_inc(kones, 1)
            k_high(1)
            for g in range(G0):
                q_high(1, g)
            m_rows(0)
            act.wait_ge(consts, 3)
            for hp in range(8):
                exps(0, hp)
                if hp in (4, 6):
                    acc_copy(0, hp // 2 - 2)
            acc_copy(0, 2)
            m_rows(1)
            acc_copy(0, 3)
            for hp in range(8):
                exps(1, hp)
                if hp == 2:
                    out_copy(0, 5)
                if hp == 0:
                    act.wait_ge(mn_ps, 1)
                    copy(mnT[:, :, :], PS[:, 4, 0:B * KC].rearrange("p (b k) -> p b k", b=B)).then_inc(mnt_ok, 1)
                    act.wait_ge(t_min, 1)
                    nc.scalar.activation(tscale[:, :], tscale[:, :], ACT.Exp).then_inc(t_exp, 1)
                if hp in (4, 6):
                    acc_copy(1, hp // 2 - 2)
                if hp == 7:
                    z_split(0, 5)
            nc.scalar.preload_act_table(ACT.Silu)
            acc_copy(1, 2)
            acc_copy(1, 3)

            def hidden(i, j, first=False):
                act.wait_ge(h_ps, US * i + j + 1)
                if not (first and j < LAG):
                    act.wait_ge(h_ok, US * i + j - LAG + 1)
                nc.scalar.activation(Sf[:, j % LAG, :], PS[:, j % LAG, :], ACT.Silu).then_inc(silu_ok, 1)
                act.wait_ge(silu_ok, US * i + j + 1)
                if not (first and j < NH):
                    act.wait_ge(down_ok, US * i + j - NH + 1)
                copy(Hhi[:, j % NH, :], Sf[:, j % LAG, :]).then_inc(h_hi, 1)

            def half_tanh(b):
                act.wait_ge(margin, b + 1)
                nc.scalar.activation(gw[:, b, 0, :], gw[:, b, 0, :], ACT.Tanh, scale=0.5).then_inc(gw_ok, 1)

            def gate_rows(b):
                act.wait_ge(gt_ps, b + 1)
                copy(gT[:, tokens(b)], PS[0:2 * E, 7 - b, :]).then_inc(gt_ok, 1)

            def gate_copy(i, b):
                act.wait_ge(gate_ps, 4 * i + 2 * b + 1)
                act.wait_ge(y_used, 4 * i + 2 * b + 1)
                copy(Gs[:, 0, :], PS[:, 6, :]).then_inc(gate_sb[0], 1)

            for j in range(LAG):
                if j == 2:
                    half_tanh(0)
                    out_copy(1, 7)
                hidden(0, j, True)
            for j in range(US):
                hidden(j + LAG >= US, (j + LAG) % US, j + LAG < US)
                if j == 2:
                    gate_rows(0)
                if j == 3:
                    gate_copy(0, 0)
                    z_split(1, 0)
                if j == 8:
                    half_tanh(1)
                if j == 13:
                    gate_rows(1)
                if j == 14:
                    gate_copy(0, 1)
            with act.Fori(1, PAIRS - 1) as i:
                for j in range(US):
                    hidden(i + (j + LAG) // US, (j + LAG) % US)
                    if j in (2, 10):
                        gate_copy(i, j // 8)
            for j in range(US - LAG):
                hidden(PAIRS - 1, j + LAG)
                if j in (2, 10):
                    gate_copy(PAIRS - 1, j // 8)
            nc.scalar.preload_act_table(ACT.Exp)

            def q1_high(b):
                act.wait_ge(q1_rot, b + 1)
                copy(Q1hi[:, tokens(b)], Qr[:, b, 0:S]).then_inc(q1_hi, 1)

            def exp1(b, t):
                act.wait_ge(sub1_ok[b], t + 1)
                nc.scalar.activation(Pn1[:, b, t, :], Pn1[:, b, t, :], ACT.Exp, scale=float(HD1) ** -0.5).then_inc(exp1_ok[b], 1)

            def turned_copy(b, t):
                act.wait_ge(tr1_ps[b], t + 1)
                if t >= 2:
                    act.wait_ge(pv1_ok[b], t - 1)
                copy(PT1[:, b, t % 2, :], PS[0:KC, BANKS[b][0], :]).then_inc(pt1_ok[b], 1)

            def out1_copy(b):
                act.wait_ge(ont1_ps, b + 1)
                copy(OnT1[:, b, :], PS[:, BANKS[b][3], :]).then_inc(ont1_ok, 1)

            def low_rank_exp(b):
                act.wait_ge(d_ok, b + 1)
                nc.scalar.activation(ex[:, b, :, :], ex[:, b, :, :], ACT.Exp).then_inc(ex_ok, 1)

            def gated_down_copy(b):
                act.wait_ge(gd_ps, b + 1)
                copy(gdT[:, b, :], PS[0:RSUM, BANKS[b][2], :]).then_inc(gdt_ok, 1)

            zt_copy(2, 0, 0)
            q1_high(0)
            exp1(0, 0)
            zt_copy(2, 1, BANKS[1][0])
            exp1(0, 1)
            turned_copy(0, 0)
            exp1(0, 2)
            turned_copy(0, 1)
            exp1(0, 3)
            turned_copy(0, 2)
            turned_copy(0, 3)
            q1_high(1)
            exp1(1, 0)
            out1_copy(0)
            exp1(1, 1)
            turned_copy(1, 0)
            exp1(1, 2)
            turned_copy(1, 1)
            exp1(1, 3)
            turned_copy(1, 2)
            zt_copy(3, 0, BANKS[0][0])
            turned_copy(1, 3)
            out1_copy(1)
            low_rank_exp(0)
            zt_copy(3, 1, BANKS[1][0])
            gated_down_copy(0)
            low_rank_exp(1)
            gated_down_copy(1)

        @block.vector
        def _(dve):
            def link(ins, count=[0]):
                count[0] += 1
                ins.then_inc(dve_step, 1)
                dve.wait_ge(dve_step, count[0])

            def norm_stats(layer, b):
                dve.wait_ge(ld_x[b], 16) if layer == 0 else dve.wait_ge(x_ok[b], layer)
                for t in range(b * NT, (b + 1) * NT):
                    last = nc.vector.bn_stats(stats[:, t, :], X[:, t, :])
                link(last)
                for t in range(b * NT, (b + 1) * NT):
                    last = nc.vector.bn_aggr(mv[:, t, :], stats[:, t, :])
                link(last)
                e1, e2 = 1e-5, 1e-6
                a, c = (1.0 + e2, e1 * e2) if layer == 2 else (1.0, e1)
                nc.vector.tensor_scalar(ve[:, tiles(b)], mv[:, tiles(b), 1], a, c, ALU.mult, ALU.add).then_inc(stats_ok[b], 1)

            def norm_apply(layer, b):
                dve.wait_ge(rstd_ok[b], layer + 1)
                for t in range(b * NT, (b + 1) * NT):
                    last = nc.vector.tensor_scalar(Z[:, t, :], X[:, t, :], mv[:, t, 0:1], rstd[:, t:t + 1],
                                                   ALU.subtract, ALU.mult)
                last.then_inc(z_ok[b], 1)

            def add_to_x(b, bank):
                nc.vector.tensor_tensor(X[:, tiles(b), :], PS[:, bank, :].rearrange("p (t d) -> p t d", d=D),
                                        X[:, tiles(b), :], ALU.add).then_inc(x_ok[b], 1)

            def k_block(b, g):
                dve.wait_ge(k_ps, g // 2 + 1)
                src = PS[0:96, 6 + g // 2, (g % 2) * B * KC + b * KC:(g % 2) * B * KC + (b + 1) * KC]
                ins = nc.vector.tensor_tensor(Kf[:, b, g, :, :], src.unsqueeze(1).broadcast_to([96, GH, KC]),
                                              C0s[0:96, C0["block"]].rearrange("p (i k) -> p i k", i=GH), ALU.mult)
                if g == G0 - 1:
                    ins.then_inc(k_full, 1)

            def k_low():
                dve.wait_ge(k_hi, 1)
                lo = Kaug[64:96, 0, :, :]
                nc.vector.tensor_tensor(lo, Kf[64:96, 0, :, :, :].rearrange("p g i k -> p g (i k)"), lo.bitcast(fp32), ALU.subtract).then_inc(k_ok[0], 1)

            def q_low(b, g):
                dve.wait_ge(q_hi, G0 * b + g + 1)
                lo = Qaug[32:64, b, g, :]
                nc.vector.tensor_tensor(lo, PS[32:64, QBANK[g], :], lo.bitcast(fp32), ALU.subtract).then_inc(q_ok, 1)

            def nat(b, n):
                u = 8 * b + n
                t, gp = n // 2, n % 2
                bank = (4, 6)[n % 2] if b == 0 else 4
                dve.wait_ge(nat_ps, u + 1)
                nc.vector.tensor_reduce(negm[:, b, t, 2 * gp:2 * gp + 2, :],
                                        PS[:, bank:bank + 2, 0:GH * KC].rearrange("p g (i k) -> p g i k", i=GH),
                                        AX.X, ALU.max, negate=True).then_inc(nat_max, 1)

            def max_parts(b):
                dve.wait_ge(nat_max, 8 * (b + 1))
                dve.wait_ge(consts, 1)
                parts = mcat[:, b, :, :].rearrange("p t (g c) -> p t g c", g=G0)
                for part in (0, 1):
                    for t in range(NT):
                        if part == 0:
                            ins = nc.vector.tensor_copy(parts[:, t, :, 0:GH], negm[:, b, t, :, :])
                        else:
                            ins = nc.vector.tensor_tensor(parts[:, t, :, GH:2 * GH], negm[:, b, t, :, :],
                                                          parts[:, t, :, 0:GH].bitcast(fp32), ALU.subtract)
                    if part == 0:
                        link(ins)
                ins.then_inc(m_cat, 1)

            def normalise(b, half, bank):
                dve.wait_ge(on_ps, SETS * b + 2 * half + 2)
                for s in range(2):
                    at = 2 * half + s
                    got = PS[:, bank, 0:NT * 72].rearrange("p (t s c) -> p t s c", s=2, c=VS + GH)[:, :, s, :]
                    link(nc.vector.reciprocal(rs[:, at, :, :], got[:, :, VS:VS + GH]))
                    if b and not at:
                        dve.wait_ge(ont_ps, b)
                    last = nc.vector.tensor_tensor(On[:, :, VS * at:VS * at + VS].rearrange("p t (h d) -> p t h d", d=HD0),
                                                   got[:, :, 0:VS].rearrange("p t (h d) -> p t h d", d=HD0),
                                                   rs[:, at, :, :].unsqueeze(3).broadcast_to([P, NT, GH, HD0]), ALU.mult)
                last.then_inc(on_ok, 1)

            def v_low():
                dve.wait_ge(v_hi, B)
                for b in range(B):
                    heads = Vp[0:KC, b, :, :].rearrange("p s (i c) -> p s i c", i=GH)
                    nc.vector.tensor_tensor(heads[:, :, :, VS + GH:VS + GH + HD0], PS[0:KC, 5, b * D:(b + 1) * D].rearrange("p (s i c) -> p s i c", s=SETS, c=HD0),
                                            heads[:, :, :, 0:HD0].bitcast(fp32), ALU.subtract).then_inc(v_ok, 1)

            def probs_parts(u):
                if u == 0:
                    dve.wait_ge(consts, 3)
                dve.wait_ge(exp_ok, u + 1)
                if u >= 3:
                    dve.wait_ge(pv_ok, u - 2)
                hi = PThi[u % 3][0:KC, 1, :]
                nc.vector.tensor_copy(hi, PT[:, u % 3, 1, :]).then_inc(pt_hi[1], 1)
                dve.wait_ge(pt_hi[1], u + 1)
                nc.vector.tensor_tensor(PTlo[u % 3][0:KC, 1, :], PT[:, u % 3, 1, :], hi.bitcast(fp32), ALU.subtract).then_inc(pt_lo[1], 1)

            def z_low(b, bank):
                dve.wait_ge(z_hi, b + 1)
                dve.wait_ge(zt_ok[b], 2)
                nc.vector.tensor_tensor(Zlo[:, tokens(b)], PS[:, bank, :], Zhi[:, tokens(b)].bitcast(fp32),
                                        ALU.subtract).then_inc(zsplit_ok, 1)

            def context_norms():
                dve.wait_ge(ld_ctxn, 16)
                link(nc.vector.tensor_tensor(mn[:, :, :], ctxn[:, :, :], ctxn[:, :, :], ALU.mult))
                link(nc.vector.reduce_sum(cstat[:, :], mn[:, :, :], AX.X))
                nc.vector.tensor_scalar(cstat[:, :], cstat[:, :], 1.0 / D, 1e-6, ALU.mult, ALU.add).then_inc(c_ss, 1)

            def weights_second():
                dve.wait_ge(ld_w1, 16)
                sim = W1s[:, W1["sim"]].rearrange("p (e n) -> p e n", e=E1)
                link(nc.vector.tensor_tensor(simq[:, :, :], sim, sim, ALU.mult))
                link(nc.vector.reduce_sum(sims[:, :], simq[:, :, :], AX.X))
                nc.vector.tensor_scalar_max(sims[:, :], sims[:, :], 1e-24).then_inc(sim_ss, 1)
                nc.vector.tensor_scalar_min(tscale[:, :], W1s[:, W1["temp"]], CLAMP).then_inc(t_min, 1)
                link(nc.vector.tensor_scalar_add(W1s[:, W1["rms"]], W1s[:, W1["rms"]], 1.0))
                scaled = W1s[:, W1["q"].start:W1["v"].stop]
                nc.vector.tensor_scalar(scaled, scaled, W1s[:, W1["rms"]], None, ALU.mult).then_inc(w1s_ok, 1)

            def mask_rows():
                dve.wait_ge(ld_mask, 16)
                link(nc.vector.tensor_copy(keep[:, :, :], maskw[:, :].bitcast(u8).rearrange("p (b k) -> p b k", b=B)[:, :, 0:KC]))
                link(nc.vector.memset(onesf[:, :], 1.0))
                link(nc.vector.tensor_copy(onesr[:, :], onesf[:, :]))
                nc.vector.tensor_scalar(fill[:, :, :].rearrange("p b (i k) -> p b i k", i=H1), keep[:, :, :].unsqueeze(2).broadcast_to([1, B, H1, KC]),
                                        -1.0, -NEVER, ALU.add, ALU.mult).then_inc(fill_ok, 1)

            def context_rows():
                dve.wait_ge(c_rms, 1)
                for b in range(B):
                    last = nc.vector.tensor_scalar(mn[:, b, :], ctxn[:, b, :], crms[:, b:b + 1], None, ALU.mult)
                last.then_inc(mn_ok, 1)

            def prepare_keys():
                dve.wait_ge(kv1_ps, 1)
                nc.vector.tensor_copy(V1[:, :, :], PS[0:KC, 4, 2 * B * KC:2 * B * KC + B * HD1].rearrange("p (b d) -> p b d", b=B))
                dve.wait_ge(ld_c1, 16)
                for n, table in enumerate(("kcos", "ksin")):
                    last = nc.vector.tensor_tensor(Kr[:, n, :, :], PS[:, 4, n * B * KC:(n + 1) * B * KC].rearrange("p (b k) -> p b k", b=B),
                                                   C1s[:, C1[table]].unsqueeze(1).broadcast_to([P, B, KC]), ALU.mult)
                last.then_inc(kv1_read, 1)

            def key_blocks():
                dve.wait_ge(kv1_read, 1)
                link(nc.vector.tensor_tensor(Kr[:, 0, :, :], Kr[:, 0, :, :], Kr[:, 1, :, :], ALU.add))
                link(nc.vector.tensor_tensor(Kb[:, :, :, :], Kr[:, 0, :, :].unsqueeze(2).broadcast_to([P, B, H1, KC]),
                                             C1s[:, C1["block"]].rearrange("p (i k) -> p i k", i=H1).unsqueeze(1).broadcast_to([P, B, H1, KC]), ALU.mult))

            def key_parts():
                whole = Kb[:, :, :, :].rearrange("p b i k -> p b (i k)")
                link(nc.vector.tensor_copy(Kbhi[:, :, :], whole))
                nc.vector.tensor_tensor(Kblo[:, :, :], whole, Kbhi[:, :, :].bitcast(fp32), ALU.subtract).then_inc(k1_ok, 1)

            def directions():
                dve.wait_ge(sim_rn, 1)
                dve.wait_ge(t_exp, 1)
                link(nc.vector.tensor_scalar(sims[:, :], sims[:, :], tscale[:, :], None, ALU.mult))
                link(nc.vector.tensor_tensor(simn[:, :, :], W1s[:, W1["sim"]].rearrange("p (e n) -> p e n", e=E1),
                                             sims[:, :].unsqueeze(2).broadcast_to([P, E1, PROJ]), ALU.mult))

            nc.vector.memset(Yacc[:, :], 0.0).then_inc(y_used, 2)
            norm_stats(0, 0)
            norm_apply(0, 0)
            dve.wait_ge(ld_c0, 16)
            for g in range(G0):
                k_block(0, g)
            norm_stats(0, 1)
            k_low()
            norm_apply(0, 1)
            q_low(0, 0)
            k_block(1, 0)
            k_block(1, 1)
            q_low(0, 1)
            q_low(0, 2)
            k_block(1, 2)
            k_block(1, 3)
            q_low(0, 3)
            v_low()
            for n in range(8):
                nat(0, n)
                if n % 2 and n > 2:
                    q_low(1, n // 2 - 1)
            max_parts(0)
            q_low(1, 3)
            context_norms()
            weights_second()
            for n in range(8):
                nat(1, n)
                if n == 0:
                    context_rows()
                else:
                    probs_parts(n - 1)
            max_parts(1)
            probs_parts(7)
            normalise(0, 0, 5)
            mask_rows()
            for u in range(8, 16):
                probs_parts(u)
                if u == 8:
                    normalise(0, 1, 5)
                if u == 9:
                    prepare_keys()
                if u == 10:
                    key_blocks()
                if u == 11:
                    dve.wait_ge(proj_ps, 1)
                    add_to_x(0, 4)
                    norm_stats(1, 0)
                if u == 12:
                    norm_apply(1, 0)
                if u == 14:
                    key_parts()
            z_low(0, 5)

            def logits_copy(b, bank):
                dve.wait_ge(lg_ps, b + 1)
                nc.vector.tensor_copy(Lg[:, tiles(b), :], PS[:, bank, 0:NT * E].rearrange("p (t e) -> p t e", e=E)).then_inc(lg_read, 1)
                dve.wait_ge(lg_read, b + 1)

            def choose(b, n):
                def bc(ap):
                    return ap.unsqueeze(2).broadcast_to([P, NT, E])
                row, tied = Lg[:, tiles(b), :], tie[:, tiles(b), :]
                if n == 1:
                    link(nc.vector.scalar_tensor_tensor(row, pick[:, b, 0, :, :], -3.0e38, row, ALU.mult, ALU.add))
                link(nc.vector.tensor_reduce(top[:, b, n, :], row, AX.X, ALU.max))
                if n == 1:
                    nc.vector.tensor_tensor(gw[:, b, 0, :], top[:, b, 0, :], top[:, b, 1, :], ALU.subtract).then_inc(margin, 1)
                link(nc.vector.tensor_tensor(tied, row, bc(top[:, b, n, :]), ALU.is_equal))
                link(nc.vector.tensor_tensor(tied, tied, C1s[:, C1["tie8"]].unsqueeze(1).broadcast_to([P, NT, E]), ALU.mult))
                link(nc.vector.tensor_reduce(tiem[:, tiles(b)], tied, AX.X, ALU.max))
                link(nc.vector.tensor_tensor(pick[:, b, n, :, :], tied, bc(tiem[:, tiles(b)]), ALU.is_equal))

            def weigh(b):
                def bc(ap):
                    return ap.unsqueeze(2).broadcast_to([P, NT, E])
                dve.wait_ge(gw_ok, b + 1)
                nc.vector.tensor_scalar(gw[:, b, 1, :], gw[:, b, 0, :], -0.5, 0.5, ALU.mult, ALU.add)
                link(nc.vector.tensor_scalar(gw[:, b, 0, :], gw[:, b, 0, :], 0.5, 0.5, ALU.mult, ALU.add))
                g = gate[:, tiles(b), :]
                nc.vector.tensor_tensor(g, pick[:, b, 0, :, :], bc(gw[:, b, 0, :]), ALU.mult)
                link(nc.vector.tensor_tensor(tie[:, tiles(b), :], pick[:, b, 1, :, :], bc(gw[:, b, 1, :]), ALU.mult))
                link(nc.vector.tensor_tensor(g, g, tie[:, tiles(b), :], ALU.add))
                link(nc.vector.tensor_copy(gcat[:, tiles(b), 0:E], g))
                nc.vector.tensor_tensor(gcat[:, tiles(b), E:2 * E], g, gcat[:, tiles(b), 0:E].bitcast(fp32), ALU.subtract).then_inc(gcat_ok, 1)

            def hidden_low(i, j):
                dve.wait_ge(h_hi, US * i + j + 1)
                nc.vector.tensor_tensor(Hlo[:, j % NH, :], Sf[:, j % LAG, :], Hhi[:, j % NH, :].bitcast(fp32), ALU.subtract).then_inc(h_ok, 1)

            def gated(i, n):
                b, k = n // 2, n % 2
                if k == 0:
                    dve.wait_ge(gate_sb[0], 2 * i + b + 1)
                else:
                    dve.wait_ge(gate_ps, 4 * i + n + 1)
                    nc.vector.tensor_copy(Gs[:, 1, :], PS[:, 7, :]).then_inc(gate_sb[1], 1)
                    dve.wait_ge(gate_sb[1], 2 * i + b + 1)
                dve.wait_ge(down_ok, US * i + FC * (n + 1))
                nc.vector.tensor_tensor(Yg[:, :], PS[:, 4 + k, :], Gs[:, k, :], ALU.mult).then_inc(y_used, 1)
                dve.wait_ge(y_used, 4 * i + n + 3)
                acc = Yacc[:, tokens(b)]
                nc.vector.tensor_tensor(acc, acc, Yg[:, :], ALU.add).then_inc(y_added, 1)
                dve.wait_ge(y_added, 4 * i + n + 1)

            normalise(1, 0, 4)
            logits_copy(0, 4)
            choose(0, 0)
            normalise(1, 1, 6)
            choose(0, 1)
            hidden_low(0, 0)
            hidden_low(0, 1)
            weigh(0)
            hidden_low(0, 2)
            dve.wait_ge(proj_ps, 2)
            add_to_x(1, 6)
            norm_stats(1, 1)
            hidden_low(0, 3)
            for j in range(US):
                hidden_low(j + LAG >= US, (j + LAG) % US)
                if j == 0:
                    norm_apply(1, 1)
                if j == 3:
                    gated(0, 0)
                    z_low(1, 0)
                    logits_copy(1, 3)
                if j == 5:
                    choose(1, 0)
                if j == 6:
                    choose(1, 1)
                if j == 7:
                    gated(0, 1)
                if j == 10:
                    weigh(1)
                if j == 14:
                    gated(0, 2)
                if j == 15:
                    gated(0, 3)
                    directions()
            with dve.Fori(1, PAIRS - 1) as i:
                for j in range(US):
                    hidden_low(i + (j + LAG) // US, (j + LAG) % US)
                    if j % FC == FC - 1:
                        gated(i, j // FC)
            for j in range(US):
                if j + LAG < US:
                    hidden_low(PAIRS - 1, j + LAG)
                if j % FC == FC - 1:
                    gated(PAIRS - 1, j // FC)
                if j == 9:
                    dve.wait_ge(y_ps, 1)
                    add_to_x(0, BANKS[0][1])
                    norm_stats(2, 0)
                if j == 10:
                    norm_apply(2, 0)

            def rotate(b):
                for n, table in enumerate(("qcos", "qsin")):
                    dve.wait_ge(q1_ps, 2 * b + n + 1)
                    last = nc.vector.tensor_tensor(Qr[:, b, n * S:(n + 1) * S], PS[:, QBANK1[b][n], :], C1s[:, C1[table]], ALU.mult)
                link(last)
                nc.vector.tensor_tensor(Qr[:, b, 0:S], Qr[:, b, 0:S], Qr[:, b, S:2 * S], ALU.add).then_inc(q1_rot, 1)

            def q1_low(b):
                dve.wait_ge(q1_hi, b + 1)
                nc.vector.tensor_tensor(Q1lo[:, tokens(b)], Qr[:, b, 0:S], Q1hi[:, tokens(b)].bitcast(fp32), ALU.subtract).then_inc(q1_ok, 1)

            def subtract_max(b, t):
                dve.wait_ge(nat1_ps[b], t + 1)
                got = PS[:, BANKS[b][2 + t % 2], 0:H1 * KC].rearrange("p (i k) -> p i k", i=H1)
                link(nc.vector.tensor_reduce(mx1[:, b, t, :], got, AX.X, ALU.max))
                nc.vector.tensor_tensor(Pn1[:, b, t, :].rearrange("p (i k) -> p i k", i=H1), got,
                                        mx1[:, b, t, :].unsqueeze(2).broadcast_to([P, H1, KC]), ALU.subtract).then_inc(sub1_ok[b], 1)

            def sums(b, t):
                dve.wait_ge(exp1_ok[b], t + 1)
                return nc.vector.reduce_sum(rs1[:, b, t, :], Pn1[:, b, t, :].rearrange("p (i k) -> p i k", i=H1), AX.X)

            def reciprocals(b):
                link(sums(b, NT - 1))
                link(nc.vector.reciprocal(rs1[:, b, :, :], rs1[:, b, :, :]))

            def normalise1(b):
                dve.wait_ge(pv1_ok[b], NT)
                nc.vector.tensor_tensor(On1[:, b, :, :].rearrange("p t (h d) -> p t h d", d=HD1),
                                        PS[:, BANKS[b][1], :].rearrange("p (t h d) -> p t h d", t=NT, h=H1),
                                        rs1[:, b, :, :].unsqueeze(3).broadcast_to([P, NT, H1, HD1]), ALU.mult).then_inc(on1_ok[b], 1)

            def residual1(b):
                dve.wait_ge(proj1_ps, b + 1)
                add_to_x(b, BANKS[b][1])

            def bc4(ap):
                return ap.unsqueeze(2).broadcast_to([P, NT, E1])

            def project(b):
                dve.wait_ge(pd_ps, b + 1)
                got = PS[:, BANKS[b][3], 0:NT * (PROJ + RSUM)].rearrange("p (t c) -> p t c", t=NT)
                link(nc.vector.tensor_tensor(pj[:, b, :, :], got[:, :, 0:PROJ], W1s[:, W1["bp"]].unsqueeze(1).broadcast_to([P, NT, PROJ]), ALU.add))
                link(nc.vector.tensor_tensor(sq[:, b, :, 0, :], pj[:, b, :, :], pj[:, b, :, :], ALU.mult))
                link(nc.vector.reduce_sum(ss[:, b, :], sq[:, b, :, 0, :], AX.X))
                nc.vector.tensor_scalar_max(ss[:, b, :], ss[:, b, :], 1e-24).then_inc(pss_ok, 1)
                nc.vector.tensor_copy(dn[:, b, :, :], got[:, :, PROJ:PROJ + RSUM])

            def match(b):
                link(nc.vector.tensor_tensor(sq[:, b, :, :, :], pj[:, b, :, :].unsqueeze(2).broadcast_to([P, NT, E1, PROJ]),
                                             simn[:, :, :].unsqueeze(1).broadcast_to([P, NT, E1, PROJ]), ALU.mult))
                link(nc.vector.reduce_sum(lg[:, b, :, :], sq[:, b, :, :, :], AX.X))

            def margins(b):
                dve.wait_ge(prn_ok, b + 1)
                link(nc.vector.tensor_tensor(lg[:, b, :, :], lg[:, b, :, :], bc4(rn[:, b, :]), ALU.mult))
                link(nc.vector.reduce_max(mx[:, b, :], lg[:, b, :, :], AX.X))
                nc.vector.tensor_tensor(ex[:, b, :, :], lg[:, b, :, :], bc4(mx[:, b, :]), ALU.subtract).then_inc(d_ok, 1)

            def choose_one(b):
                link(nc.vector.tensor_tensor(eq[:, b, :, :], lg[:, b, :, :], bc4(mx[:, b, :]), ALU.is_equal))
                link(nc.vector.tensor_tensor(eq[:, b, :, :], eq[:, b, :, :], C1s[:, C1["tie4"]].unsqueeze(1).broadcast_to([P, NT, E1]), ALU.mult))
                link(nc.vector.reduce_max(mx[:, b, :], eq[:, b, :, :], AX.X))
                link(nc.vector.tensor_tensor(eq[:, b, :, :], eq[:, b, :, :], bc4(mx[:, b, :]), ALU.is_equal))
                dve.wait_ge(ex_ok, b + 1)
                link(nc.vector.reduce_sum(lw[:, b, :], ex[:, b, :, :], AX.X))
                link(nc.vector.reciprocal(lw[:, b, :], lw[:, b, :]))
                link(nc.vector.tensor_tensor(eq[:, b, :, :], eq[:, b, :, :], bc4(lw[:, b, :]), ALU.mult))
                c = 0
                for e, r in enumerate(RANKS):
                    part = dn[:, b, :, c:c + r]
                    last = nc.vector.tensor_tensor(part, part, eq[:, b, :, e:e + 1].broadcast_to([P, NT, r]), ALU.mult)
                    c += r
                last.then_inc(gd_ok, 1)

            def finish(b):
                dve.wait_ge(f_ps, b + 1)
                add_to_x(b, BANKS[b][1])

            def second_residual():
                dve.wait_ge(y_ps, 2)
                add_to_x(1, BANKS[1][1])

            rotate(0)
            second_residual()
            q1_low(0)
            norm_stats(2, 1)
            norm_apply(2, 1)
            subtract_max(0, 0)
            subtract_max(0, 1)
            sums(0, 0)
            subtract_max(0, 2)
            sums(0, 1)
            subtract_max(0, 3)
            sums(0, 2)
            reciprocals(0)
            rotate(1)
            q1_low(1)
            normalise1(0)
            subtract_max(1, 0)
            sums(1, 0)
            subtract_max(1, 1)
            residual1(0)
            norm_stats(3, 0)
            subtract_max(1, 2)
            sums(1, 1)
            subtract_max(1, 3)
            norm_apply(3, 0)
            sums(1, 2)
            reciprocals(1)
            normalise1(1)
            project(0)
            residual1(1)
            norm_stats(3, 1)
            match(0)
            margins(0)
            norm_apply(3, 1)
            choose_one(0)
            project(1)
            match(1)
            finish(0)
            margins(1)
            choose_one(1)
            finish(1)

        @block.tensor
        def _(pe):
            def transposes(layer, b, bank):
                pe.wait_ge(z_ok[b], layer + 1)
                for t in range(NT):
                    last = nc.tensor.transpose(PS[:, bank, t * P:(t + 1) * P], Z[:, b * NT + t, :], ident)
                last.then_inc(zt_ps[b], 1)

            def q_proj(b, g):
                pe.wait_ge(zt_ok[b], 1)
                if b:
                    pe.wait_ge(q_ok, g + 1)
                nc.tensor.matmul(PS[0:96, QBANK[g], :], W0s[:, W0["q"]][:, 96 * g:96 * g + 96],
                                 ZT[:, tokens(b)], start=True, stop=True).then_inc(q_ps, 1)

            def nat(b, n):
                t, gp = n // 2, n % 2
                if b == 0:
                    bank = (4, 6)[n % 2]
                    if n < 2:
                        pe.wait_ge(q_ok, 2 * n + 2)
                    if n >= 2:
                        pe.wait_ge(nat_max, n - 1)
                else:
                    bank = 4
                    pe.wait_ge(nat_max, 8 + n)
                for g in (2 * gp, 2 * gp + 1):
                    last = nc.tensor.matmul(PS[:, bank + g % 2, 0:GH * KC], Qaug[0:96, b, g, t * P:(t + 1) * P],
                                            Kaug[0:96, b, g, :], start=True, stop=True)
                last.then_inc(nat_ps, 1)

            def max_rows(b):
                pe.wait_ge(m_cat, b + 1)
                pe.wait_ge(idr_ok, 1)
                for t in range(NT):
                    last = nc.tensor.matmul(PS[:, 4, t * P:(t + 1) * P], mcat[:, b, t, :], identr[:, :], start=True, stop=True)
                last.then_inc(m_ps, 1)

            def scores(b, hp):
                u = 8 * b + hp
                if hp % 2 == 0:
                    pe.wait_ge(m_ok, G0 * b + hp // 2 + 1)
                if u >= 2:
                    pe.wait_ge(exp_ok, u - 1)
                for j in range(2):
                    g, i = (2 * hp + j) // GH, (2 * hp + j) % GH
                    last = nc.tensor.matmul(PS[0:KC, 2 * (u % 2) + j, :], Kaug[:, b, g, i * KC:(i + 1) * KC],
                                            Qaug[:, b, g, :], start=True, stop=True)
                last.then_inc(sc_ps, 1)

            def values(b, hp):
                u, s = 8 * b + hp, hp // 2
                pe.wait_ge(pt_lo[0], u + 1)
                pe.wait_ge(pt_lo[1], u + 1)
                if hp % 2 == 0 and SETS * b + s >= 2:
                    pe.wait_ge(acc_sb, SETS * b + s - 1)
                for j in range(2):
                    i = (2 * hp + j) % GH
                    stationary = Vp[:, b, s, VM * i:VM * (i + 1)]
                    nc.tensor.matmul(PS[0:VM, 6 + s % 2, :], stationary, PThi[u % 3][:, j, :], start=(i == 0), stop=False)
                    last = nc.tensor.matmul(PS[0:VM, 6 + s % 2, :], stationary, PTlo[u % 3][:, j, :], start=False, stop=(i == GH - 1))
                last.then_inc(pv_ok, 1)

            def out_turn(b, s, bank):
                pe.wait_ge(acc_sb, SETS * b + s + 1)
                for t in range(NT):
                    at = 72 * t + (VS + GH) * (s % 2)
                    last = nc.tensor.matmul(PS[:, bank, at:at + VS + GH], Osb[:, s, t * P:(t + 1) * P], C0s[0:VM, C0["fold"]], start=True, stop=True)
                last.then_inc(on_ps, 1)

            def out_back(b, bank):
                pe.wait_ge(on_ok, 2 * b + 2)
                for t in range(NT):
                    last = nc.tensor.transpose(PS[:, bank, t * P:(t + 1) * P], On[:, t, :], ident)
                last.then_inc(ont_ps, 1)

            def out_proj(b, bank):
                pe.wait_ge(ont_ok, b + 1)
                for t in range(NT):
                    last = nc.tensor.matmul(PS[:, bank, t * P:(t + 1) * P], OnT[:, t * P:(t + 1) * P], W0s[:, W0["o"]],
                                            start=True, stop=True)
                last.then_inc(proj_ps, 1)

            def router(b, bank):
                pe.wait_ge(zt_ok[b], 2)
                for t in range(NT):
                    last = nc.tensor.matmul(PS[:, bank, t * E:(t + 1) * E], ZT[:, b * S + t * P:b * S + (t + 1) * P], W1s[:, W1["r"]], start=True, stop=True)
                last.then_inc(lg_ps, 1)

            pe.wait_ge(ld_wk, 16)
            pe.wait_ge(ld_ctx, 16)
            for g in range(G0):
                last = nc.tensor.matmul(PS[0:96, 6 + g // 2, (g % 2) * B * KC:(g % 2 + 1) * B * KC],
                                        W0s[:, W0["k"]][:, 96 * g:96 * g + 96], ctxT[:, :], start=True, stop=True)
                if g % 2:
                    last.then_inc(k_ps, 1)
            pe.wait_ge(ld_id, 16)
            transposes(0, 0, 0)
            pe.wait_ge(ld_wq, 16)
            for g in range(G0):
                q_proj(0, g)
            pe.wait_ge(ld_wvo, 16)
            for b in range(B):
                last = nc.tensor.matmul(PS[0:KC, 5, b * D:(b + 1) * D], ctxT[:, b * KC:(b + 1) * KC], W0s[:, W0["v"]],
                                        start=True, stop=True)
            last.then_inc(v_ps, 1)
            transposes(0, 1, 4)
            pe.wait_ge(k_ok[0], 1)
            pe.wait_ge(zt_ok[1], 1)
            pe.wait_ge(v_ok, B)
            for n in range(8):
                if n == 1:
                    pe.wait_ge(k_full, 2)
                nat(0, n)
                if n % 2:
                    q_proj(1, n // 2)
            max_rows(0)
            pe.wait_ge(q_ok, 2 * G0)
            pe.wait_ge(kones, 1)
            pe.wait_ge(k_ok[1], 1)
            for hp in range(8):
                scores(0, hp)
                if hp == 0:
                    pe.wait_ge(m_ok, G0)
                nat(1, hp)
                if hp >= 3:
                    values(0, hp - 3)
            values(0, 5)
            values(0, 6)
            max_rows(1)
            out_turn(0, 0, 5)
            out_turn(0, 1, 5)
            values(0, 7)
            for hp in range(8):
                scores(1, hp)
                if hp >= 3:
                    values(1, hp - 3)
                if hp == 1:
                    pe.wait_ge(on_ok, 1)
                    out_turn(0, 2, 5)
                    out_turn(0, 3, 5)
                if hp == 2:
                    out_back(0, 5)
                if hp == 0:
                    pe.wait_ge(m_ok, 2 * G0)
                    pe.wait_ge(mn_ok, 1)
                    for b in range(B):
                        last = nc.tensor.transpose(PS[:, 4, b * KC:(b + 1) * KC], mn[:, b, :], ident[0:KC, 0:KC])
                    last.then_inc(mn_ps, 1)
                if hp == 1:
                    pe.wait_ge(w1s_ok, 1)
                    pe.wait_ge(mnt_ok, 1)
                    for n, name in enumerate(("k", "krot")):
                        nc.tensor.matmul(PS[:, 4, n * B * KC:(n + 1) * B * KC], W1s[:, W1[name]], mnT[:, :, :].rearrange("p b k -> p (b k)"), start=True, stop=True)
                    at = 2 * B * KC
                    for b in range(B):
                        last = nc.tensor.matmul(PS[0:KC, 4, at + b * HD1:at + (b + 1) * HD1], mnT[:, b, :], W1s[:, W1["v"]], start=True, stop=True)
                    last.then_inc(kv1_ps, 1)
                if hp == 3:
                    pe.wait_ge(kv1_read, 1)
                    out_proj(0, 4)
                if hp == 6:
                    transposes(1, 0, 5)
                if hp == 7:
                    out_turn(1, 0, 4)
            values(1, 5)
            values(1, 6)
            out_turn(1, 1, 4)
            values(1, 7)
            pe.wait_ge(on_ok, 3)
            router(0, 4)

            def gate_rows(b):
                pe.wait_ge(gcat_ok, b + 1)
                for t in range(NT):
                    last = nc.tensor.matmul(PS[0:2 * E, 7 - b, t * P:(t + 1) * P], gcat[:, b * NT + t, :], identr[:, :], start=True, stop=True)
                last.then_inc(gt_ps, 1)

            def gate_spread(i, n):
                b, k = n // 2, n % 2
                if b == 0:
                    pe.wait_ge(gsel_ok, 2 * i + k + 1)
                nc.tensor.matmul(PS[:, 6 + k, :], gsel[:, k, :], gT[:, tokens(b)], start=True, stop=True).then_inc(gate_ps, 1)

            def three(to, half, k, c, right_hi, right_lo, start, stop):
                hi, lo = Whi[:, k, half, c * P:(c + 1) * P], Wlo[:, k, half, c * P:(c + 1) * P]
                nc.tensor.matmul(to, hi, right_hi, start=start, stop=False)
                nc.tensor.matmul(to, lo, right_hi, start=False, stop=False)
                return nc.tensor.matmul(to, hi, right_lo, start=False, stop=stop)

            def up(i, j, first=False):
                b, k, c = j // (2 * FC), j // FC % 2, j % FC
                if b == 0 and c == 0:
                    pe.wait_ge(w_up[k], i + 1)
                if not first:
                    pe.wait_ge(silu_ok, US * i + j - LAG + 1)
                three(PS[:, j % LAG, :], 0, k, c, Zhi[:, tokens(b)], Zlo[:, tokens(b)], True, True).then_inc(h_ps, 1)

            def down(i, j):
                b, k, c = j // (2 * FC), j // FC % 2, j % FC
                if b == 0 and c == 0:
                    pe.wait_ge(w_down[k], i + 1)
                pe.wait_ge(h_ok, US * i + j + 1)
                if c == 0:
                    pe.wait_ge(y_used, 4 * i + j // FC + 1)
                three(PS[:, 4 + k, :], 1, k, c, Hhi[:, j % NH, :], Hlo[:, j % NH, :], c == 0, c == FC - 1).then_inc(down_ok, 1)

            pe.wait_ge(zsplit_ok, 1)
            pe.wait_ge(exp_ok, 16)
            up(0, 0, True)
            out_turn(1, 2, 6)
            out_turn(1, 3, 6)
            up(0, 1, True)
            up(0, 2, True)
            up(0, 3, True)
            out_back(1, 7)
            pe.wait_ge(lg_read, 1)
            down(0, 0)
            out_proj(1, 6)
            for j in range(US):
                if j:
                    down(0, j)
                if j == 7:
                    pe.wait_ge(silu_ok, 2 * FC)
                    router(1, 3)
                    pe.wait_ge(zsplit_ok, 2)
                    for n in range(2 * FC, 2 * FC + LAG):
                        if n % LAG == 3:
                            pe.wait_ge(lg_read, 2)
                        up(0, n)
                elif not LAG <= j < 2 * FC:
                    up(j + LAG >= US, (j + LAG) % US)
                if j == 2:
                    gate_rows(0)
                if j == 4:
                    pe.wait_ge(gt_ok, 1)
                    pe.wait_ge(x_ok[1], 1)
                    gate_spread(0, 0)
                if j == 5:
                    pe.wait_ge(silu_ok, LAG + 1)
                    transposes(1, 1, 0)
                if j == 6:
                    gate_spread(0, 1)
                if j == 13:
                    gate_rows(1)
                if j == 14:
                    pe.wait_ge(gt_ok, 2)
                    gate_spread(0, 2)
                if j == 15:
                    gate_spread(0, 3)
            with pe.Fori(1, PAIRS - 1) as i:
                for j in range(US):
                    down(i, j)
                    up(i + (j + LAG) // US, (j + LAG) % US)
                    if j % FC == 1:
                        gate_spread(i, j // FC)

            def y_back(b, bank):
                pe.wait_ge(y_added, 4 * PAIRS - 2 * (1 - b))
                for t in range(NT):
                    last = nc.tensor.transpose(PS[:, bank, t * P:(t + 1) * P], Yacc[:, b * S + t * P:b * S + (t + 1) * P], ident)
                last.then_inc(y_ps, 1)

            for j in range(US):
                down(PAIRS - 1, j)
                if j + LAG < US:
                    up(PAIRS - 1, j + LAG)
                if j % FC == 1 and j < 13:
                    gate_spread(PAIRS - 1, j // FC)
                if j == 10:
                    y_back(0, BANKS[0][1])
                if j == 13:
                    pe.wait_ge(x_ok[0], 2)
                    gate_spread(PAIRS - 1, 3)
                if j == 14:
                    pe.wait_ge(silu_ok, PAIRS * US - FC + 1)
                    transposes(2, 0, 0)

            def q1_proj(b, n):
                pe.wait_ge(zt_ok[b], 3)
                pe.wait_ge(x_ok[b], 2)
                nc.tensor.matmul(PS[:, QBANK1[b][n], :], W1s[:, W1[("q", "qrot")[n]]], ZT[:, tokens(b)], start=True, stop=True).then_inc(q1_ps, 1)

            def nat1(b, t):
                if t == 0:
                    pe.wait_ge(q1_ok, b + 1)
                    pe.wait_ge(fill_ok, 1)
                    pe.wait_ge(k1_ok, 1)
                    if b:
                        pe.wait_ge(q1_rot, 1)
                if t >= 2:
                    pe.wait_ge(sub1_ok[b], t - 1)
                to = PS[:, BANKS[b][2 + t % 2], 0:H1 * KC]
                at = slice(b * S + t * P, b * S + (t + 1) * P)
                nc.tensor.matmul(to, Q1hi[:, at], Kbhi[:, b, :], start=True, stop=False)
                nc.tensor.matmul(to, Q1hi[:, at], Kblo[:, b, :], start=False, stop=False)
                nc.tensor.matmul(to, Q1lo[:, at], Kbhi[:, b, :], start=False, stop=False)
                nc.tensor.matmul(to, onesr[:, :], fill[:, b, :], start=False, stop=True).then_inc(nat1_ps[b], 1)

            def turn(b, t):
                pe.wait_ge(exp1_ok[b], t + 1)
                if t:
                    pe.wait_ge(pt1_ok[b], t)
                elif b == 0:
                    pe.wait_ge(y_used, 4 * PAIRS + 2)
                for h in range(H1):
                    last = nc.tensor.transpose(PS[0:KC, BANKS[b][0], h * P:(h + 1) * P], Pn1[:, b, t, h * KC:(h + 1) * KC], ident)
                last.then_inc(tr1_ps[b], 1)

            def values1(b, t):
                pe.wait_ge(pt1_ok[b], t + 1)
                for h in range(H1):
                    at = t * P + h * HD1
                    last = nc.tensor.matmul(PS[:, BANKS[b][1], at:at + HD1], PT1[:, b, t % 2, h * P:(h + 1) * P],
                                            V1[:, b, :], start=True, stop=True)
                last.then_inc(pv1_ok[b], 1)

            def out1_back(b):
                pe.wait_ge(on1_ok[b], 1)
                for t in range(NT):
                    last = nc.tensor.transpose(PS[:, BANKS[b][3], t * P:(t + 1) * P], On1[:, b, t, :], ident)
                last.then_inc(ont1_ps, 1)

            def out1_proj(b):
                pe.wait_ge(ont1_ok, b + 1)
                for t in range(NT):
                    last = nc.tensor.matmul(PS[:, BANKS[b][1], t * P:(t + 1) * P], OnT1[:, b, t * P:(t + 1) * P], W1s[:, W1["o"]], start=True, stop=True)
                last.then_inc(proj1_ps, 1)

            def projections(b):
                pe.wait_ge(zt_ok[b], 4)
                w = PROJ + RSUM
                for t in range(NT):
                    last = nc.tensor.matmul(PS[:, BANKS[b][3], t * w:(t + 1) * w], ZT[:, b * S + t * P:b * S + (t + 1) * P], W1s[:, W1["pd"]], start=True, stop=True)
                last.then_inc(pd_ps, 1)

            def gated_down_rows(b):
                pe.wait_ge(gd_ok, b + 1)
                for t in range(NT):
                    last = nc.tensor.transpose(PS[0:RSUM, BANKS[b][2], t * P:(t + 1) * P], dn[:, b, t, :], ident)
                last.then_inc(gd_ps, 1)

            def base_product(b):
                pe.wait_ge(x_ok[b], 3)
                for t in range(NT):
                    nc.tensor.matmul(PS[:, BANKS[b][1], t * P:(t + 1) * P], ZT[:, b * S + t * P:b * S + (t + 1) * P], W1s[:, W1["base"]], start=(t == 0), stop=False)

            def last_product(b):
                pe.wait_ge(gdt_ok, b + 1)
                for t in range(NT):
                    last = nc.tensor.matmul(PS[:, BANKS[b][1], t * P:(t + 1) * P], gdT[:, b, t * P:(t + 1) * P], W1s[0:RSUM, W1["up"]], start=False, stop=(t == NT - 1))
                last.then_inc(f_ps, 1)

            pe.wait_ge(silu_ok, PAIRS * US)
            def keep_clock(n, bank):
                for _ in range(n):
                    nc.tensor.matmul(PS[:, bank, :], identr[:, :], Whi[:, 0, 0, :], start=True, stop=True)

            q1_proj(0, 0)
            q1_proj(0, 1)
            y_back(1, BANKS[1][1])
            keep_clock(16, 1)
            nat1(0, 0)
            nat1(0, 1)
            transposes(2, 1, BANKS[1][0])
            nat1(0, 2)
            turn(0, 0)
            nat1(0, 3)
            q1_proj(1, 0)
            turn(0, 1)
            values1(0, 0)
            q1_proj(1, 1)
            turn(0, 2)
            values1(0, 1)
            turn(0, 3)
            values1(0, 2)
            values1(0, 3)
            keep_clock(3, 0)
            nat1(1, 0)
            out1_back(0)
            nat1(1, 1)
            keep_clock(2, 0)
            out1_proj(0)
            turn(1, 0)
            nat1(1, 2)
            keep_clock(2, 0)
            turn(1, 1)
            values1(1, 0)
            nat1(1, 3)
            keep_clock(2, 0)
            turn(1, 2)
            values1(1, 1)
            transposes(3, 0, BANKS[0][0])
            keep_clock(2, 0)
            turn(1, 3)
            values1(1, 2)
            values1(1, 3)
            keep_clock(3, 0)
            out1_back(1)
            projections(0)
            keep_clock(2, 0)
            out1_proj(1)
            base_product(0)
            keep_clock(12, 0)
            transposes(3, 1, BANKS[1][0])
            keep_clock(4, 0)
            gated_down_rows(0)
            keep_clock(3, 6)
            projections(1)
            last_product(0)
            base_product(1)
            keep_clock(14, 6)
            gated_down_rows(1)
            keep_clock(4, 6)
            last_product(1)


def kernel(**inputs):
    import numpy as np
    import concourse.bacc as bacc
    from concourse.bass_utils import run_bass_kernel_spmd as run

    a = {k: np.asarray(v) for k, v in inputs.items()}
    f4 = np.float32

    def pack(cols, width, **parts):
        out = np.zeros((P, width), f4)
        for name, (row, part) in parts.items():
            out[row:row + part.shape[0], cols[name]] = part
        return out

    row = np.arange(P)
    def block_mask(rows, per, heads):
        m = np.zeros((rows, heads, KC), f4)
        m[np.arange(rows), (np.arange(rows) // per) % heads, :] = 1
        return m.reshape(rows, -1)
    ones = np.zeros((32, GH, KC), f4)
    for i in range(GH):
        ones[i, i] = 1
        ones[GH + i, i] = 1
    fold = np.concatenate([np.eye(VS + GH, dtype=f4), np.eye(VS, VS + GH, dtype=f4)])
    c0 = pack(C0, C0W, ident=(0, np.eye(P, dtype=f4)), block=(0, block_mask(96, HD0, GH)),
              ones=(96, ones.reshape(32, -1)), fold=(0, fold))
    half = HD1 // 2
    timescale = np.power(f4(10000.0), f4(2.0 / HD1) * np.arange(half, dtype=f4)).astype(f4)
    def rope(pos):
        rad = pos.astype(f4)[None, :] / timescale[:, None]
        sin, cos = np.sin(rad), np.cos(rad)
        return np.tile(np.concatenate([cos, cos]), (H1, 1)), np.tile(np.concatenate([-sin, sin]), (H1, 1))
    qcos, qsin = rope(np.arange(KC, KC + S))
    kcos, ksin = rope(np.arange(KC))
    gsel = np.zeros((2 * E, E, P), f4)
    for e in range(E):
        gsel[e, e] = 1
        gsel[E + e, e] = 1
    c1 = pack(C1, C1W, qcos=(0, qcos), qsin=(0, qsin), kcos=(0, kcos), ksin=(0, ksin), block=(0, block_mask(P, HD1, H1)),
              gsel=(0, gsel.reshape(2 * E, -1)),
              tie8=(0, np.tile(np.arange(E, 0, -1, dtype=f4), (P, 1))), tie4=(0, np.tile(np.arange(E1, 0, -1, dtype=f4), (P, 1))))

    def thrice(w):
        w = w.T.reshape(D, G0, 1, GH * HD0)
        return np.broadcast_to(w, (D, G0, 3, GH * HD0)).reshape(D, -1)
    w0 = pack(W0, W0W, k=(0, thrice(a["L0_xattn_Wk"])), q=(0, thrice(a["L0_xattn_Wq"])),
              v=(0, a["L0_xattn_Wv"].T), o=(0, a["L0_xattn_Wo"].T))
    qw = a["L1_xattn_q_w"].transpose(1, 0, 2)
    swap = np.r_[half:HD1, 0:half]
    kw = a["L1_xattn_kv_w"][0, 0]
    downs = np.concatenate([a[f"L1_ffn_Wd{i}"] for i in range(E1)], 0).T
    ups = np.concatenate([a[f"L1_ffn_Wu{i}"] for i in range(E1)], 1).T
    w1 = pack(W1, W1W, r=(0, a["L0_ffn_Wr"].T), q=(0, qw.reshape(D, -1)), qrot=(0, qw[:, :, swap].reshape(D, -1)),
              k=(0, np.tile(kw, (1, H1))), krot=(0, np.tile(kw[:, swap], (1, H1))), v=(0, a["L1_xattn_kv_w"][1, 0]),
              o=(0, a["L1_xattn_out_w"].reshape(D, D)), rms=(0, a["L1_xattn_rms_scale"][:, None]),
              pd=(0, np.concatenate([a["L1_ffn_Wp"].T, downs], 1)), base=(0, a["L1_ffn_W"].T), up=(0, ups),
              bp=(0, np.tile(a["L1_ffn_bp"], (P, 1))), sim=(0, np.tile(a["L1_ffn_sim"].T.reshape(1, -1), (P, 1))),
              temp=(0, np.tile(a["L1_ffn_temp"], (P, 1))))
    up = a["L0_ffn_W1"].transpose(0, 2, 1)
    down = a["L0_ffn_W2"].reshape(E, D, FC, P).transpose(0, 3, 2, 1).reshape(E, P, FC * D)
    mask = np.zeros((B, KCP), np.bool_)
    mask[:, :KC] = a["mask_BxS2_bk0"]
    arrays = {
        "x": a["x"], "ctx_nat": a["ctx_1024"].transpose(1, 0, 2), "ctx_t": a["ctx_1024"].transpose(2, 0, 1).reshape(D, B * KC),
        "mask": mask.view(np.uint32).reshape(1, -1),
        "c0": c0, "w0": w0, "c1": c1, "w1": w1, "moe": np.concatenate([up, down], 2),
    }
    arrays = {k: np.ascontiguousarray(v) for k, v in arrays.items()}
    nc = bacc.Bacc("TRN2", target_bir_lowering=False, num_devices=1)
    args = [nc.dram_tensor(n, v.shape, mybir.dt.from_np(v.dtype), kind="ExternalInput").ap() for n, v in arrays.items()]
    args.append(nc.dram_tensor("out", (B, S, D), mybir.dt.float32, kind="ExternalOutput").ap())
    fused_layers(nc, *args)
    return run(nc, [arrays], core_ids=[0]).results[0]["out"]
```
